# Optimizing a Trainium2 kernel written in Bass

```python
import numpy as np
import jax
import jax.numpy as jnp

def _softmax(x, axis=-1):
    return jax.nn.softmax(x, axis=axis)

def _gelu(x):
    return jax.nn.gelu(x, approximate=True)

def _silu(x):
    return jax.nn.silu(x)

def _sigmoid(x):
    return jax.nn.sigmoid(x)

def _layernorm(x, axis=-1, eps=1e-05):
    m = jnp.mean(x, axis=axis, keepdims=True)
    v = jnp.var(x, axis=axis, keepdims=True)
    return (x - m) / jnp.sqrt(v + eps)

def _scatter_add(tgt, idx, src, axis=0):
    return tgt.at[idx].add(src)

def _segment_sum(src, seg, n):
    return jax.ops.segment_sum(src, seg, n)
kernel_name = 'mk_xattn_ffn_d4_seqx_r8_7a6f7d'

def setup_inputs(seed: int=0):
    np.random.seed(seed)
    _w = jnp.asarray

    def _rec_inputs():
        import jax
        import jax.numpy as jnp
        _rk = jax.random.key(seed)
        x = -0.0003929 + 0.9999 * jax.random.normal(jax.random.fold_in(_rk, 1), (8, 256, 128), jnp.float32)
        _lenS = 256 - jax.random.randint(jax.random.fold_in(_rk, 7), (8,), 0, max(1, 256 // 4) + 1, jnp.int32)
        _lenS2 = 1601 - jax.random.randint(jax.random.fold_in(_rk, 8), (8,), 0, max(1, 1601 // 4) + 1, jnp.int32)
        _ctx_1024P = jax.random.normal(jax.random.fold_in(_rk, 11), (8, 16, 128), jnp.float32)
        _ctx_1024c = jax.random.dirichlet(jax.random.fold_in(_rk, 511), 0.3 * jnp.ones((16,), jnp.float32), (8, 1601))
        _ctx_1024t = jnp.einsum('bsk,bkd->bsd', _ctx_1024c, _ctx_1024P)
        _ctx_1024t = _ctx_1024t * jax.lax.rsqrt(jnp.mean(jnp.square(_ctx_1024t)) + 1e-12) * 0.953939
        ctx_1024 = 2.81802e-05 + 1.00001 * (_ctx_1024t + 0.3 * jax.random.normal(jax.random.fold_in(_rk, 611), (8, 1601, 128), jnp.float32))
        _validS = jnp.arange(256)[None, :] < _lenS[:, None]
        _validS2 = jnp.arange(1601)[None, :] < _lenS2[:, None]
        _causal = jnp.tril(jnp.ones((256, 256), dtype=bool))
        mask_BxSxS2_bk0 = jnp.logical_not(jnp.broadcast_to(_validS2[:, None, :], (8, 256, 1601)))
        return (x, ctx_1024, mask_BxSxS2_bk0)
    x, ctx_1024, mask_BxSxS2_bk0 = _rec_inputs()

    def _L0_xattn_setup():
        import jax, jax.numpy as jnp
        import numpy as np
        DIM = 128
        B, TI, TJ = (8, 256, 256)
        EPS = 1e-05

        def layernorm(x, g, b):
            mu = jnp.mean(x, axis=-1, keepdims=True)
            var = jnp.var(x, axis=-1, keepdims=True)
            return (x - mu) * jax.lax.rsqrt(var + EPS) * g + b
        key = jax.random.key(seed)
        ks = jax.random.split(key, 12)
        s = 1.0 / np.sqrt(DIM)
        return {'target': jax.random.normal(ks[0], (B, TI, DIM), jnp.float32), 'source_k': jax.random.normal(ks[1], (B, TJ, DIM), jnp.float32), 'source_v': jax.random.normal(ks[2], (B, TJ, DIM), jnp.float32), 'Wq': jax.random.uniform(ks[3], (DIM, DIM), jnp.float32, -s, s), 'bq': jax.random.uniform(ks[4], (DIM,), jnp.float32, -s, s), 'Wk': jax.random.uniform(ks[5], (DIM, DIM), jnp.float32, -s, s), 'bk': jax.random.uniform(ks[6], (DIM,), jnp.float32, -s, s), 'Wv': jax.random.uniform(ks[7], (DIM, DIM), jnp.float32, -s, s), 'bv': jax.random.uniform(ks[8], (DIM,), jnp.float32, -s, s), 'g_t': jnp.ones((DIM,), jnp.float32), 'b_t': jnp.zeros((DIM,), jnp.float32), 'g_k': jnp.ones((DIM,), jnp.float32), 'b_k': jnp.zeros((DIM,), jnp.float32), 'g_v': jnp.ones((DIM,), jnp.float32), 'b_v': jnp.zeros((DIM,), jnp.float32)}
    _L0_xattn_all = _L0_xattn_setup()
    _L0_xattn_in = {k: v for k, v in _L0_xattn_all.items() if k in ('Wq', 'bq', 'Wk', 'bk', 'Wv', 'bv', 'g_t', 'b_t', 'g_k', 'b_k', 'g_v', 'b_v')}
    del _L0_xattn_all

    def _L0_ffn_setup():
        import jax, jax.numpy as jnp
        import numpy as np
        B, S, D = (1, 256, 128)
        E, F = (16, 128)
        NG, TKG, K = (4, 2, 4)
        NSH = 2
        SCALE = 2.5
        STD = 0.02
        EPG = E // NG

        def _route(x_flat, router_w, bias):
            logits = x_flat.astype(jnp.float32) @ router_w.T
            scores = jax.nn.sigmoid(logits)
            s = scores + bias[None, :]
            sg = s.reshape(-1, NG, EPG)
            group_score = jax.lax.top_k(sg, 2)[0].sum(-1)
            gidx = jax.lax.top_k(group_score, TKG)[1]
            gmask = jnp.sum(jax.nn.one_hot(gidx, NG, dtype=jnp.float32), axis=1) > 0
            emask = jnp.repeat(gmask, EPG, axis=1)
            masked = jnp.where(emask, s, -1.0)
            topk_idx = jax.lax.top_k(masked, K)[1]
            tw = jnp.take_along_axis(scores, topk_idx, axis=1)
            tw = tw / (tw.sum(-1, keepdims=True) + 1e-20)
            tw = tw * SCALE
            return (topk_idx, tw)
        key = jax.random.key(seed)
        ks = jax.random.split(key, 8)
        return {'hidden_states': jax.random.normal(ks[0], (B, S, D), jnp.float32), 'router_w': jax.random.normal(ks[1], (E, D), jnp.float32) * STD, 'bias': jnp.zeros((E,), jnp.float32), 'gate_w': jax.random.normal(ks[2], (E, D, F), jnp.float32) * STD, 'up_w': jax.random.normal(ks[3], (E, D, F), jnp.float32) * STD, 'down_w': jax.random.normal(ks[4], (E, F, D), jnp.float32) * STD, 'sh_gate_w': jax.random.normal(ks[5], (D, NSH * F), jnp.float32) * STD, 'sh_up_w': jax.random.normal(ks[6], (D, NSH * F), jnp.float32) * STD, 'sh_down_w': jax.random.normal(ks[7], (NSH * F, D), jnp.float32) * STD}
    _L0_ffn_all = _L0_ffn_setup()
    _L0_ffn_in = {k: v for k, v in _L0_ffn_all.items() if k in ('router_w', 'bias', 'gate_w', 'up_w', 'down_w', 'sh_gate_w', 'sh_up_w', 'sh_down_w')}
    del _L0_ffn_all

    def _L1_xattn_setup():
        import jax, jax.numpy as jnp
        import numpy as np
        Q_DIM = 128
        K_DIM = 128
        V_DIM = 128
        ATTEN_DIM = 128
        NUM_HEADS = 16
        HEAD_DIM = ATTEN_DIM // NUM_HEADS
        B, L = (4, 256)
        key = jax.random.key(seed)
        ks = jax.random.split(key, 11)
        s = 0.02
        return {'query': jax.random.normal(ks[0], (B, L, Q_DIM), dtype=jnp.float32), 'key': jax.random.normal(ks[1], (B, L, K_DIM), dtype=jnp.float32), 'value': jax.random.normal(ks[2], (B, L, V_DIM), dtype=jnp.float32), 'Wq': jax.random.normal(ks[3], (Q_DIM, ATTEN_DIM), dtype=jnp.float32) * s, 'bq': jnp.zeros((ATTEN_DIM,), dtype=jnp.float32), 'Wk': jax.random.normal(ks[4], (K_DIM, ATTEN_DIM), dtype=jnp.float32) * s, 'bk': jnp.zeros((ATTEN_DIM,), dtype=jnp.float32), 'Wv': jax.random.normal(ks[5], (V_DIM, ATTEN_DIM), dtype=jnp.float32) * s, 'bv': jnp.zeros((ATTEN_DIM,), dtype=jnp.float32), 'Wo': jax.random.normal(ks[6], (ATTEN_DIM, V_DIM), dtype=jnp.float32) * s, 'bo': jnp.zeros((V_DIM,), dtype=jnp.float32)}
    _L1_xattn_all = _L1_xattn_setup()
    _L1_xattn_in = {k: v for k, v in _L1_xattn_all.items() if k in ('Wq', 'bq', 'Wk', 'bk', 'Wv', 'bv', 'Wo', 'bo')}
    del _L1_xattn_all

    def _L1_ffn_setup():
        import jax, jax.numpy as jnp
        import numpy as np
        E = 16
        G = 4
        EPG = E // G
        K = 4
        TOPK_GROUP = 2
        PER_GROUP_K = K // TOPK_GROUP

        def _route(xf, router_w, correction_bias):
            S = xf.shape[0]
            logits = xf @ router_w.T
            scores = jax.nn.sigmoid(logits)
            sb = scores + correction_bias
            grp_top = jax.lax.top_k(sb.reshape(S, G, EPG), PER_GROUP_K)[0]
            group_scores = grp_top.sum(axis=-1)
            _, group_idx = jax.lax.top_k(group_scores, TOPK_GROUP)
            group_mask = jnp.zeros((S, G), sb.dtype).at[jnp.arange(S)[:, None], group_idx].set(1.0)
            score_mask = jnp.broadcast_to(group_mask[:, :, None], (S, G, EPG)).reshape(S, E)
            masked = jnp.where(score_mask > 0, sb, -jnp.inf)
            _, topk_idx = jax.lax.top_k(masked, K)
            w = jnp.take_along_axis(scores, topk_idx, axis=1)
            w = w / (w.sum(axis=-1, keepdims=True) + 1e-20)
            return (topk_idx, w, scores)
        key = jax.random.key(seed)
        ks = jax.random.split(key, 9)
        B, T, C, H, HS = (2, 128, 128, 32, 256)
        std = 0.02
        return {'x': jax.random.normal(ks[0], (B, T, C), jnp.float32), 'router_w': jax.random.normal(ks[1], (E, C), jnp.float32) * std, 'correction_bias': jnp.zeros((E,), jnp.float32), 'gate_w': jax.random.normal(ks[2], (E, C, H), jnp.float32) * std, 'up_w': jax.random.normal(ks[3], (E, C, H), jnp.float32) * std, 'down_w': jax.random.normal(ks[4], (E, H, C), jnp.float32) * std, 'shared_gate_w': jax.random.normal(ks[5], (HS, C), jnp.float32) * std, 'shared_up_w': jax.random.normal(ks[6], (HS, C), jnp.float32) * std, 'shared_down_w': jax.random.normal(ks[7], (C, HS), jnp.float32) * std}
    _L1_ffn_all = _L1_ffn_setup()
    _L1_ffn_in = {k: v for k, v in _L1_ffn_all.items() if k in ('router_w', 'correction_bias', 'gate_w', 'up_w', 'down_w', 'shared_gate_w', 'shared_up_w', 'shared_down_w')}
    del _L1_ffn_all

    def _L2_xattn_setup():
        import jax, jax.numpy as jnp
        import numpy as np
        B, S, D = (2, 256, 128)
        H, HD = (16, 64)
        key = jax.random.key(seed)
        ks = jax.random.split(key, 10)
        scale = 1.0 / np.sqrt(D)
        inputs_q = jax.random.normal(ks[0], (B, S, D), dtype=jnp.float32)
        inputs_kv = jax.random.normal(ks[1], (B, S, D), dtype=jnp.float32)
        mask = jnp.broadcast_to(jnp.tril(jnp.ones((S, S), dtype=bool)), (B, S, S))
        Wq = jax.random.normal(ks[2], (D, H * HD), dtype=jnp.float32) * scale
        bq = jnp.zeros((H * HD,), dtype=jnp.float32)
        Wk = jax.random.normal(ks[3], (D, H * HD), dtype=jnp.float32) * scale
        bk = jnp.zeros((H * HD,), dtype=jnp.float32)
        Wv = jax.random.normal(ks[4], (D, H * HD), dtype=jnp.float32) * scale
        bv = jnp.zeros((H * HD,), dtype=jnp.float32)
        Wo = jax.random.normal(ks[5], (H * HD, D), dtype=jnp.float32) * scale
        bo = jnp.zeros((D,), dtype=jnp.float32)
        return {'inputs_q': inputs_q, 'inputs_kv': inputs_kv, 'mask': mask, 'Wq': Wq, 'bq': bq, 'Wk': Wk, 'bk': bk, 'Wv': Wv, 'bv': bv, 'Wo': Wo, 'bo': bo}
    _L2_xattn_all = _L2_xattn_setup()
    _L2_xattn_in = {k: v for k, v in _L2_xattn_all.items() if k in ('Wq', 'bq', 'Wk', 'bk', 'Wv', 'bv', 'Wo', 'bo')}
    del _L2_xattn_all

    def _L2_ffn_setup():
        import jax, jax.numpy as jnp
        import numpy as np
        H = 128
        I = 64
        IS = 128
        E = 16
        G = 4
        TOPK_G = 2
        TOPK = 4
        SCALE = 2.5
        B, S = (2, 128)

        def _relu2(x):
            r = jax.nn.relu(x)
            return r * r

        def _route(scores, bias_corr):
            T = scores.shape[0]
            s_choice = scores + bias_corr
            gs = s_choice.reshape(T, G, E // G)
            group_scores = jnp.sum(jax.lax.top_k(gs, 2)[0], axis=-1)
            gidx = jax.lax.top_k(group_scores, TOPK_G)[1]
            gmask = jnp.sum(jax.nn.one_hot(gidx, G, dtype=scores.dtype), axis=1)
            smask = jnp.repeat(gmask, E // G, axis=1)
            masked = jnp.where(smask > 0, s_choice, 0.0)
            topk_idx = jax.lax.top_k(masked, TOPK)[1]
            topk_w = jnp.take_along_axis(scores, topk_idx, axis=1)
            topk_w = topk_w / (jnp.sum(topk_w, axis=-1, keepdims=True) + 1e-20)
            topk_w = topk_w * SCALE
            return (topk_idx, topk_w)
        key = jax.random.key(seed)
        ks = jax.random.split(key, 8)
        sd = 0.02
        return {'hidden_states': jax.random.normal(ks[0], (B, S, H), jnp.float32), 'Wg': jax.random.normal(ks[1], (E, H), jnp.float32) * sd, 'bias_corr': jax.random.normal(ks[2], (E,), jnp.float32) * 0.01, 'W1': jax.random.normal(ks[3], (E, I, H), jnp.float32) * sd, 'W2': jax.random.normal(ks[4], (E, H, I), jnp.float32) * sd, 'Ws1': jax.random.normal(ks[5], (IS, H), jnp.float32) * sd, 'Ws2': jax.random.normal(ks[6], (H, IS), jnp.float32) * sd}
    _L2_ffn_all = _L2_ffn_setup()
    _L2_ffn_in = {k: v for k, v in _L2_ffn_all.items() if k in ('Wg', 'bias_corr', 'W1', 'W2', 'Ws1', 'Ws2')}
    del _L2_ffn_all

    def _L3_xattn_setup():
        import jax, jax.numpy as jnp
        import numpy as np
        B, M, N, DIM, DH, H = (8, 512, 64, 128, 128, 8)
        INNER = DH * H
        EPS = 1e-05

        def _layernorm(x, g, b):
            mu = jnp.mean(x, axis=-1, keepdims=True)
            var = jnp.var(x, axis=-1, keepdims=True)
            return (x - mu) * jax.lax.rsqrt(var + EPS) * g + b
        key = jax.random.key(seed)
        ks = jax.random.split(key, 8)
        sd = 0.02
        return {'x': jax.random.normal(ks[0], (B, M, DIM), jnp.float32), 'latents': jax.random.normal(ks[1], (B, N, DIM), jnp.float32), 'gamma_media': jnp.ones((DIM,), jnp.float32), 'beta_media': jnp.zeros((DIM,), jnp.float32), 'gamma_lat': jnp.ones((DIM,), jnp.float32), 'beta_lat': jnp.zeros((DIM,), jnp.float32), 'Wq': jax.random.normal(ks[2], (DIM, INNER), jnp.float32) * sd, 'bq': jnp.zeros((INNER,), jnp.float32), 'Wkv': jax.random.normal(ks[3], (DIM, 2 * INNER), jnp.float32) * sd, 'bkv': jnp.zeros((2 * INNER,), jnp.float32), 'Wo': jax.random.normal(ks[4], (INNER, DIM), jnp.float32) * sd, 'bo': jnp.zeros((DIM,), jnp.float32)}
    _L3_xattn_all = _L3_xattn_setup()
    _L3_xattn_in = {k: v for k, v in _L3_xattn_all.items() if k in ('gamma_media', 'beta_media', 'gamma_lat', 'beta_lat', 'Wq', 'bq', 'Wkv', 'bkv', 'Wo', 'bo')}
    del _L3_xattn_all

    def _L3_ffn_setup():
        import jax, jax.numpy as jnp
        import numpy as np
        B, N, D, H, E = (4, 128, 128, 16, 8)
        DK = D // H
        HID = 4 * D
        EPS = 1e-05

        def _layernorm(x, w, b):
            m = jnp.mean(x, axis=-1, keepdims=True)
            v = jnp.mean(jnp.square(x - m), axis=-1, keepdims=True)
            return (x - m) * jax.lax.rsqrt(v + EPS) * w + b

        def _msa(x, w_qkv, w_proj):
            b, n, d = x.shape
            qkv = (x @ w_qkv).reshape(b, n, 3, H, DK)
            q = qkv[:, :, 0].transpose(0, 2, 1, 3)
            k = qkv[:, :, 1].transpose(0, 2, 1, 3)
            v = qkv[:, :, 2].transpose(0, 2, 1, 3)
            attn = jnp.einsum('bhnd,bhmd->bhnm', q, k) * (1.0 / np.sqrt(DK))
            attn = jax.nn.softmax(attn, axis=-1)
            y = jnp.einsum('bhnm,bhmd->bhnd', attn, v)
            y = y.transpose(0, 2, 1, 3).reshape(b, n, d)
            return y @ w_proj

        def _moe_mlp(x, gate_w, gate_b, w1, w2):
            b, n, d = x.shape
            xf = x.reshape(b * n, d)
            logits = xf @ gate_w + gate_b
            one_hot = jax.nn.one_hot(jnp.argmax(logits, axis=-1), E, dtype=xf.dtype)
            h = jax.nn.gelu(jnp.einsum('td,edh->teh', xf, w1), approximate=True)
            y = jnp.einsum('teh,ehd->ted', h, w2)
            out = jnp.einsum('te,ted->td', one_hot, y)
            return out.reshape(b, n, d)
        key = jax.random.key(seed)
        ks = jax.random.split(key, 8)
        s = 0.02
        return {'x': jax.random.normal(ks[0], (B, N, D), jnp.float32), 'ln1_w': jnp.ones((D,), jnp.float32), 'ln1_b': jnp.zeros((D,), jnp.float32), 'w_qkv': jax.random.normal(ks[1], (D, 3 * D), jnp.float32) * s, 'w_proj': jax.random.normal(ks[2], (D, D), jnp.float32) * s, 'ln2_w': jnp.ones((D,), jnp.float32), 'ln2_b': jnp.zeros((D,), jnp.float32), 'gate_w': jax.random.normal(ks[3], (D, E), jnp.float32) * s, 'gate_b': jnp.zeros((E,), jnp.float32), 'w1': jax.random.normal(ks[4], (E, D, HID), jnp.float32) * s, 'w2': jax.random.normal(ks[5], (E, HID, D), jnp.float32) * s}
    _L3_ffn_all = _L3_ffn_setup()
    _L3_ffn_in = {k: v for k, v in _L3_ffn_all.items() if k in ('ln1_w', 'ln1_b', 'w_qkv', 'w_proj', 'ln2_w', 'ln2_b', 'gate_w', 'gate_b', 'w1', 'w2')}
    del _L3_ffn_all
    return {'x': x, 'ctx_1024': ctx_1024, 'mask_BxSxS2_bk0': mask_BxSxS2_bk0, 'L0_xattn_Wq': _L0_xattn_in['Wq'], 'L0_xattn_bq': _L0_xattn_in['bq'], 'L0_xattn_Wk': _L0_xattn_in['Wk'], 'L0_xattn_bk': _L0_xattn_in['bk'], 'L0_xattn_Wv': _L0_xattn_in['Wv'], 'L0_xattn_bv': _L0_xattn_in['bv'], 'L0_xattn_g_t': _L0_xattn_in['g_t'], 'L0_xattn_b_t': _L0_xattn_in['b_t'], 'L0_xattn_g_k': _L0_xattn_in['g_k'], 'L0_xattn_b_k': _L0_xattn_in['b_k'], 'L0_xattn_g_v': _L0_xattn_in['g_v'], 'L0_xattn_b_v': _L0_xattn_in['b_v'], 'L0_ffn_router_w': _L0_ffn_in['router_w'], 'L0_ffn_bias': _L0_ffn_in['bias'], 'L0_ffn_gate_w': _L0_ffn_in['gate_w'], 'L0_ffn_up_w': _L0_ffn_in['up_w'], 'L0_ffn_down_w': _L0_ffn_in['down_w'], 'L0_ffn_sh_gate_w': _L0_ffn_in['sh_gate_w'], 'L0_ffn_sh_up_w': _L0_ffn_in['sh_up_w'], 'L0_ffn_sh_down_w': _L0_ffn_in['sh_down_w'], 'L1_xattn_Wq': _L1_xattn_in['Wq'], 'L1_xattn_bq': _L1_xattn_in['bq'], 'L1_xattn_Wk': _L1_xattn_in['Wk'], 'L1_xattn_bk': _L1_xattn_in['bk'], 'L1_xattn_Wv': _L1_xattn_in['Wv'], 'L1_xattn_bv': _L1_xattn_in['bv'], 'L1_xattn_Wo': _L1_xattn_in['Wo'], 'L1_xattn_bo': _L1_xattn_in['bo'], 'L1_ffn_router_w': _L1_ffn_in['router_w'], 'L1_ffn_correction_bias': _L1_ffn_in['correction_bias'], 'L1_ffn_gate_w': _L1_ffn_in['gate_w'], 'L1_ffn_up_w': _L1_ffn_in['up_w'], 'L1_ffn_down_w': _L1_ffn_in['down_w'], 'L1_ffn_shared_gate_w': _L1_ffn_in['shared_gate_w'], 'L1_ffn_shared_up_w': _L1_ffn_in['shared_up_w'], 'L1_ffn_shared_down_w': _L1_ffn_in['shared_down_w'], 'L2_xattn_Wq': _L2_xattn_in['Wq'], 'L2_xattn_bq': _L2_xattn_in['bq'], 'L2_xattn_Wk': _L2_xattn_in['Wk'], 'L2_xattn_bk': _L2_xattn_in['bk'], 'L2_xattn_Wv': _L2_xattn_in['Wv'], 'L2_xattn_bv': _L2_xattn_in['bv'], 'L2_xattn_Wo': _L2_xattn_in['Wo'], 'L2_xattn_bo': _L2_xattn_in['bo'], 'L2_ffn_Wg': _L2_ffn_in['Wg'], 'L2_ffn_bias_corr': _L2_ffn_in['bias_corr'], 'L2_ffn_W1': _L2_ffn_in['W1'], 'L2_ffn_W2': _L2_ffn_in['W2'], 'L2_ffn_Ws1': _L2_ffn_in['Ws1'], 'L2_ffn_Ws2': _L2_ffn_in['Ws2'], 'L3_xattn_gamma_media': _L3_xattn_in['gamma_media'], 'L3_xattn_beta_media': _L3_xattn_in['beta_media'], 'L3_xattn_gamma_lat': _L3_xattn_in['gamma_lat'], 'L3_xattn_beta_lat': _L3_xattn_in['beta_lat'], 'L3_xattn_Wq': _L3_xattn_in['Wq'], 'L3_xattn_bq': _L3_xattn_in['bq'], 'L3_xattn_Wkv': _L3_xattn_in['Wkv'], 'L3_xattn_bkv': _L3_xattn_in['bkv'], 'L3_xattn_Wo': _L3_xattn_in['Wo'], 'L3_xattn_bo': _L3_xattn_in['bo'], 'L3_ffn_ln1_w': _L3_ffn_in['ln1_w'], 'L3_ffn_ln1_b': _L3_ffn_in['ln1_b'], 'L3_ffn_w_qkv': _L3_ffn_in['w_qkv'], 'L3_ffn_w_proj': _L3_ffn_in['w_proj'], 'L3_ffn_ln2_w': _L3_ffn_in['ln2_w'], 'L3_ffn_ln2_b': _L3_ffn_in['ln2_b'], 'L3_ffn_gate_w': _L3_ffn_in['gate_w'], 'L3_ffn_gate_b': _L3_ffn_in['gate_b'], 'L3_ffn_w1': _L3_ffn_in['w1'], 'L3_ffn_w2': _L3_ffn_in['w2']}

def reference(x, ctx_1024, mask_BxSxS2_bk0, L0_xattn_Wq, L0_xattn_bq, L0_xattn_Wk, L0_xattn_bk, L0_xattn_Wv, L0_xattn_bv, L0_xattn_g_t, L0_xattn_b_t, L0_xattn_g_k, L0_xattn_b_k, L0_xattn_g_v, L0_xattn_b_v, L0_ffn_router_w, L0_ffn_bias, L0_ffn_gate_w, L0_ffn_up_w, L0_ffn_down_w, L0_ffn_sh_gate_w, L0_ffn_sh_up_w, L0_ffn_sh_down_w, L1_xattn_Wq, L1_xattn_bq, L1_xattn_Wk, L1_xattn_bk, L1_xattn_Wv, L1_xattn_bv, L1_xattn_Wo, L1_xattn_bo, L1_ffn_router_w, L1_ffn_correction_bias, L1_ffn_gate_w, L1_ffn_up_w, L1_ffn_down_w, L1_ffn_shared_gate_w, L1_ffn_shared_up_w, L1_ffn_shared_down_w, L2_xattn_Wq, L2_xattn_bq, L2_xattn_Wk, L2_xattn_bk, L2_xattn_Wv, L2_xattn_bv, L2_xattn_Wo, L2_xattn_bo, L2_ffn_Wg, L2_ffn_bias_corr, L2_ffn_W1, L2_ffn_W2, L2_ffn_Ws1, L2_ffn_Ws2, L3_xattn_gamma_media, L3_xattn_beta_media, L3_xattn_gamma_lat, L3_xattn_beta_lat, L3_xattn_Wq, L3_xattn_bq, L3_xattn_Wkv, L3_xattn_bkv, L3_xattn_Wo, L3_xattn_bo, L3_ffn_ln1_w, L3_ffn_ln1_b, L3_ffn_w_qkv, L3_ffn_w_proj, L3_ffn_ln2_w, L3_ffn_ln2_b, L3_ffn_gate_w, L3_ffn_gate_b, L3_ffn_w1, L3_ffn_w2):
    import jax
    import jax.numpy as jnp

    def _L0_xattn_ref(target, source_k, source_v, Wq, bq, Wk, bk, Wv, bv, g_t, b_t, g_k, b_k, g_v, b_v):
        import jax, jax.numpy as jnp
        import numpy as np
        DIM = 128
        B, TI, TJ = (8, 256, 256)
        EPS = 1e-05

        def layernorm(x, g, b):
            mu = jnp.mean(x, axis=-1, keepdims=True)
            var = jnp.var(x, axis=-1, keepdims=True)
            return (x - mu) * jax.lax.rsqrt(var + EPS) * g + b
        scale = DIM ** (-0.5)
        t = layernorm(target, g_t, b_t)
        sk = layernorm(source_k, g_k, b_k)
        sv = layernorm(source_v, g_v, b_v)
        q = jnp.einsum('bid,ed->bie', t, Wq) + bq
        k = jnp.einsum('bjd,ed->bje', sk, Wk) + bk
        v = jnp.einsum('bjd,ed->bje', sv, Wv) + bv
        dots = jnp.einsum('bid,bjd->bij', q, k) * scale
        attn = jax.nn.softmax(dots, axis=2)
        return jnp.einsum('bij,bjd->bid', attn, v)

    def _L0_ffn_ref(hidden_states, router_w, bias, gate_w, up_w, down_w, sh_gate_w, sh_up_w, sh_down_w):
        import jax, jax.numpy as jnp
        import numpy as np
        B, S, D = (1, 256, 128)
        E, F = (16, 128)
        NG, TKG, K = (4, 2, 4)
        NSH = 2
        SCALE = 2.5
        STD = 0.02
        EPG = E // NG

        def _route(x_flat, router_w, bias):
            logits = x_flat.astype(jnp.float32) @ router_w.T
            scores = jax.nn.sigmoid(logits)
            s = scores + bias[None, :]
            sg = s.reshape(-1, NG, EPG)
            group_score = jax.lax.top_k(sg, 2)[0].sum(-1)
            gidx = jax.lax.top_k(group_score, TKG)[1]
            gmask = jnp.sum(jax.nn.one_hot(gidx, NG, dtype=jnp.float32), axis=1) > 0
            emask = jnp.repeat(gmask, EPG, axis=1)
            masked = jnp.where(emask, s, -1.0)
            topk_idx = jax.lax.top_k(masked, K)[1]
            tw = jnp.take_along_axis(scores, topk_idx, axis=1)
            tw = tw / (tw.sum(-1, keepdims=True) + 1e-20)
            tw = tw * SCALE
            return (topk_idx, tw)
        x = hidden_states.reshape(-1, D)
        topk_idx, tw = _route(x, router_w, bias)
        combine = (jax.nn.one_hot(topk_idx, E, dtype=tw.dtype) * tw[..., None]).sum(1)
        h = jnp.einsum('td,edf->etf', x, gate_w)
        u = jnp.einsum('td,edf->etf', x, up_w)
        y = jnp.einsum('etf,efd->etd', jax.nn.silu(h) * u, down_w)
        routed = jnp.einsum('etd,te->td', y, combine)
        sh = jax.nn.silu(x @ sh_gate_w) * (x @ sh_up_w) @ sh_down_w
        return (routed + sh).reshape(hidden_states.shape)

    def _L1_xattn_ref(query, key, value, Wq, bq, Wk, bk, Wv, bv, Wo, bo):
        import jax, jax.numpy as jnp
        import numpy as np
        Q_DIM = 128
        K_DIM = 128
        V_DIM = 128
        ATTEN_DIM = 128
        NUM_HEADS = 16
        HEAD_DIM = ATTEN_DIM // NUM_HEADS
        B, L = (4, 256)
        q = query @ Wq + bq
        k = key @ Wk + bk
        v = value @ Wv + bv

        def split_heads(x):
            return x.reshape(x.shape[:-1] + (NUM_HEADS, HEAD_DIM))
        q, k, v = (split_heads(q), split_heads(k), split_heads(v))
        scale = 1.0 / HEAD_DIM ** 0.5
        scores = jnp.einsum('bqhd,bkhd->bhqk', q, k) * scale
        attn = jax.nn.softmax(scores, axis=-1)
        out = jnp.einsum('bhqk,bkhd->bqhd', attn, v)
        out = out.reshape(out.shape[0], out.shape[1], ATTEN_DIM)
        return out @ Wo + bo

    def _L1_ffn_ref(x, router_w, correction_bias, gate_w, up_w, down_w, shared_gate_w, shared_up_w, shared_down_w):
        import jax, jax.numpy as jnp
        import numpy as np
        E = 16
        G = 4
        EPG = E // G
        K = 4
        TOPK_GROUP = 2
        PER_GROUP_K = K // TOPK_GROUP

        def _route(xf, router_w, correction_bias):
            S = xf.shape[0]
            logits = xf @ router_w.T
            scores = jax.nn.sigmoid(logits)
            sb = scores + correction_bias
            grp_top = jax.lax.top_k(sb.reshape(S, G, EPG), PER_GROUP_K)[0]
            group_scores = grp_top.sum(axis=-1)
            _, group_idx = jax.lax.top_k(group_scores, TOPK_GROUP)
            group_mask = jnp.zeros((S, G), sb.dtype).at[jnp.arange(S)[:, None], group_idx].set(1.0)
            score_mask = jnp.broadcast_to(group_mask[:, :, None], (S, G, EPG)).reshape(S, E)
            masked = jnp.where(score_mask > 0, sb, -jnp.inf)
            _, topk_idx = jax.lax.top_k(masked, K)
            w = jnp.take_along_axis(scores, topk_idx, axis=1)
            w = w / (w.sum(axis=-1, keepdims=True) + 1e-20)
            return (topk_idx, w, scores)
        B, T, C = x.shape
        S = B * T
        xf = x.reshape(S, C)
        sg = xf @ shared_gate_w.T
        su = xf @ shared_up_w.T
        shared_out = jax.nn.silu(sg) * su @ shared_down_w.T
        topk_idx, w, _scores = _route(xf, router_w, correction_bias)
        combine = jnp.zeros((S, E), xf.dtype).at[jnp.arange(S)[:, None], topk_idx].add(w)
        g = jnp.einsum('sc,ech->esh', xf, gate_w)
        u = jnp.einsum('sc,ech->esh', xf, up_w)
        h = jax.nn.silu(g) * u
        hw = h * combine.T[:, :, None]
        routed = jnp.einsum('esh,ehc->sc', hw, down_w)
        return (shared_out + routed).reshape(B, T, C)

    def _L2_xattn_ref(inputs_q, inputs_kv, mask, Wq, bq, Wk, bk, Wv, bv, Wo, bo):
        import jax, jax.numpy as jnp
        import numpy as np
        B, S, D = (2, 256, 128)
        H, HD = (16, 64)
        b, s_q, _ = inputs_q.shape
        s_k = inputs_kv.shape[1]
        q = (inputs_q @ Wq + bq).reshape(b, s_q, H, HD)
        k = (inputs_kv @ Wk + bk).reshape(b, s_k, H, HD)
        v = (inputs_kv @ Wv + bv).reshape(b, s_k, H, HD)
        q = q / jnp.sqrt(jnp.asarray(HD, dtype=q.dtype))
        attn = jnp.einsum('bqhd,bkhd->bhqk', q, k)
        m = mask[:, None, :, :]
        attn = jnp.where(m, attn, jnp.asarray(-1e+30, dtype=attn.dtype))
        attn = jax.nn.softmax(attn, axis=-1)
        out = jnp.einsum('bhqk,bkhd->bqhd', attn, v).reshape(b, s_q, H * HD)
        return out @ Wo + bo

    def _L2_ffn_ref(hidden_states, Wg, bias_corr, W1, W2, Ws1, Ws2):
        import jax, jax.numpy as jnp
        import numpy as np
        H = 128
        I = 64
        IS = 128
        E = 16
        G = 4
        TOPK_G = 2
        TOPK = 4
        SCALE = 2.5
        B, S = (2, 128)

        def _relu2(x):
            r = jax.nn.relu(x)
            return r * r

        def _route(scores, bias_corr):
            T = scores.shape[0]
            s_choice = scores + bias_corr
            gs = s_choice.reshape(T, G, E // G)
            group_scores = jnp.sum(jax.lax.top_k(gs, 2)[0], axis=-1)
            gidx = jax.lax.top_k(group_scores, TOPK_G)[1]
            gmask = jnp.sum(jax.nn.one_hot(gidx, G, dtype=scores.dtype), axis=1)
            smask = jnp.repeat(gmask, E // G, axis=1)
            masked = jnp.where(smask > 0, s_choice, 0.0)
            topk_idx = jax.lax.top_k(masked, TOPK)[1]
            topk_w = jnp.take_along_axis(scores, topk_idx, axis=1)
            topk_w = topk_w / (jnp.sum(topk_w, axis=-1, keepdims=True) + 1e-20)
            topk_w = topk_w * SCALE
            return (topk_idx, topk_w)
        b, s, h = hidden_states.shape
        flat = hidden_states.reshape(-1, h)
        T = flat.shape[0]
        logits = flat.astype(jnp.float32) @ Wg.T
        scores = jax.nn.sigmoid(logits)
        topk_idx, topk_w = _route(scores, bias_corr)
        topk_w = topk_w.astype(hidden_states.dtype)
        cw = jnp.zeros((T, E), flat.dtype)
        cw = cw.at[jnp.arange(T)[:, None], topk_idx].add(topk_w)
        hid = _relu2(jnp.einsum('th,eih->eti', flat, W1))
        y = jnp.einsum('eti,ehi->eth', hid, W2)
        out = jnp.einsum('eth,te->th', y, cw)
        shared = _relu2(flat @ Ws1.T) @ Ws2.T
        return (out + shared).reshape(b, s, h)

    def _L3_xattn_ref(x, latents, gamma_media, beta_media, gamma_lat, beta_lat, Wq, bq, Wkv, bkv, Wo, bo):
        import jax, jax.numpy as jnp
        import numpy as np
        B, M, N, DIM, DH, H = (8, 512, 64, 128, 128, 8)
        INNER = DH * H
        EPS = 1e-05

        def _layernorm(x, g, b):
            mu = jnp.mean(x, axis=-1, keepdims=True)
            var = jnp.var(x, axis=-1, keepdims=True)
            return (x - mu) * jax.lax.rsqrt(var + EPS) * g + b
        b = x.shape[0]
        xn = _layernorm(x, gamma_media, beta_media)
        ln = _layernorm(latents, gamma_lat, beta_lat)
        q = ln @ Wq + bq
        kv_input = jnp.concatenate([xn, ln], axis=1)
        kv = kv_input @ Wkv + bkv
        k, v = jnp.split(kv, 2, axis=-1)

        def to_heads(t):
            return t.reshape(b, t.shape[1], H, DH).transpose(0, 2, 1, 3)
        q, k, v = (to_heads(q), to_heads(k), to_heads(v))
        q = q * DH ** (-0.5)
        sim = jnp.einsum('bhid,bhjd->bhij', q, k)
        attn = jax.nn.softmax(sim, axis=-1)
        out = jnp.einsum('bhij,bhjd->bhid', attn, v)
        out = out.transpose(0, 2, 1, 3).reshape(b, -1, INNER)
        return out @ Wo + bo

    def _L3_ffn_ref(x, ln1_w, ln1_b, w_qkv, w_proj, ln2_w, ln2_b, gate_w, gate_b, w1, w2):
        import jax, jax.numpy as jnp
        import numpy as np
        B, N, D, H, E = (4, 128, 128, 16, 8)
        DK = D // H
        HID = 4 * D
        EPS = 1e-05

        def _layernorm(x, w, b):
            m = jnp.mean(x, axis=-1, keepdims=True)
            v = jnp.mean(jnp.square(x - m), axis=-1, keepdims=True)
            return (x - m) * jax.lax.rsqrt(v + EPS) * w + b

        def _msa(x, w_qkv, w_proj):
            b, n, d = x.shape
            qkv = (x @ w_qkv).reshape(b, n, 3, H, DK)
            q = qkv[:, :, 0].transpose(0, 2, 1, 3)
            k = qkv[:, :, 1].transpose(0, 2, 1, 3)
            v = qkv[:, :, 2].transpose(0, 2, 1, 3)
            attn = jnp.einsum('bhnd,bhmd->bhnm', q, k) * (1.0 / np.sqrt(DK))
            attn = jax.nn.softmax(attn, axis=-1)
            y = jnp.einsum('bhnm,bhmd->bhnd', attn, v)
            y = y.transpose(0, 2, 1, 3).reshape(b, n, d)
            return y @ w_proj

        def _moe_mlp(x, gate_w, gate_b, w1, w2):
            b, n, d = x.shape
            xf = x.reshape(b * n, d)
            logits = xf @ gate_w + gate_b
            one_hot = jax.nn.one_hot(jnp.argmax(logits, axis=-1), E, dtype=xf.dtype)
            h = jax.nn.gelu(jnp.einsum('td,edh->teh', xf, w1), approximate=True)
            y = jnp.einsum('teh,ehd->ted', h, w2)
            out = jnp.einsum('te,ted->td', one_hot, y)
            return out.reshape(b, n, d)
        x = x + _msa(_layernorm(x, ln1_w, ln1_b), w_qkv, w_proj)
        x = x + _moe_mlp(_layernorm(x, ln2_w, ln2_b), gate_w, gate_b, w1, w2)
        return x
    x = x + _L0_xattn_ref(_layernorm(x, axis=-1), ctx_1024, ctx_1024, L0_xattn_Wq, L0_xattn_bq, L0_xattn_Wk, L0_xattn_bk, L0_xattn_Wv, L0_xattn_bv, L0_xattn_g_t, L0_xattn_b_t, L0_xattn_g_k, L0_xattn_b_k, L0_xattn_g_v, L0_xattn_b_v)
    x = x + _L0_ffn_ref(_layernorm(x, axis=-1), L0_ffn_router_w, L0_ffn_bias, L0_ffn_gate_w, L0_ffn_up_w, L0_ffn_down_w, L0_ffn_sh_gate_w, L0_ffn_sh_up_w, L0_ffn_sh_down_w)
    x = x + _L1_xattn_ref(_layernorm(x, axis=-1), ctx_1024, ctx_1024, L1_xattn_Wq, L1_xattn_bq, L1_xattn_Wk, L1_xattn_bk, L1_xattn_Wv, L1_xattn_bv, L1_xattn_Wo, L1_xattn_bo)
    x = x + _L1_ffn_ref(_layernorm(x, axis=-1), L1_ffn_router_w, L1_ffn_correction_bias, L1_ffn_gate_w, L1_ffn_up_w, L1_ffn_down_w, L1_ffn_shared_gate_w, L1_ffn_shared_up_w, L1_ffn_shared_down_w)
    x = x + _L2_xattn_ref(_layernorm(x, axis=-1), ctx_1024, mask_BxSxS2_bk0, L2_xattn_Wq, L2_xattn_bq, L2_xattn_Wk, L2_xattn_bk, L2_xattn_Wv, L2_xattn_bv, L2_xattn_Wo, L2_xattn_bo)
    x = x + _L2_ffn_ref(_layernorm(x, axis=-1), L2_ffn_Wg, L2_ffn_bias_corr, L2_ffn_W1, L2_ffn_W2, L2_ffn_Ws1, L2_ffn_Ws2)
    x = x + _L3_xattn_ref(ctx_1024, _layernorm(x, axis=-1), L3_xattn_gamma_media, L3_xattn_beta_media, L3_xattn_gamma_lat, L3_xattn_beta_lat, L3_xattn_Wq, L3_xattn_bq, L3_xattn_Wkv, L3_xattn_bkv, L3_xattn_Wo, L3_xattn_bo)
    x = x + _L3_ffn_ref(_layernorm(x, axis=-1), L3_ffn_ln1_w, L3_ffn_ln1_b, L3_ffn_w_qkv, L3_ffn_w_proj, L3_ffn_ln2_w, L3_ffn_ln2_b, L3_ffn_gate_w, L3_ffn_gate_b, L3_ffn_w1, L3_ffn_w2)
    return x

_drawn_inputs = setup_inputs


def setup_inputs(seed=0):
    import zlib

    import numpy as np

    out = dict(_drawn_inputs(seed))
    spreads = {'L0_xattn_g_t': (1.0, 0.6),
     'L0_xattn_b_t': (0.0, 0.8),
     'L0_xattn_g_k': (1.0, 0.6),
     'L0_xattn_b_k': (0.0, 2.0),
     'L0_xattn_g_v': (1.0, 0.2),
     'L0_xattn_b_v': (0.0, 0.1),
     'L0_ffn_bias': (0.0, 0.8),
     'L1_xattn_bq': (0.0, 0.8),
     'L1_xattn_bk': (0.0, 2.0),
     'L1_xattn_bv': (0.0, 0.597),
     'L1_xattn_bo': (0.0, 0.1),
     'L1_ffn_correction_bias': (0.0, 0.8),
     'L2_xattn_bq': (0.0, 0.1),
     'L2_xattn_bk': (0.0, 2.0),
     'L2_xattn_bv': (0.0, 0.1),
     'L2_xattn_bo': (0.0, 0.1),
     'L3_xattn_gamma_media': (1.0, 0.6),
     'L3_xattn_beta_media': (0.0, 2.0),
     'L3_xattn_gamma_lat': (1.0, 0.6),
     'L3_xattn_beta_lat': (0.0, 2.0),
     'L3_xattn_bq': (0.0, 2.0),
     'L3_xattn_bkv': (0.0, 0.8),
     'L3_xattn_bo': (0.0, 0.8),
     'L3_ffn_ln1_w': (1.0, 0.6),
     'L3_ffn_ln1_b': (0.0, 0.8),
     'L3_ffn_ln2_w': (1.0, 0.6),
     'L3_ffn_ln2_b': (0.0, 0.8),
     'L3_ffn_gate_b': (0.0, 1.631)}
    factors = {'L0_xattn_bq': 8.0,
     'L0_xattn_bk': 200.0,
     'L0_ffn_router_w': 8.0,
     'L0_ffn_gate_w': 8.0,
     'L0_ffn_up_w': 8.0,
     'L0_ffn_down_w': 8.0,
     'L0_ffn_sh_gate_w': 8.0,
     'L0_ffn_sh_up_w': 8.0,
     'L0_ffn_sh_down_w': 8.0,
     'L1_xattn_Wq': 8.0,
     'L1_xattn_Wk': 8.0,
     'L1_xattn_Wv': 3.796,
     'L1_xattn_Wo': 2.847,
     'L1_ffn_router_w': 8.0,
     'L1_ffn_gate_w': 8.0,
     'L1_ffn_up_w': 8.0,
     'L1_ffn_down_w': 8.0,
     'L1_ffn_shared_gate_w': 8.0,
     'L1_ffn_shared_up_w': 8.0,
     'L1_ffn_shared_down_w': 8.0,
     'L2_ffn_Wg': 8.0,
     'L2_ffn_bias_corr': 8.0,
     'L2_ffn_W1': 8.0,
     'L2_ffn_W2': 8.0,
     'L2_ffn_Ws1': 8.0,
     'L2_ffn_Ws2': 7.408,
     'L3_xattn_Wq': 64.0,
     'L3_ffn_w_qkv': 3.646,
     'L3_ffn_w_proj': 3.546,
     'L3_ffn_gate_w': 3.294,
     'L3_ffn_w1': 3.1,
     'L3_ffn_w2': 3.082,
     'L3_xattn_Wkv': 4.034,
     'L3_xattn_Wo': 3.973}
    for name, (base, spread) in spreads.items():
        noise = np.random.default_rng([zlib.crc32(name.encode()), seed]).standard_normal(out[name].shape)
        drawn = base * np.exp(spread * noise) if base else spread * noise
        out[name] = jnp.asarray(drawn.astype(out[name].dtype))
    for name, factor in factors.items():
        out[name] = (out[name] * factor).astype(out[name].dtype)
    return out
```

```python
from contextlib import ExitStack

import numpy as np

import concourse.bass as bass
from concourse import mybir

F32 = mybir.dt.float32
F32R = mybir.dt.float32r
BF16 = mybir.dt.bfloat16
I32 = mybir.dt.int32
U8 = mybir.dt.uint8
ALU = mybir.AluOpType
ACT = mybir.ActivationFunctionType
AX = mybir.AxisListType.X

P = 128
D = 128
B = 8
S = 256
SH = S // P
J_CTX = 1601
CT = -(-J_CTX // P)
CTAIL = J_CTX - (CT - 1) * P
N_TOK = B * S
CHUNK = 512
CTILES = CHUNK // P
N_CHUNK = N_TOK // CHUNK
EPS = 1e-5
MASKED = 1e30
LOWEST = -3.0e38
S_BANKS = 3
P_SLOTS = 4


def split_steps(n_items, n_steps):
    return [(k + 1) * n_items // n_steps - k * n_items // n_steps for k in range(n_steps)]


class Attention:

    def __init__(self, name, heads, head_dim, context, latents, norm_source, norms, v_cols, v_block,
                 key_bias, mask=False, own_affine=False, shared_affine=False, fold_wo=False,
                 keep_norm=False, k_affine=False, v_bias=False, out_bias=None):
        self.name, self.H, self.dh = name, heads, head_dim
        self.LT = SH if latents else 0
        self.C = CT if context else 0
        self.T = self.LT + self.C
        self.J = (S if latents else 0) + (J_CTX if context else 0)
        self.norm_source = norm_source
        self.norms = norms
        self.v_cols = v_cols
        self.v_block = v_block
        self.key_bias = key_bias
        self.mask = mask
        self.own_affine = own_affine
        self.shared_affine = shared_affine
        self.k_affine = k_affine
        self.fold_wo = fold_wo
        self.keep_norm = keep_norm
        self.HU = min(heads, 2)
        self.W = self.HU * S
        self.NP = heads // self.HU
        self.QG = max(1, heads * head_dim // P)
        self.PPG = 2 if v_block == 32 else 1
        self.NG = self.NP // self.PPG
        self.NU = self.NP * self.T
        self.parts = (3 if key_bias else 0) + 2
        self.K_ROWS = self.parts * self.HU
        self.scale = float(head_dim) ** -0.5
        self.ones_column = v_block == 32
        self.M_CH = [(c, min(c + 1024, self.J)) for c in range(0, self.J, 1024)]
        self.M_ITEMS = [(e, hf, c) for e in range(self.HU) for hf in range(SH) for c in range(len(self.M_CH))]
        self.KB = -(-self.T // 4)
        self.NV = self.T * (v_cols // 512)
        self.FIN = heads if fold_wo else self.NG
        self.tail = CTAIL if context else P

    def ring(self):
        q = self.KB
        qk = q + self.QG
        v = qk + self.NP
        return 0, q, qk, v, v + self.NV


ATTENTIONS = {
    "L0a": Attention("L0a", 1, 128, True, False, True, 2, 0, 128, True, own_affine=True, k_affine=True),
    "L1a": Attention("L1a", 16, 8, True, False, False, 1, 512, 32, True),
    "L2a": Attention("L2a", 16, 64, True, False, False, 1, 1024, 64, True, mask=True),
    "L3a": Attention("L3a", 8, 128, True, True, True, 2, 0, 128, True, own_affine=True,
                     shared_affine=True, fold_wo=True),
    "L3s": Attention("L3s", 16, 8, False, True, False, 2, 512, 32, False, own_affine=True, keep_norm=True),
}


def clear(nc, sems):
    for s in sems:
        nc.sync.sem_clear(s)
    nc.all_engine_barrier()


def rsqrt_steps(dve, y, v, t, n):
    dve.tensor_scalar(v, v, EPS, None, ALU.add)
    dve.drain()
    dve.tensor_scalar(t.bitcast(I32), v.bitcast(I32), 1, None, ALU.logical_shift_right)
    dve.drain()
    dve.tensor_scalar(y.bitcast(I32), t.bitcast(I32), -1.0, 1597463007.0, ALU.mult, ALU.add)
    dve.tensor_scalar(v, v, -0.5, None, ALU.mult)
    dve.drain()
    for _ in range(3):
        dve.tensor_tensor(t, y, y, ALU.mult)
        dve.drain()
        dve.tensor_tensor(t, t, v, ALU.mult)
        dve.drain()
        dve.scalar_tensor_tensor(y, t, 1.5, y, ALU.add, ALU.mult)
        dve.drain()


def normalise(dve, out, src, st, n, last=None):
    for t in range(n):
        dve.bn_stats(st["six"][:, t, :], src[:, t, :])
    dve.drain()
    for t in range(n):
        dve.bn_aggr(st["mv"][:, t, :], st["six"][:, t, :])
    dve.drain()
    dve.tensor_copy(st["var"][:, 0:n], st["mv"][:, 0:n, 1])
    dve.drain()
    rsqrt_steps(dve, st["rs"][:, 0:n], st["var"][:, 0:n], st["tmp"][:, 0:n], n)
    for t in range(n):
        ins = dve.tensor_scalar(out[:, t, :], src[:, t, :], st["mv"][:, t, 0:1], st["rs"][:, t:t + 1],
                                ALU.subtract, ALU.mult)
    return ins


def affine(dve, out, src, g, b, n):
    dve.tensor_tensor(out, src, g.unsqueeze(1).broadcast_to([P, n, D]), ALU.mult)
    dve.drain()
    return dve.tensor_tensor(out, out, b.unsqueeze(1).broadcast_to([P, n, D]), ALU.add)


def build_attention(nc, c, io, x_in, x_out):
    kt0, q0, qk0, v0, u0 = c.ring()
    T, H, W, HU, NP, NG, NU, NI = c.T, c.H, c.W, c.HU, c.NP, c.NG, c.NU, len(c.M_ITEMS)
    JP = T * P
    NA = NP * (T - 1)
    summed = lambda u: u // T * (T - 1) + max(u % T, 1)
    a = lambda key: io[f"{c.name}_{key}"]
    with ExitStack() as ctx, ExitStack() as done:
        done.callback(lambda: clear(nc, sems))
        sb = lambda name, shape, dt=F32: ctx.enter_context(nc.sbuf_tensor(f"{c.name}_{name}", shape, dt))
        pb = lambda name, shape, dt=F32: ctx.enter_context(nc.psum_tensor(f"{c.name}_{name}", shape, dt))
        sems = []

        def sem(name):
            sems.append(ctx.enter_context(nc.semaphore(f"{c.name}_{name}")))
            return sems[-1]


        ident = sb("ident", [P, P])
        ident_b = sb("ident_b", [P, P], BF16)
        ones_b = sb("ones_b", [P, P], BF16)
        ones_f = sb("ones_f", [P, P])
        pick = sb("pick", [c.K_ROWS, HU])
        wq = sb("wq", [P, c.QG, P])
        wk = sb("wk", [P, H, P])
        bq = sb("bq", [P, c.QG])
        wfin = sb("wfin", [P, c.FIN, P])
        bfin = sb("bfin", [P, 1])
        loads = [(ident, io["ident"]), (pick, a("pick")), (wq, a("wq")), (wk, a("wk")), (bq, a("bq"))]
        if c.fold_wo:
            wvt, wo = sb("wvt", [P, H, P]), sb("wo", [P, H, P])
            bvh, bo = sb("bvh", [P, H]), sb("bo", [P, 1])
            loads += [(wvt, a("wvt")), (wo, a("wo")), (bvh, a("bvh")), (bo, a("bo"))]
        else:
            loads += [(wfin, a("wfin")), (bfin, a("bfin"))]
        if c.key_bias:
            bk = sb("bk", [P, H])
            loads += [(bk, a("bk"))]
        if c.ones_column:
            spread = sb("spread", [P, P])
            loads += [(spread, io["spread"])]
        if c.v_cols:
            wv = sb("wv", [P, c.v_cols])
            wv_hi, wv_lo = sb("wv_hi", [P, c.v_cols], F32R), sb("wv_lo", [P, c.v_cols], F32R)
            bv = sb("bv", [P, c.v_cols])
            loads += [(wv, a("wv")), (bv, a("bv"))]
        if c.own_affine:
            gx, bx = sb("gx", [P, D]), sb("bx", [P, D])
            loads += [(gx, a("gx")), (bx, a("bx"))]
        if c.norm_source:
            gk, bkk = sb("gk", [P, D]), sb("bkk", [P, D])
            loads += [(gk, a("gk")), (bkk, a("bkk"))]
        if c.k_affine:
            gv, bvv = sb("gv", [P, D]), sb("bvv", [P, D])
            loads += [(gv, a("gv")), (bvv, a("bvv"))]

        xin = sb("xin", [P, SH, D])
        xn = sb("xn", [P, SH, D])
        y = xn if c.norms == 1 else sb("y", [P, SH, D])
        xo = sb("xo", [P, SH, D])
        if c.C:
            cx = sb("cx", [P, CT, D])
        src = sb("src", [P, T, D]) if (c.norm_source or c.LT) else cx
        ksrc = sb("ksrc", [P, T, D]) if c.k_affine else src
        kt_hi, kt_lo = sb("kt_hi", [P, JP], F32R), sb("kt_lo", [P, JP], F32R)
        yt = sb("yt", [P, S])
        qt = sb("qt", [P, c.QG, S])
        q_hi, q_lo = sb("q_hi", [P, H * S], F32R), sb("q_lo", [P, H * S], F32R)
        v = sb("v", [P, T, c.v_cols]) if c.v_cols else src
        qb = sb("qb", [P, SH, H])
        r1 = sb("r1", [P, SH, H])
        mx = sb("mx", [P, 2, SH, HU, len(c.M_CH)])
        top = sb("top", [P, SH, HU])
        rest = sb("rest", [P, SH, HU])
        parts = sb("parts", [P, NP, SH, c.parts, HU], BF16)
        rows = sb("rows", [P, 2, HU, S], BF16)
        probs = sb("probs", [P, P_SLOTS, W])
        on = sb("on", [P, NG, W if c.v_block == 128 else S])
        rden = sb("rden", [P, W if c.v_block == 128 else S])
        ft = sb("ft", [P, S])
        n_st = max(c.C, SH)
        st = {"six": sb("st_six", [P, n_st, 6]), "mv": sb("st_mv", [P, n_st, 2]), "var": sb("st_var", [P, n_st]),
              "rs": sb("st_rs", [P, n_st]), "tmp": sb("st_tmp", [P, n_st])}
        if c.ones_column:
            oraw = sb("oraw", [P, S])
        else:
            acc = sb("acc", [P, 2, W])
        if c.mask:
            mask_u8 = sb("mask_u8", [P, SH, J_CTX], U8)
            mask_n = sb("mask_n", [P, SH, JP], BF16)
            mask_t = sb("mask_t", [P, T, S], BF16)
            junk, stub = sb("junk", [P, 1024], BF16), sb("stub", [P, 1])

        score = [pb(f"score{k}", [P, 512]) for k in range(S_BANKS)]
        mpass = pb("mpass", [P, 1024])
        res = [pb(f"res{k}", [P, 512]) for k in range(2)]
        misc = pb("misc", [P, 512])
        misc_b = misc[:, :].bitcast(BF16)

        w_in, x_got, c_got = sem("w_in"), sem("x_got"), sem("c_got")
        zero_ok, const_ok, fold_mm, fold_ok = sem("zero_ok"), sem("const_ok"), sem("fold_mm"), sem("fold_ok")
        c_free, y_ok, src_ok, ktp_ok, kh_ok, kl_ok = [sem(n) for n in ("c_free", "y_ok", "src_ok", "ktp_ok", "kh_ok", "kl_ok")]
        ytp_ok, yt_ok, qp_ok, q_ok, qkp_ok, qh_ok, ql_ok = [sem(n) for n in (
            "ytp_ok", "yt_ok", "qp_ok", "q_ok", "qkp_ok", "qh_ok", "ql_ok")]
        qbp_ok, qb_ok, vp_ok, v_ok = [sem(n) for n in ("qbp_ok", "qb_ok", "vp_ok", "v_ok")]
        mp_ok, mred_ok, parts_ok, xt_ok, rows_ok = [sem(n) for n in ("mp_ok", "mred_ok", "parts_ok", "xt_ok", "rows_ok")]
        s_ok, exp_ok, pv_ok, acc_ok, oraw_ok, den_ok, on_ok = [sem(n) for n in (
            "s_ok", "exp_ok", "pv_ok", "acc_ok", "oraw_ok", "den_ok", "on_ok")]
        fp_ok, ft_ok, ftp_ok, xo_ok, x_put = [sem(n) for n in ("fp_ok", "ft_ok", "ftp_ok", "xo_ok", "x_put")]
        mn_ok, mtp_ok, mt_ok = [sem(n) for n in ("mn_ok", "mtp_ok", "mt_ok")]

        x_v = x_in.rearrange("(b h p) d -> b p h d", b=B, p=P)
        xo_v = x_out.rearrange("(b h p) d -> b p h d", b=B, p=P)
        C_DMAS = 3 if c.mask else 2

        block = done.enter_context(nc.Block())

        @block.sync
        def _(sp):
            for tile, dram in loads:
                sp.dma_start(tile[:], dram).then_inc(w_in, 16)

            def load_source(b):
                sp.dma_start(cx[:, 0:CT - 1, :],
                             io["ctx"][b, 0:(CT - 1) * P, :].rearrange("(t p) d -> p t d", p=P)).then_inc(c_got, 16)
                sp.dma_start(cx[0:CTAIL, CT - 1, :], io["ctx"][b, (CT - 1) * P:J_CTX, :]).then_inc(c_got, 16)
                if c.mask:
                    sp.dma_start(mask_u8[:, :, :],
                                 io["mask"][b].rearrange("(h p) j -> p h j", p=P)).then_inc(c_got, 16)

            if c.C:
                sp.wait_ge(zero_ok, 1)
                load_source(0)
            sp.dma_start(xin[:, :, :], x_v[0]).then_inc(x_got, 16)
            with sp.Fori(0, B - 1) as b:
                if c.C:
                    sp.wait_ge(c_free, b + 1)
                    load_source(b + 1)
                sp.wait_ge(xo_ok, b + 1)
                sp.dma_start(xo_v[b], xo[:, :, :]).then_inc(x_put, 16)
                sp.wait_ge(x_put, b * 16 + 16)
                sp.dma_start(xin[:, :, :], x_v[b + 1]).then_inc(x_got, 16)
            sp.wait_ge(xo_ok, B)
            sp.dma_start(xo_v[B - 1], xo[:, :, :]).then_inc(x_put, 16)
            sp.wait_ge(x_put, 16 * B)

        due = split_steps(NI, max(T - 4, 1)) + [0] * (T - max(T - 4, 1))
        v_due = split_steps(NI, c.NV) if c.NV else []

        @block.tensor
        def _(pe):
            pe.wait_ge(w_in, 16 * len(loads))
            pe.wait_ge(const_ok, 3)
            if c.fold_wo:
                for h in range(H):
                    if h >= 2:
                        pe.wait_ge(fold_ok, h - 1)
                    pe.matmul(score[h % 2][:, 0:P], wvt[:, h, :], wo[:, h, :], start=True, stop=True).then_inc(fold_mm, 1)
                for h in range(H):
                    mm = pe.matmul(misc[:, 0:1], wo[:, h, :], bvh[:, h:h + 1], start=(h == 0), stop=(h == H - 1))
                mm.then_inc(fold_mm, 1)
                pe.wait_ge(fold_ok, H + 1)

            with pe.Fori(0, B) as b:
                freed = []

                def claim(r):
                    if r >= S_BANKS and not (r >= u0 and freed[r - S_BANKS][0] is ql_ok):
                        who, per, k = freed[r - S_BANKS]
                        pe.wait_ge(who, b * per + k)
                    return score[r % S_BANKS]

                pe.wait_ge(src_ok, b + 1)
                for k in range(c.KB):
                    bank = claim(kt0 + k)
                    for t in range(4 * k, min(4 * k + 4, T)):
                        mm = pe.transpose(bank[:, (t % 4) * P:(t % 4 + 1) * P], ksrc[:, t, :], ident[:, :])
                    mm.then_inc(ktp_ok, 1)
                    freed.append((kl_ok, c.KB, k + 1))
                pe.wait_ge(y_ok, b + 1)
                for hf in range(SH):
                    mm = pe.transpose(misc[:, hf * P:(hf + 1) * P], y[:, hf, :], ident[:, :])
                mm.then_inc(ytp_ok, 1)
                pe.wait_ge(yt_ok, b + 1)
                for g in range(c.QG):
                    bank = claim(q0 + g)
                    pe.matmul(bank[:, 0:S], wq[:, g, :], yt[:, :], start=True, stop=True).then_inc(qp_ok, 1)
                    freed.append((q_ok, c.QG, g + 1))
                for p in range(NP):
                    bank = claim(qk0 + p)
                    for e in range(HU):
                        h = p * HU + e
                        pe.wait_ge(q_ok, b * c.QG + h * c.QG // H + 1)
                        mm = pe.matmul(bank[:, e * S:(e + 1) * S], wk[:, h, :], qt[:, h * c.QG // H, :], start=True, stop=True)
                    mm.then_inc(qkp_ok, 1)
                    freed.append((ql_ok, NP, p + 1))
                if c.key_bias:
                    hq = H // c.QG
                    for hf in range(SH):
                        for g in range(c.QG):
                            mm = pe.matmul(misc[:, hf * H + g * hq:hf * H + (g + 1) * hq], qt[:, g, hf * P:(hf + 1) * P],
                                           bk[:, g * hq:(g + 1) * hq], start=True, stop=True)
                    mm.then_inc(qbp_ok, 1)
                    pe.wait_ge(qb_ok, b + 1)
                if c.mask:
                    pe.wait_ge(mn_ok, b + 1)
                    for k in range(c.KB):
                        if k:
                            pe.wait_ge(mt_ok, b * c.KB + k)
                        for t in range(4 * k, min(4 * k + 4, T)):
                            for hf in range(SH):
                                n = (t % 4) * S + hf * P
                                mm = pe.transpose(misc_b[:, n:n + P], mask_n[:, hf, t * P:(t + 1) * P], ident_b[:, :])
                        mm.then_inc(mtp_ok, 1)
                    pe.wait_ge(mt_ok, b * c.KB + c.KB)

                def max_item(m):
                    p, (e, hf, ch) = m // NI, c.M_ITEMS[m % NI]
                    if m:
                        pe.wait_ge(mred_ok, b * NP * NI + m)
                    pe.wait_ge(qh_ok, b * NP + p + 1)
                    lo, hi = c.M_CH[ch]
                    q_at = (p * HU + e) * S + hf * P
                    for n in range(lo, hi, 512):
                        w = min(512, hi + hi % 2 - n)
                        mm = pe.matmul(mpass[:, n - lo:n - lo + w], q_hi[:, q_at:q_at + P], kt_hi[:, n:n + w],
                                       start=True, stop=True)
                    mm.then_inc(mp_ok, 1)

                pe.wait_ge(kl_ok, b * c.KB + c.KB)
                done = 0
                if c.NV:
                    for n in range(c.NV):
                        bank = claim(v0 + n)
                        t, part = n // (c.v_cols // 512), n % (c.v_cols // 512)
                        w = slice(part * 512, part * 512 + 512)
                        k = slice(t * P, t * P + P)
                        pe.matmul(bank[:, :], kt_hi[:, k], wv_hi[:, w], start=True, stop=False)
                        pe.matmul(bank[:, :], kt_lo[:, k], wv_hi[:, w], start=False, stop=False)
                        pe.matmul(bank[:, :], kt_hi[:, k], wv_lo[:, w], start=False, stop=True).then_inc(vp_ok, 1)
                        freed.append((v_ok, c.NV, n + 1))
                        for _ in range(v_due[n]):
                            max_item(done)
                            done += 1
                while done < NI:
                    max_item(done)
                    done += 1

                def turn_parts(p):
                    pe.wait_ge(parts_ok, b * NP + p + 1)
                    if p and (p - 1) // c.PPG and not (p - 1) % c.PPG:
                        pe.wait_ge(on_ok, b * NG + (p - 1) // c.PPG)
                    for hf in range(SH):
                        mm = pe.transpose(misc_b[0:c.K_ROWS, hf * P:(hf + 1) * P],
                                          parts[:, p, hf, :, :].rearrange("p k e -> p (k e)"), ident_b[:, :])
                    mm.then_inc(xt_ok, 1)

                def values(u):
                    p, t = u // T, u % T
                    g = p // c.PPG
                    rws = c.tail if t == T - 1 else P
                    pe.wait_ge(exp_ok, b * NU + u + 1)
                    if t == 0 and g >= 2:
                        pe.wait_ge(on_ok, b * NG + g - 1)
                    if u == 0 and c.NV:
                        pe.wait_ge(v_ok, b * c.NV + c.NV)
                    pr = probs[0:rws, u % P_SLOTS, :]
                    if c.v_block == 128:
                        mm = pe.matmul(res[g % 2][:, 0:W], v[0:rws, t, :], pr, start=(t == 0), stop=(t == T - 1))
                    else:
                        for e in range(HU):
                            h = p * HU + e
                            at = (h % (P // c.v_block)) * c.v_block
                            mm = pe.matmul(res[g % 2][at:at + c.v_block, 0:S], v[0:rws, t, h * c.v_block:(h + 1) * c.v_block],
                                           pr[:, e * S:(e + 1) * S], start=(t == 0), stop=(t == T - 1))
                    mm.then_inc(pv_ok, 1)

                def sums(g):
                    if g:
                        pe.wait_ge(on_ok, b * NG + g)
                    if c.ones_column:
                        pe.wait_ge(oraw_ok, b * NG + g + 1)
                        mm = pe.matmul(misc[:, 0:S], spread[:, :], oraw[:, :], start=True, stop=True)
                    else:
                        pe.wait_ge(acc_ok, b * NA + (g + 1) * (T - 1))
                        if c.v_block == 128:
                            mm = pe.matmul(misc[:, 0:W], ones_f[:, :], acc[:, g % 2, :], start=True, stop=True)
                        else:
                            for e in range(HU):
                                mm = pe.matmul(misc[e * c.v_block:(e + 1) * c.v_block, 0:S], ones_f[:, 0:c.v_block],
                                               acc[:, g % 2, e * S:(e + 1) * S], start=True, stop=True)
                    mm.then_inc(den_ok, 1)

                pe.wait_ge(ql_ok, b * NP + NP)
                turn_parts(0)
                m = NI
                for p in range(NP):
                    pe.wait_ge(rows_ok, b * NP + p + 1)
                    cols = slice(p * W, (p + 1) * W)
                    for t in range(T):
                        u = p * T + t
                        bank = claim(u0 + u)
                        k = slice(t * P, t * P + P)
                        pe.matmul(bank[:, 0:W], kt_hi[:, k], q_hi[:, cols], start=True, stop=False)
                        pe.matmul(bank[:, 0:W], kt_lo[:, k], q_hi[:, cols], start=False, stop=False)
                        pe.matmul(bank[:, 0:W], kt_hi[:, k], q_lo[:, cols], start=False, stop=False)
                        if c.mask:
                            pe.matmul(bank[:, :].rearrange("p (e s) -> p e s", e=HU), ident_b[:, :],
                                      mask_t[:, t, :].unsqueeze(1).broadcast_to([P, HU, S]), start=False, stop=False)
                        pe.matmul(bank[:, 0:W], ones_b[:, :], rows[:, p % 2, :, :].rearrange("p e s -> p (e s)"),
                                  start=False, stop=True).then_inc(s_ok, 1)
                        freed.append((exp_ok, NU, u + 1))
                        if u >= 2:
                            values(u - 2)
                        if t == 2 and p and p % c.PPG == 0:
                            sums(p // c.PPG - 1)
                        if p + 1 < NP:
                            for _ in range(due[t]):
                                max_item(m)
                                m += 1
                            if t == T - 1 - (T > 2):
                                if T == 2 and p and p % c.PPG == 0:
                                    sums(p // c.PPG - 1)
                                turn_parts(p + 1)
                    if T == 2 and p + 1 == NP and p % c.PPG == 0 and p:
                        sums(p // c.PPG - 1)
                values(NU - 2)
                values(NU - 1)
                sums(NG - 1)
                pe.wait_ge(on_ok, b * NG + NG)
                for k in range(c.FIN):
                    if c.v_block == 128 and HU == 2:
                        o = on[:, k // 2, (k % 2) * S:(k % 2 + 1) * S]
                    else:
                        o = on[:, k, 0:S]
                    mm = pe.matmul(misc[:, 0:S], wfin[:, k, :], o, start=(k == 0), stop=(k == c.FIN - 1))
                mm.then_inc(fp_ok, 1)
                pe.wait_ge(ft_ok, b + 1)
                for hf in range(SH):
                    mm = pe.transpose(misc[:, S + hf * P:S + (hf + 1) * P], ft[:, hf * P:(hf + 1) * P], ident[:, :])
                mm.then_inc(ftp_ok, 1)
                pe.wait_ge(xo_ok, b + 1)

        @block.scalar
        def _(act):
            with act.Fori(0, B) as b:
                for k in range(c.KB):
                    act.wait_ge(ktp_ok, b * c.KB + k + 1)
                    w = min(4, T - 4 * k) * P
                    act.activation(kt_hi[:, k * 512:k * 512 + w], score[(kt0 + k) % S_BANKS][:, 0:w],
                                   ACT.Copy).then_inc(kh_ok, 1)
                act.wait_ge(ytp_ok, b + 1)
                act.activation(yt[:, :], misc[:, 0:S], ACT.Copy).then_inc(yt_ok, 1)
                for p in range(NP):
                    act.wait_ge(qkp_ok, b * NP + p + 1)
                    act.activation(q_hi[:, p * W:(p + 1) * W], score[(qk0 + p) % S_BANKS][:, 0:W],
                                   ACT.Copy).then_inc(qh_ok, 1)
                if c.mask:
                    for k in range(c.KB):
                        act.wait_ge(mtp_ok, b * c.KB + k + 1)
                        n = min(4, T - 4 * k)
                        act.activation(mask_t[:, 4 * k:4 * k + n, :],
                                       misc_b[:, 0:n * S].rearrange("p (t s) -> p t s", s=S), ACT.Copy).then_inc(mt_ok, 1)
                for u in range(NU):
                    act.wait_ge(s_ok, b * NU + u + 1)
                    if u >= P_SLOTS:
                        act.wait_ge(pv_ok, b * NU + u - P_SLOTS + 1)
                        if not c.ones_column:
                            act.wait_ge(acc_ok, b * NA + summed(u - P_SLOTS))
                    act.activation(probs[:, u % P_SLOTS, :], score[(u0 + u) % S_BANKS][:, 0:W],
                                   ACT.Exp).then_inc(exp_ok, 1)

        @block.gpsimd
        def _(pool):
            pool.memset(ones_f[:, :], 1.0)
            if not c.ones_column:
                with pool.Fori(0, B) as b:
                    for u in range(NU):
                        p, t = u // T, u % T
                        rws = c.tail if t == T - 1 else P
                        if t:
                            pool.wait_ge(exp_ok, b * NU + u + 1)
                        if t == 1:
                            pool.tensor_tensor(acc[:, p % 2, :], probs[:, (u - 1) % P_SLOTS, :], probs[:, u % P_SLOTS, :],
                                               ALU.add).then_inc(acc_ok, 1)
                        elif t > 1:
                            pool.wait_ge(acc_ok, b * NA + p * (T - 1) + t - 1)
                            pool.tensor_tensor(acc[0:rws, p % 2, :], acc[0:rws, p % 2, :], probs[0:rws, u % P_SLOTS, :],
                                               ALU.add).then_inc(acc_ok, 1)

        def queries(dve, b):
            dve.wait_ge(x_got, b * 16 + 16)
            ins = normalise(dve, xn, xin, st, SH)
            if c.norms == 2:
                dve.drain()
                normalise(dve, y, xn, st, SH)
                dve.drain()
                ins = affine(dve, y[:, :, :], y[:, :, :], gx[:, :], bx[:, :], SH)
            ins.then_inc(y_ok, 1)
            if c.LT:
                dve.drain()
                dve.tensor_copy(src[:, 0:SH, :], y[:, :, :])
                dve.drain()

        @block.vector
        def _(dve):
            dve.memset(rows[:, :, :, :], 0.0)
            if c.mask:
                dve.memset(mask_n[:, :, :], 0.0)
            if c.C:
                dve.memset(cx[:, CT - 1, :], 0.0).then_inc(zero_ok, 1)
            dve.memset(ones_b[:, :], 1.0).then_inc(const_ok, 1)
            dve.wait_ge(w_in, 16 * len(loads))
            dve.tensor_copy(ident_b[:, :], ident[:, :]).then_inc(const_ok, 1)
            if c.v_cols:
                dve.tensor_copy(wv_hi[:, :], wv[:, :])
                dve.drain()
                dve.tensor_tensor(wv_lo[:, :], wv[:, :], wv_hi[:, :].bitcast(F32), ALU.subtract).then_inc(const_ok, 1)
            else:
                dve.nop().then_inc(const_ok, 1)
            if c.fold_wo:
                for h in range(H):
                    dve.wait_ge(fold_mm, h + 1)
                    dve.tensor_copy(wfin[:, h, :], score[h % 2][:, 0:P]).then_inc(fold_ok, 1)
                dve.wait_ge(fold_mm, H + 1)
                dve.tensor_tensor(bfin[:, :], misc[:, 0:1], bo[:, :], ALU.add).then_inc(fold_ok, 1)

            with dve.Fori(0, B) as b:
                if c.LT:
                    queries(dve, b)
                if c.C:
                    dve.wait_ge(c_got, b * 16 * C_DMAS + 16 * C_DMAS)
                if c.norm_source:
                    normalise(dve, src[:, c.LT:T, :], cx, st, CT).then_inc(c_free, 1)
                    dve.drain()
                    if c.k_affine:
                        affine(dve, ksrc[:, :, :], src[:, :, :], gk[:, :], bkk[:, :], CT).then_inc(src_ok, 1)
                        affine(dve, src[:, :, :], src[:, :, :], gv[:, :], bvv[:, :], CT)
                    else:
                        part = src[:, c.LT:T, :]
                        affine(dve, part, part, gk[:, :], bkk[:, :], CT).then_inc(src_ok, 1)
                else:
                    if c.mask:
                        dve.tensor_scalar(mask_n[:, :, 0:J_CTX], mask_u8[:, :, :], MASKED, -MASKED, ALU.mult,
                                          ALU.add).then_inc(mn_ok, 1)
                    dve.nop().then_inc(src_ok, 1)
                if not c.LT:
                    queries(dve, b)
                for k in range(c.KB):
                    dve.wait_ge(kh_ok, b * c.KB + k + 1)
                    w = min(4, T - 4 * k) * P
                    ins = dve.tensor_tensor(kt_lo[:, k * 512:k * 512 + w], score[(kt0 + k) % S_BANKS][:, 0:w],
                                            kt_hi[:, k * 512:k * 512 + w].bitcast(F32), ALU.subtract)
                    ins.then_inc(kl_ok, 1)
                if c.C and not c.norm_source:
                    dve.nop().then_inc(c_free, 1)
                for g in range(c.QG):
                    dve.wait_ge(qp_ok, b * c.QG + g + 1)
                    dve.tensor_scalar(qt[:, g, :], score[(q0 + g) % S_BANKS][:, 0:S], bq[:, g:g + 1], c.scale,
                                      ALU.add, ALU.mult).then_inc(q_ok, 1)
                for p in range(NP):
                    dve.wait_ge(qh_ok, b * NP + p + 1)
                    cols = slice(p * W, (p + 1) * W)
                    dve.tensor_tensor(q_lo[:, cols], score[(qk0 + p) % S_BANKS][:, 0:W], q_hi[:, cols].bitcast(F32),
                                      ALU.subtract).then_inc(ql_ok, 1)
                if c.key_bias:
                    view = lambda k: parts[:, :, :, k, :].rearrange("p n h e -> p h n e")
                    whole = lambda x: x[:, :, :].rearrange("p h (n e) -> p h n e", e=HU)
                    dve.wait_ge(qbp_ok, b + 1)
                    dve.tensor_copy(qb[:, :, :], misc[:, 0:SH * H].rearrange("p (h n) -> p h n", h=SH)).then_inc(qb_ok, 1)
                    dve.drain()
                    for hf in range(SH):
                        dve.tensor_copy(view(0)[:, hf], whole(qb)[:, hf])
                    dve.drain()
                    for hf in range(SH):
                        dve.tensor_tensor(whole(r1)[:, hf], whole(qb)[:, hf], view(0)[:, hf], ALU.subtract)
                    dve.drain()
                    for hf in range(SH):
                        dve.tensor_copy(view(1)[:, hf], whole(r1)[:, hf])
                    dve.drain()
                    for hf in range(SH):
                        dve.tensor_tensor(view(2)[:, hf], whole(r1)[:, hf], view(1)[:, hf], ALU.subtract)

                def max_item(m):
                    p, (e, hf, ch) = m // NI, c.M_ITEMS[m % NI]
                    lo, hi = c.M_CH[ch]
                    out = mx[:, p % 2, hf, e, ch:ch + 1]
                    dve.wait_ge(mp_ok, b * NP * NI + m + 1)
                    if c.mask:
                        dve.memset(stub[:, :], 0.0)
                        dve.tensor_tensor_reduce(junk[:, 0:hi - lo], mpass[:, 0:hi - lo], mask_n[:, hf, lo:hi], 1.0,
                                                 LOWEST, ALU.add, ALU.max, out).then_inc(mred_ok, 1)
                    else:
                        dve.tensor_reduce(out, mpass[:, 0:hi - lo], AX, ALU.max).then_inc(mred_ok, 1)

                def max_parts(p):
                    dve.drain()
                    dve.tensor_reduce(top[:, :, :], mx[:, p % 2, :, :, :], AX, ALU.max)
                    dve.drain()
                    if c.key_bias:
                        dve.tensor_tensor(top[:, :, :], top[:, :, :], qb[:, :, p * HU:(p + 1) * HU], ALU.add)
                        dve.drain()
                    k = c.parts - 2
                    dve.tensor_scalar(parts[:, p, :, k, :], top[:, :, :], -1.0, None, ALU.mult)
                    dve.drain()
                    dve.scalar_tensor_tensor(parts[:, p, :, k + 1, :], top[:, :, :], -1.0, parts[:, p, :, k, :],
                                             ALU.mult, ALU.subtract).then_inc(parts_ok, 1)

                def max_rows(p):
                    dve.wait_ge(xt_ok, b * NP + p + 1)
                    for e in range(HU):
                        ins = dve.tensor_scalar(rows[0:c.K_ROWS, p % 2, e, :], misc_b[0:c.K_ROWS, 0:S], pick[:, e:e + 1],
                                                None, ALU.mult)
                    ins.then_inc(rows_ok, 1)

                def results(g):
                    w = W if c.v_block == 128 else S
                    dve.wait_ge(pv_ok, b * NU + (g + 1) * c.PPG * T)
                    if c.ones_column:
                        dve.tensor_copy(oraw[:, :], res[g % 2][:, 0:S]).then_inc(oraw_ok, 1)
                    dve.wait_ge(den_ok, b * NG + g + 1)
                    dve.reciprocal(rden[:, :], misc[:, 0:w])
                    dve.drain()
                    dve.tensor_tensor(on[:, g, :], res[g % 2][:, 0:w], rden[:, :], ALU.mult).then_inc(on_ok, 1)

                done = 0
                for n in range(c.NV):
                    dve.wait_ge(vp_ok, b * c.NV + n + 1)
                    t, part = n // (c.v_cols // 512), n % (c.v_cols // 512)
                    w = slice(part * 512, part * 512 + 512)
                    dve.tensor_tensor(v[:, t, w], score[(v0 + n) % S_BANKS][:, :], bv[:, w], ALU.add).then_inc(v_ok, 1)
                    for _ in range(v_due[n]):
                        max_item(done)
                        done += 1
                while done < NI:
                    max_item(done)
                    done += 1
                max_parts(0)
                max_rows(0)
                m = NI
                for p in range(NP):
                    for t in range(T):
                        if t == 2 and p and p % c.PPG == 0:
                            results(p // c.PPG - 1)
                        if p + 1 < NP:
                            for _ in range(due[t]):
                                max_item(m)
                                m += 1
                            if t == T - 1 - (T > 2):
                                max_parts(p + 1)
                                if T == 2 and p and p % c.PPG == 0:
                                    results(p // c.PPG - 1)
                                max_rows(p + 1)
                    if T == 2 and p + 1 == NP and p % c.PPG == 0 and p:
                        results(p // c.PPG - 1)
                results(NG - 1)
                dve.wait_ge(fp_ok, b + 1)
                dve.tensor_scalar(ft[:, :], misc[:, 0:S], bfin[:, 0:1], None, ALU.add).then_inc(ft_ok, 1)
                dve.wait_ge(ftp_ok, b + 1)
                base = xn if c.keep_norm else xin
                dve.tensor_tensor(xo[:, :, :], misc[:, S:2 * S].rearrange("p (h d) -> p h d", h=SH), base[:, :, :],
                                  ALU.add).then_inc(xo_ok, 1)


class Mixture:

    def __init__(self, name, E, chunks, routed, act, fill=0.0, scale=1.0, top1=False):
        self.name, self.E = name, E
        self.KC, self.KR = chunks, routed
        self.act = act
        self.fill, self.scale = fill, scale
        self.top1 = top1
        self.SEL = max(1, min(E, routed))
        self.share = max(1, routed // E)


MIXTURES = {
    "L0f": Mixture("L0f", 16, 18, 16, "silu", fill=-1.0, scale=2.5),
    "L1f": Mixture("L1f", 16, 6, 4, "silu", fill=LOWEST),
    "L2f": Mixture("L2f", 16, 9, 8, "relu2", fill=0.0, scale=2.5),
    "L3f": Mixture("L3f", 8, 32, 32, "gelu", top1=True),
}
G = 4


def build_mixture(nc, c, io, x_in, x_out, x_more=None):
    E, KC, KR, CN = c.E, c.KC, c.KR, N_CHUNK
    a = lambda key: io[f"{c.name}_{key}"]
    gated = c.act == "silu"
    EG = E // G
    with ExitStack() as ctx, ExitStack() as done:
        done.callback(lambda: clear(nc, sems))
        sb = lambda name, shape, dt=F32: ctx.enter_context(nc.sbuf_tensor(f"{c.name}_{name}", shape, dt))
        pb = lambda name, shape, dt=F32: ctx.enter_context(nc.psum_tensor(f"{c.name}_{name}", shape, dt))
        sems = []

        def sem(name):
            sems.append(ctx.enter_context(nc.semaphore(f"{c.name}_{name}")))
            return sems[-1]

        ident = sb("ident", [P, P])
        ident_b = sb("ident_b", [P, P], BF16)
        wr = sb("wr", [P, E])
        rb = sb("rb", [P, E])
        lower, upper = sb("lower", [P, E, E]), sb("upper", [P, E, E])
        sel_f = sb("sel_f", [3 * E, c.SEL, P])
        sel = sb("sel", [3 * E, c.SEL, P], BF16)
        w1, w2 = sb("w1", [P, KC, P]), sb("w2", [P, KC, P])
        loads = [(ident, io["ident"]), (wr, a("wr")), (rb, a("rb")), (lower, a("lower")), (upper, a("upper")),
                 (sel_f, a("sel")), (w1, a("w1")), (w2, a("w2"))]
        if gated:
            wu = sb("wu", [P, KC, P])
            loads.append((wu, a("wu")))
        if x_more is not None:
            gx, bx = sb("gx", [P, D]), sb("bx", [P, D])
            loads += [(gx, a("gx")), (bx, a("bx"))]
        xin = sb("xin", [P, CTILES, D])
        more = sb("more", [P, CTILES, D]) if x_more is not None else None
        y = sb("y", [P, CTILES, D])
        xo = sb("xo", [P, CTILES, D])
        yt = sb("yt", [P, CHUNK])
        score = sb("score", [P, CTILES, E])
        choice = sb("choice", [P, CTILES, E])
        rank = sb("rank", [P, CTILES, E])
        kept = sb("kept", [P, CTILES, E])
        pair = sb("pair", [P, CTILES, E, E])
        pair2 = sb("pair2", [P, CTILES, E, E])
        gsum = sb("gsum", [P, CTILES, G])
        wsum = sb("wsum", [P, CTILES, 1])
        comb = sb("comb", [P, CTILES, E])
        cparts = sb("cparts", [P, CTILES, P], BF16)
        cpart = lambda k: cparts[:, :, k * E:(k + 1) * E]
        ct = sb("ct", [3 * E, CHUNK], BF16)
        g1 = sb("g1", [P, 2, CHUNK])
        hid = sb("hid", [P, 2, CHUNK])
        ft = sb("ft", [P, CHUNK])
        st = {"six": sb("st_six", [P, CTILES, 6]), "mv": sb("st_mv", [P, CTILES, 2]), "var": sb("st_var", [P, CTILES]),
              "rs": sb("st_rs", [P, CTILES]), "tmp": sb("st_tmp", [P, CTILES])}
        hp = [pb(f"hp{k}", [P, CHUNK]) for k in range(2)]
        up = [pb(f"up{k}", [P, CHUNK]) for k in range(2)]
        wp = [pb(f"wp{k}", [P, CHUNK]) for k in range(2)]
        yp = pb("yp", [P, CHUNK])
        misc = pb("misc", [P, CHUNK])
        misc_b = misc[:, :].bitcast(BF16)

        w_in, x_got, const_ok, y_ok, ytp_ok, yt_ok, lg_ok, sc_ok, cp_ok, ctp_ok, ct_ok = [sem(n) for n in (
            "w_in", "x_got", "const_ok", "y_ok", "ytp_ok", "yt_ok", "lg_ok", "sc_ok", "cp_ok", "ctp_ok", "ct_ok")]
        hp_ok, g1_ok, hid_ok, dn_ok, ft_ok, ftp_ok, xo_ok, x_put = [sem(n) for n in (
            "hp_ok", "g1_ok", "hid_ok", "dn_ok", "ft_ok", "ftp_ok", "xo_ok", "x_put")]
        view = lambda x: x.rearrange("(c t p) d -> c p t d", t=CTILES, p=P)
        X_DMAS = 2 if x_more is not None else 1

        block = done.enter_context(nc.Block())

        @block.sync
        def _(sp):
            def load_x(n):
                sp.dma_start(xin[:, :, :], view(x_in)[n]).then_inc(x_got, 16)
                if x_more is not None:
                    sp.dma_start(more[:, :, :], view(x_more)[n]).then_inc(x_got, 16)

            load_x(0)
            for tile, dram in loads:
                sp.dma_start(tile[:], dram).then_inc(w_in, 16)
            with sp.Fori(0, CN - 1) as n:
                sp.wait_ge(xo_ok, n + 1)
                sp.dma_start(view(x_out)[n], xo[:, :, :]).then_inc(x_put, 16)
                sp.wait_ge(x_put, n * 16 + 16)
                load_x(n + 1)
            sp.wait_ge(xo_ok, CN)
            sp.dma_start(view(x_out)[CN - 1], xo[:, :, :]).then_inc(x_put, 16)
            sp.wait_ge(x_put, 16 * CN)

        @block.tensor
        def _(pe):
            pe.wait_ge(w_in, 16 * len(loads))
            pe.wait_ge(const_ok, 1)
            with pe.Fori(0, CN) as n:
                pe.wait_ge(y_ok, n + 1)
                for t in range(CTILES):
                    mm = pe.transpose(misc[:, t * P:(t + 1) * P], y[:, t, :], ident[:, :])
                mm.then_inc(ytp_ok, 1)
                pe.wait_ge(yt_ok, n + 1)
                for t in range(CTILES):
                    mm = pe.matmul(misc[:, t * E:(t + 1) * E], yt[:, t * P:(t + 1) * P], wr[:, :], start=True, stop=True)
                mm.then_inc(lg_ok, 1)

                def up_products(k):
                    if k >= 2:
                        pe.wait_ge(hid_ok, n * KC + k - 1)
                    mm = pe.matmul(hp[k % 2][:, :], w1[:, k, :], yt[:, :], start=True, stop=True)
                    if gated:
                        mm = pe.matmul(up[k % 2][:, :], wu[:, k, :], yt[:, :], start=True, stop=True)
                    if k < KR:
                        if k == 0:
                            pe.wait_ge(cp_ok, n + 1)
                            for t in range(CTILES):
                                pe_t = pe.transpose(misc_b[:, t * P:(t + 1) * P], cparts[:, t, :], ident_b[:, :])
                            pe_t.then_inc(ctp_ok, 1)
                            pe.wait_ge(ct_ok, n + 1)
                        mm = pe.matmul(wp[k % 2][:, :], sel[:, k // c.share, :], ct[:, :], start=True, stop=True)
                    mm.then_inc(hp_ok, 1)

                def down_product(k):
                    pe.wait_ge(hid_ok, n * KC + k + 1)
                    pe.matmul(yp[:, :], w2[:, k, :], hid[:, k % 2, :], start=(k == 0), stop=(k == KC - 1)).then_inc(dn_ok, 1)

                for k in range(KC):
                    up_products(k)
                    if k:
                        down_product(k - 1)
                down_product(KC - 1)
                pe.wait_ge(ft_ok, n + 1)
                for t in range(CTILES):
                    mm = pe.transpose(misc[:, t * P:(t + 1) * P], ft[:, t * P:(t + 1) * P], ident[:, :])
                mm.then_inc(ftp_ok, 1)
                pe.wait_ge(xo_ok, n + 1)

        @block.scalar
        def _(act):
            with act.Fori(0, CN) as n:
                act.wait_ge(ytp_ok, n + 1)
                act.activation(yt[:, :], misc[:, :], ACT.Copy).then_inc(yt_ok, 1)
                act.wait_ge(lg_ok, n + 1)
                act.activation(score[:, :, :], misc[:, 0:CTILES * E].rearrange("p (t e) -> p t e", t=CTILES),
                               ACT.Copy if c.top1 else ACT.Sigmoid).then_inc(sc_ok, 1)
                func = {"silu": ACT.Sigmoid, "relu2": ACT.Relu, "gelu": ACT.Gelu_apprx_tanh}[c.act]
                for k in range(KC):
                    act.wait_ge(hp_ok, n * KC + k + 1)
                    if k >= 2:
                        act.wait_ge(hid_ok, n * KC + k - 1)
                    act.activation(g1[:, k % 2, :], hp[k % 2][:, :], func).then_inc(g1_ok, 1)
                act.wait_ge(dn_ok, n * KC + KC)
                act.activation(ft[:, :], yp[:, :], ACT.Copy).then_inc(ft_ok, 1)

        def group_ranks(dve):
            v4 = lambda x: x[:, :, :].rearrange("p t (g k) -> p (t g) k", g=G)
            cv, rv = v4(choice), v4(rank)
            tmp = pair[:, :, :, :].rearrange("p t a b -> p (t a b)")
            n = CTILES * G
            for i in range(EG):
                others = [j for j in range(EG) if j != i]
                for q, j in enumerate(others):
                    slot = tmp[:, (i * EG + q) * n:(i * EG + q + 1) * n]
                    dve.tensor_tensor(slot, cv[:, :, j], cv[:, :, i], ALU.is_ge if j < i else ALU.is_gt)
            dve.drain()
            cell = lambda i, q: tmp[:, (i * EG + q) * n:(i * EG + q + 1) * n]
            for i in range(EG):
                dve.tensor_tensor(cell(i, 0), cell(i, 0), cell(i, 1), ALU.add)
            dve.drain()
            for i in range(EG):
                dve.tensor_tensor(rv[:, :, i], cell(i, 0), cell(i, 2), ALU.add)
            dve.drain()

        @block.vector
        def _(dve):
            dve.memset(cparts[:, :, :], 0.0)
            dve.drain()
            dve.wait_ge(w_in, 16 * len(loads))
            dve.tensor_copy(sel[:, :, :], sel_f[:, :, :])
            dve.tensor_copy(ident_b[:, :], ident[:, :]).then_inc(const_ok, 1)

            def ranks(x, w, n_t, out, scratch, scratch2):
                mine = x.unsqueeze(3).broadcast_to([P, n_t, w, w])
                others = x.unsqueeze(2).broadcast_to([P, n_t, w, w])
                s1, s2 = scratch[:, 0:n_t, 0:w, 0:w], scratch2[:, 0:n_t, 0:w, 0:w]
                low = lower[:, 0:w, 0:w].unsqueeze(1).broadcast_to([P, n_t, w, w])
                upp = upper[:, 0:w, 0:w].unsqueeze(1).broadcast_to([P, n_t, w, w])
                for t in range(n_t):
                    dve.tensor_tensor(s1[:, t], others[:, t], mine[:, t], ALU.is_ge)
                    dve.tensor_tensor(s2[:, t], others[:, t], mine[:, t], ALU.is_gt)
                dve.drain()
                for t in range(n_t):
                    dve.tensor_tensor(s1[:, t], s1[:, t], low[:, t], ALU.mult)
                    dve.tensor_tensor(s2[:, t], s2[:, t], upp[:, t], ALU.mult)
                dve.drain()
                for t in range(n_t):
                    dve.tensor_tensor(s1[:, t], s1[:, t], s2[:, t], ALU.add)
                dve.drain()
                for t in range(n_t):
                    dve.tensor_reduce(out[:, t], s1[:, t], AX, ALU.add)
                dve.drain()

            with dve.Fori(0, CN) as n:
                dve.wait_ge(x_got, n * 16 * X_DMAS + 16 * X_DMAS)
                ins = normalise(dve, y, xin, st, CTILES)
                if x_more is not None:
                    dve.drain()
                    ins = affine(dve, y[:, :, :], y[:, :, :], gx[:, :], bx[:, :], CTILES)
                ins.then_inc(y_ok, 1)
                dve.wait_ge(sc_ok, n + 1)
                bias = rb[:, :].unsqueeze(1).broadcast_to([P, CTILES, E])
                dve.tensor_tensor(choice[:, :, :], score[:, :, :], bias, ALU.add)
                dve.drain()
                if c.top1:
                    ranks(choice[:, :, :], E, CTILES, rank[:, :, :], pair, pair2)
                    dve.tensor_scalar(comb[:, :, :], rank[:, :, :], 0.5, None, ALU.is_lt)
                    dve.drain()
                else:
                    group_ranks(dve)
                    dve.tensor_scalar(kept[:, :, :], rank[:, :, :], 1.5, None, ALU.is_lt)
                    dve.drain()
                    dve.tensor_tensor(kept[:, :, :], kept[:, :, :], choice[:, :, :], ALU.mult)
                    dve.drain()
                    dve.tensor_reduce(gsum[:, :, :], kept[:, :, :].rearrange("p t (g k) -> p t g k", g=G), AX, ALU.add)
                    dve.drain()
                    ranks(gsum[:, :, :], G, CTILES, rank[:, :, 0:G], pair, pair2)
                    dve.tensor_scalar(gsum[:, :, :], rank[:, :, 0:G], 1.5, None, ALU.is_lt)
                    dve.drain()
                    for k in range(EG):
                        dve.tensor_copy(kept[:, :, :].rearrange("p t (g k) -> p t g k", g=G)[:, :, :, k], gsum[:, :, :])
                    dve.drain()
                    dve.tensor_tensor(choice[:, :, :], choice[:, :, :], kept[:, :, :], ALU.mult)
                    dve.tensor_scalar(kept[:, :, :], kept[:, :, :], -c.fill, c.fill, ALU.mult, ALU.add)
                    dve.drain()
                    dve.tensor_tensor(choice[:, :, :], choice[:, :, :], kept[:, :, :], ALU.add)
                    dve.drain()
                    ranks(choice[:, :, :], E, CTILES, rank[:, :, :], pair, pair2)
                    dve.scalar_tensor_tensor(comb[:, :, :], rank[:, :, :], 3.5, score[:, :, :], ALU.is_lt, ALU.mult)
                    dve.drain()
                    dve.tensor_reduce(wsum[:, :, 0], comb[:, :, :], AX, ALU.add)
                    dve.drain()
                    dve.tensor_scalar(wsum[:, :, :], wsum[:, :, :], 1e-20, None, ALU.add)
                    dve.drain()
                    dve.reciprocal(wsum[:, :, :], wsum[:, :, :])
                    dve.drain()
                    dve.tensor_scalar(wsum[:, :, :], wsum[:, :, :], c.scale, None, ALU.mult)
                    dve.drain()
                    dve.tensor_tensor(comb[:, :, :], comb[:, :, :], wsum[:, :, :].broadcast_to([P, CTILES, E]), ALU.mult)
                    dve.drain()
                dve.tensor_copy(cpart(0), comb[:, :, :])
                dve.drain()
                dve.tensor_tensor(comb[:, :, :], comb[:, :, :], cpart(0), ALU.subtract)
                dve.drain()
                dve.tensor_copy(cpart(1), comb[:, :, :])
                dve.drain()
                dve.tensor_tensor(cpart(2), comb[:, :, :], cpart(1), ALU.subtract).then_inc(cp_ok, 1)
                dve.wait_ge(ctp_ok, n + 1)
                dve.tensor_copy(ct[:, :], misc_b[0:3 * E, 0:CHUNK]).then_inc(ct_ok, 1)
                for k in range(KC):
                    dve.wait_ge(g1_ok, n * KC + k + 1)
                    if k >= 2:
                        dve.wait_ge(dn_ok, n * KC + k - 1)
                    gk, hk = g1[:, k % 2, :], hid[:, k % 2, :]
                    routed = k < KR
                    if c.act == "silu":
                        dve.tensor_tensor(gk, hp[k % 2][:, :], gk, ALU.mult)
                        dve.drain()
                        ins = dve.tensor_tensor(hk, up[k % 2][:, :], gk, ALU.mult)
                        if routed:
                            dve.drain()
                            ins = dve.tensor_tensor(hk, wp[k % 2][:, :], hk, ALU.mult)
                    elif c.act == "relu2":
                        ins = dve.tensor_tensor(hk, gk, gk, ALU.mult)
                        if routed:
                            dve.drain()
                            ins = dve.tensor_tensor(hk, wp[k % 2][:, :], hk, ALU.mult)
                    else:
                        ins = dve.tensor_tensor(hk, wp[k % 2][:, :], gk, ALU.mult)
                    ins.then_inc(hid_ok, 1)
                dve.wait_ge(ftp_ok, n + 1)
                if x_more is not None:
                    dve.tensor_tensor(xin[:, :, :], xin[:, :, :], more[:, :, :], ALU.add)
                    dve.drain()
                dve.tensor_tensor(xo[:, :, :], misc[:, :].rearrange("p (t d) -> p t d", t=CTILES), xin[:, :, :],
                                  ALU.add).then_inc(xo_ok, 1)


PHASES = ["L0a", "L0f", "L1a", "L1f", "L2a", "L2f", "L3a", "L3s", "L3f"]


def build(nc, io, out, phases=PHASES):
    x, before = io["x"], {}
    for n, name in enumerate(phases):
        last = n == len(phases) - 1
        x_out = out if last else nc.dram_tensor(f"x_{name}", [N_TOK, D], F32, kind="Internal").ap()
        before[name] = x
        if name in ATTENTIONS:
            build_attention(nc, ATTENTIONS[name], io, x, x_out)
        else:
            more = None
            if name == "L3f":
                more = before.get("L3s", io.get("x_more"))
            build_mixture(nc, MIXTURES[name], io, x, x_out, more)
        x = x_out


def layout(i):
    f = lambda k: np.asarray(i[k])
    c = np.ascontiguousarray
    zeros = lambda *s: np.zeros(s, np.float32)
    io = {"x": c(f("x").reshape(N_TOK, D)), "ctx": f("ctx_1024"), "mask": f("mask_BxSxS2_bk0"),
          "ident": np.eye(P, dtype=np.float32)}
    row = lambda v: c(np.broadcast_to(v, (P, v.shape[-1])))
    spread = zeros(P, P)
    for k in range(4):
        spread[32 * k + 8, 32 * k:32 * k + 32] = 1
    io["spread"] = spread

    def put(name, **arrays):
        for k, v in arrays.items():
            io[f"{name}_{k}"] = c(v)

    for name, a in ATTENTIONS.items():
        pick = zeros(a.parts, a.HU, a.HU)
        for e in range(a.HU):
            pick[:, e, e] = 1
        put(name, pick=pick.reshape(a.K_ROWS, a.HU))
    def key_weights(wk, heads, dh):
        tiles = heads * dh // P
        out = zeros(P, heads, P)
        for h in range(heads):
            r = (h * dh) % P
            out[r:r + dh, h, :] = wk[:, h * dh:(h + 1) * dh].T
        return out

    def key_bias(bk, heads, dh):
        out = zeros(P, heads)
        for h in range(heads):
            r = (h * dh) % P
            out[r:r + dh, h] = bk[h * dh:(h + 1) * dh]
        return out

    def small_values(wv, bv):
        w, b = zeros(P, 16, 32), zeros(16, 32)
        w[:, :, 0:8] = wv.reshape(P, 16, 8)
        if bv is not None:
            b[:, 0:8] = bv.reshape(16, 8)
        b[:, 8] = 1
        return w.reshape(P, 512), row(b.reshape(512))

    def small_out(wo):
        w = zeros(4, 4, 32, P)
        w[:, :, 0:8, :] = wo.reshape(4, 4, 8, P)
        return w.reshape(4, P, P).transpose(1, 0, 2)

    g = lambda k: f("L0_xattn_" + k)
    put("L0a", wq=g("Wq").T.reshape(P, 1, P), bq=g("bq").reshape(P, 1), wk=g("Wk").reshape(P, 1, P),
        bk=g("bk").reshape(P, 1), wfin=g("Wv").T.reshape(P, 1, P), bfin=g("bv").reshape(P, 1), gx=row(g("g_t")),
        bx=row(g("b_t")), gk=row(g("g_k")), bkk=row(g("b_k")), gv=row(g("g_v")), bvv=row(g("b_v")))
    g = lambda k: f("L1_xattn_" + k)
    wv, bv = small_values(g("Wv"), g("bv"))
    put("L1a", wq=g("Wq").reshape(P, 1, P), bq=g("bq").reshape(P, 1), wk=key_weights(g("Wk"), 16, 8),
        bk=key_bias(g("bk"), 16, 8), wv=wv, bv=bv, wfin=small_out(g("Wo")), bfin=g("bo").reshape(P, 1))
    g = lambda k: f("L2_xattn_" + k)
    put("L2a", wq=g("Wq").reshape(P, 8, P), bq=g("bq").reshape(8, P).T, wk=key_weights(g("Wk"), 16, 64),
        bk=key_bias(g("bk"), 16, 64), wv=g("Wv"), bv=row(g("bv")), wfin=g("Wo").reshape(8, P, P).transpose(1, 0, 2),
        bfin=g("bo").reshape(P, 1))
    g = lambda k: f("L3_xattn_" + k)
    wkv, bkv = g("Wkv"), g("bkv")
    put("L3a", wq=g("Wq").reshape(P, 8, P), bq=g("bq").reshape(8, P).T, wk=key_weights(wkv[:, 0:1024], 8, 128),
        bk=key_bias(bkv[0:1024], 8, 128), wvt=wkv[:, 1024:].reshape(P, 8, P).transpose(2, 1, 0),
        bvh=bkv[1024:].reshape(8, P).T, wo=g("Wo").reshape(8, P, P).transpose(1, 0, 2), bo=g("bo").reshape(P, 1),
        gx=row(g("gamma_lat")), bx=row(g("beta_lat")), gk=row(g("gamma_media")), bkk=row(g("beta_media")))
    g = lambda k: f("L3_ffn_" + k)
    wv, bv = small_values(g("w_qkv")[:, 256:384], None)
    put("L3s", wq=g("w_qkv")[:, 0:128].reshape(P, 1, P), bq=zeros(P, 1), wk=key_weights(g("w_qkv")[:, 128:256], 16, 8),
        wv=wv, bv=bv, wfin=small_out(g("w_proj")), bfin=zeros(P, 1), gx=row(g("ln1_w")), bx=row(g("ln1_b")))

    for name, m in MIXTURES.items():
        E = m.E
        lower, sel = np.tril(np.ones((E, E), np.float32), -1), zeros(3, E, m.SEL, P)
        per = max(1, E // m.SEL)
        for k in range(m.SEL):
            for q in range(per):
                w = P // per
                sel[:, k * per + q, k, q * w:(q + 1) * w] = 1
        put(name, lower=np.broadcast_to(lower, (P, E, E)), upper=np.broadcast_to(lower.T, (P, E, E)),
            sel=sel.reshape(3 * E, m.SEL, P))
    first = lambda w: w.transpose(1, 0, 2).reshape(P, -1)
    second = lambda w: w.reshape(-1, P, P).transpose(1, 0, 2)
    tiles = lambda w: w.reshape(P, -1, P)
    g = lambda k: f("L0_ffn_" + k)
    put("L0f", wr=g("router_w").T, rb=row(g("bias")), w1=tiles(np.concatenate([first(g("gate_w")), g("sh_gate_w")], 1)),
        wu=tiles(np.concatenate([first(g("up_w")), g("sh_up_w")], 1)),
        w2=second(np.concatenate([g("down_w").reshape(-1, P), g("sh_down_w")], 0)))
    g = lambda k: f("L1_ffn_" + k)
    put("L1f", wr=g("router_w").T, rb=row(g("correction_bias")),
        w1=tiles(np.concatenate([first(g("gate_w")), g("shared_gate_w").T], 1)),
        wu=tiles(np.concatenate([first(g("up_w")), g("shared_up_w").T], 1)),
        w2=second(np.concatenate([g("down_w").reshape(-1, P), g("shared_down_w").T], 0)))
    g = lambda k: f("L2_ffn_" + k)
    put("L2f", wr=g("Wg").T, rb=row(g("bias_corr")),
        w1=tiles(np.concatenate([g("W1").transpose(2, 0, 1).reshape(P, -1), g("Ws1").T], 1)),
        w2=second(np.concatenate([g("W2").transpose(0, 2, 1).reshape(-1, P), g("Ws2").T], 0)))
    g = lambda k: f("L3_ffn_" + k)
    put("L3f", wr=g("gate_w"), rb=row(g("gate_b")), w1=tiles(first(g("w1"))), w2=second(g("w2").reshape(-1, P)),
        gx=row(g("ln2_w")), bx=row(g("ln2_b")))
    return io


def kernel(**inputs):
    import concourse.bacc as bacc
    from concourse.bass_utils import run_bass_kernel_spmd

    arrays = layout(inputs)
    nc = bacc.Bacc("TRN2", target_bir_lowering=False, num_devices=1)
    io = {k: nc.dram_tensor(f"in_{k}", v.shape, mybir.dt.from_np(v.dtype), kind="ExternalInput").ap()
          for k, v in arrays.items()}
    out = nc.dram_tensor("out_x", [N_TOK, D], F32, kind="ExternalOutput").ap()
    build(nc, io, out)
    got = run_bass_kernel_spmd(nc, [{f"in_{k}": v for k, v in arrays.items()}], core_ids=[0])
    return got.results[0]["out_x"].reshape(B, S, D)
```

```python
from contextlib import ExitStack

import numpy as np

import concourse.bass as bass
from concourse import mybir

F32 = mybir.dt.float32
F32R = mybir.dt.float32r
BF16 = mybir.dt.bfloat16
I32 = mybir.dt.int32
U8 = mybir.dt.uint8
ALU = mybir.AluOpType
ACT = mybir.ActivationFunctionType
AX = mybir.AxisListType.X

P = 128
D = 128
B = 8
S = 256
SH = S // P
J_CTX = 1601
CT = -(-J_CTX // P)
CTAIL = J_CTX - (CT - 1) * P
N_TOK = B * S
CHUNK = 512
CTILES = CHUNK // P
N_CHUNK = N_TOK // CHUNK
EPS = 1e-5
MASKED = 1e30
LOWEST = -3.0e38


class Attention:

    def __init__(self, name, heads, head_dim, context=True, latents=False, norm_source=False, norms=1, v_cols=0,
                 v_block=128, key_bias=True, mask=False, own_affine=False, k_affine=False, fold_wo=False,
                 keep_norm=False, stacked=False):
        self.name, self.H, self.dh = name, heads, head_dim
        self.LT = SH if latents else 0
        self.C = CT if context else 0
        self.T = self.LT + self.C
        self.J = (S if latents else 0) + (J_CTX if context else 0)
        self.norm_source = norm_source
        self.k_affine = k_affine
        self.norms = norms
        self.own_affine = own_affine
        self.keep_norm = keep_norm
        self.v_cols = v_cols
        self.v_block = v_block
        self.VB = v_cols // 2
        self.stacked = stacked
        self.key_bias = key_bias and not stacked
        self.mask = mask
        self.fold_wo = fold_wo
        self.HU = min(heads, 2)
        self.W = self.HU * S
        self.NP = heads // self.HU
        self.QG = 4 if stacked else heads * head_dim // P
        self.PPG = 2 if v_block == 32 else 1
        self.NG = self.NP // self.PPG
        self.NU = self.NP * self.T
        self.parts = (3 if self.key_bias else 0) + 2
        self.K_ROWS = self.parts * self.HU
        self.scale = float(head_dim) ** -0.5
        self.ones_column = v_block == 32
        self.small = self.J <= S
        n_ch = -(-self.J // 512)
        step = -(-self.J // n_ch)
        step += step % 2
        self.M_CH = [(c, min(c + step, self.J)) for c in range(0, self.J, step)]
        self.M_ITEMS = [(0, hf, 0) for hf in range(SH)] if self.small else [
            (e, hf, c) for e in range(self.HU) for hf in range(SH) for c in range(len(self.M_CH))]
        self.NI = len(self.M_ITEMS)
        self.KB = -(-self.T // 4)
        self.FIN = heads if fold_wo else self.NG
        self.tail = CTAIL if context else P
        self.RP = 4
        self.QS = 8 if self.small else 2 if self.NP == 1 else 4
        self.PS = 2 if self.NU % 2 else 4
        self.slots = self.plan()
        self.count()
        self.late = self.readers()

    def plan(self):
        T, NP, NU, NI = self.T, self.NP, self.NU, self.NI
        slots = [[] for _ in range(NU)]

        def put(u, kind, off, n=0):
            slots[u].append((kind, off, n))

        for u in range(NU):
            put(u, "values", 0 if u >= 2 else -1, (u - 2) % NU)
        for g in range(self.NG):
            at = lambda k: (((g + 1) * self.PPG * T + 2 + k) % NU, -1 if (g + 1) * self.PPG * T + 2 + k >= NU else 0)
            for kind, k, n in [("results", 0, g)] + [
                    ("recip", 2 + (i // 2 if self.small else i), (g, i)) for i in range(self.RP)] + [
                    ("scale", 3 if self.small else 6, g)]:
                u, off = at(k)
                put(u, kind, off, n)
        put(7 if self.small else 9, "project", -1)
        put(9 if self.small else 11, "finish", -1)
        if self.name == "L0a":
            put(0, "norm_x", 1)
            for t in range(CT):
                put(t // 5, "stats", 1, t)
            put(2, "rstd", 1)
            put(3, "turn_x", 1)
            put(5, "query", 1, 0)
            put(6, "query_bias", 1)
            for k in range(self.KB):
                put(3 + k, "norm_c", 1, k)
                put(4 + k, "turn_c", 1, k)
            put(7, "keyed", 1, 0)
            for i in range(NI):
                put(9 + i * 2 // NI, "max", 1, i)
            put(10, "max_parts", 1, 0)
            put(11, "max_rows", 1, 0)
            return slots
        first = lambda p, t: p * T + t
        if self.small:
            put(3, "norm_x", 1)
            put(4, "turn_x", 1)
            put(5, "turn_c", 1, 0)
            put(11, "keep", 1)
            for g, u in enumerate((6, 8, 11, 12)):
                put(u, "query", 1, g)
            for g, u in enumerate((8, 10, 12)):
                put(u, "keys", 1, g)
            put(1, "keys", 0, 3)
            for t in range(T):
                put(2 * t, "value_tile", 0, (1, t))
                put(13 + t, "value_tile", 1, (0, t))
            for p in range(NP):
                at = lambda q: (0, q) if q < NP else (1, q - NP)
                put(first(p, 0), "keyed", *at(p + 4))
                off, q = at(p + 3)
                for i in range(NI):
                    put(first(p, i), "max", off, q * NI + i)
                put(first(p, 1), "max_parts", off, q)
                put(first(p, 1), "max_rows", *at(p + 2))
        else:
            put(first(0, 8), "norm_x", 1)
            if self.norm_source:
                for t in range(CT):
                    put(first(0, 1 + t), "stats", 1, t)
                put(first(0, 14), "rstd", 1)
                for k in range(self.KB):
                    put(first(1, 1 + 3 * k), "norm_c", 1, k)
                    put(first(1, 3 + 3 * k), "turn_c", 1, k)
            else:
                for k in range(self.KB):
                    put(first(1, 1 + 3 * k), "turn_c", 1, k)
            put(first(0, 12), "turn_x", 1)
            if self.stacked:
                n = -(-self.J // 512)
                for g in range(4):
                    for k in range(n):
                        if g < 3:
                            put(first(2 * g + 2, 1 + 3 * k), "keys", 1, g * n + k)
                        else:
                            put(first(1, 2 + 3 * k), "keys", 0, g * n + k)
            if self.v_cols:
                for t in range(T):
                    put(3 + t * (4 * T - 8) // T, "value_tile", 0, (1, t))
                    put(first(4, 2) + t * (4 * T - 8) // T, "value_tile", 1, (0, t))
            for g in range(self.QG):
                put(first(NP - 3, 3 + g), "query", 1, g)
            for p in range(NP):
                off, q = (0, p + 2) if p + 2 < NP else (1, p + 2 - NP)
                put(first(p, 0), "keyed", off, q)
                off, q = (0, p + 1) if p + 1 < NP else (1, 0)
                for i in range(NI):
                    put(first(p, 1 + i * (T - 4) // NI), "max", off, q * NI + i)
                put(first(p, T - 3), "max_parts", off, q)
                put(first(p, T - 2), "max_rows", off, q)
        if self.key_bias:
            put(first(NP - 1, 1), "query_bias", 1)
        if self.mask:
            for hf in range(SH):
                put(first(NP - 1, hf), "mask", 1, hf)
            for k in range(self.KB):
                put(first(NP - 1, 3 + 2 * k), "turn_mask", 1, k)
        order = {"mask": 0, "values": 2, "max": 3}
        for u in range(NU):
            slots[u].sort(key=lambda a: 5 if a == ("keyed", 1, 0) else order.get(a[0], 4))
            first_max = next((k for k, a in enumerate(slots[u]) if a[0] == "max"), None)
            if first_max is not None:
                slots[u].insert(0, slots[u].pop(first_max))
        aux = self.PREP + self.MISC
        assert all(sum(a[0] in aux and not (self.stacked and a[0] == "keyed") for a in s) <= 2 for s in slots)
        return slots

    PREP = ("turn_x", "query", "query_bias", "turn_c", "keyed", "keys", "value_tile", "turn_mask")
    MISC = ("max_rows", "results", "project", "finish")

    def count(self):
        kinds = [k for k in self.PREP + self.MISC if not (self.stacked and k == "keyed")]
        uses = [(a[0], a[2]) for s in self.slots for a in s if a[0] in kinds]
        self.bank = {use: k % 2 for k, use in enumerate(uses)}
        self.numbered = {}
        for what in (0, 1, "split"):
            split = ("turn_c", "query", "keys") if self.stacked else ("turn_c", "keyed")
            plan = [a for s in self.slots for a in s
                    if (a[0] in split if what == "split" else self.bank.get((a[0], a[2])) == what)]
            among = lambda *offs: {(a[0], a[2]): k for k, a in enumerate([a for a in plan if a[1] in offs])}
            off = {(a[0], a[2]): a[1] for a in plan}
            self.numbered[what] = off, [among(1), among(0, 1), among(-1, 0, 1), among(-1, 0), among(-1)]

    def readers(self):
        read = lambda a: (a[0], a[2]) in self.bank
        late = []
        for u in range(self.NU):
            before = [a for a in self.slots[u - 1] if read(a)]
            if u == 0:
                before = [(kind, off - 1, n) for kind, off, n in before]
            own = [(("sums",) + a[1:]) if a[0] == "results" else a for a in self.slots[u]
                   if not read(a) or a[0] == "results"]
            late.append([a for a in own if a[0] in ("mask", "max")] + before +
                        [a for a in own if a[0] not in ("mask", "max")])
        return late

    def use(self, what, b, kind, n=0):
        off, (r_1, r_01, r_all, r_10, r_last) = self.numbered[what]
        body = b - off[kind, n]
        if isinstance(body, int) and body == -1:
            return r_1[kind, n]
        if isinstance(body, int) and body == 0:
            return len(r_1) + r_01[kind, n]
        before = len(r_1) + len(r_01)
        if isinstance(body, int) and body == B - 1:
            return before + (B - 2) * len(r_all) + r_10[kind, n]
        if isinstance(body, int) and body == B:
            return before + (B - 2) * len(r_all) + len(r_10) + r_last[kind, n]
        return body * len(r_all) + (before - len(r_all) + r_all[kind, n])


ATTENTIONS = {
    "L0a": Attention("L0a", 1, 128, norm_source=True, norms=2, own_affine=True, k_affine=True),
    "L1a": Attention("L1a", 16, 8, v_cols=512, v_block=32, stacked=True),
    "L2a": Attention("L2a", 16, 64, v_cols=1024, v_block=64, mask=True),
    "L3a": Attention("L3a", 8, 128, latents=True, norm_source=True, norms=2, own_affine=True, fold_wo=True),
    "L3s": Attention("L3s", 16, 8, context=False, latents=True, norms=2, v_cols=512, v_block=32, own_affine=True,
                     keep_norm=True, stacked=True),
}


def clear(nc, sems):
    for s in sems:
        nc.sync.sem_clear(s)
    nc.all_engine_barrier()


def rsqrt_steps(dve, y, v, t, n):
    dve.tensor_scalar(v, v, EPS, None, ALU.add)
    dve.drain()
    dve.tensor_scalar(t.bitcast(I32), v.bitcast(I32), 1, None, ALU.logical_shift_right)
    dve.drain()
    dve.tensor_scalar(y.bitcast(I32), t.bitcast(I32), -1.0, 1597463007.0, ALU.mult, ALU.add)
    dve.tensor_scalar(v, v, -0.5, None, ALU.mult)
    dve.drain()
    for _ in range(3):
        dve.tensor_tensor(t, y, y, ALU.mult)
        dve.drain()
        dve.tensor_tensor(t, t, v, ALU.mult)
        dve.drain()
        dve.scalar_tensor_tensor(y, t, 1.5, y, ALU.add, ALU.mult)
        dve.drain()


def normalise(dve, out, src, st, n, last=None):
    for t in range(n):
        dve.bn_stats(st["six"][:, t, :], src[:, t, :])
    dve.drain()
    for t in range(n):
        dve.bn_aggr(st["mv"][:, t, :], st["six"][:, t, :])
    dve.drain()
    dve.tensor_copy(st["var"][:, 0:n], st["mv"][:, 0:n, 1])
    dve.drain()
    rsqrt_steps(dve, st["rs"][:, 0:n], st["var"][:, 0:n], st["tmp"][:, 0:n], n)
    for t in range(n):
        ins = dve.tensor_scalar(out[:, t, :], src[:, t, :], st["mv"][:, t, 0:1], st["rs"][:, t:t + 1],
                                ALU.subtract, ALU.mult)
    return ins


def affine(eng, out, src, g, b, n):
    eng.tensor_tensor(out, src, g.unsqueeze(1).broadcast_to([P, n, D]), ALU.mult)
    eng.drain()
    return eng.tensor_tensor(out, out, b.unsqueeze(1).broadcast_to([P, n, D]), ALU.add)


def build_attention(nc, c, io, x_in, x_out):
    T, H, W, HU, NP, NG, NU, NI = c.T, c.H, c.W, c.HU, c.NP, c.NG, c.NU, c.NI
    JP = T * P
    NA = NP * (T - 1)
    QROWS = 96
    KROWS = QROWS + 2
    a = lambda key: io[f"{c.name}_{key}"]
    with ExitStack() as ctx, ExitStack() as done:
        sb = lambda name, shape, dt=F32: ctx.enter_context(nc.sbuf_tensor(f"{c.name}_{name}", shape, dt))
        pb = lambda name, shape, dt=F32: ctx.enter_context(nc.psum_tensor(f"{c.name}_{name}", shape, dt))
        sems = []

        def sem(name):
            sems.append(ctx.enter_context(nc.semaphore(f"{c.name}_{name}")))
            return sems[-1]

        done.callback(lambda: clear(nc, sems))

        ident = sb("ident", [P, P])
        ident_b = sb("ident_b", [P, P], BF16)
        ones_b = sb("ones_b", [P, P], BF16)
        wq = sb("wq", [P, c.QG, P])
        bq = sb("bq", [P, c.QG])
        wfin = sb("wfin", [P, c.FIN, P])
        bfin = sb("bfin", [P, 1])
        loads = [(ident, io["ident"]), (wq, a("wq")), (bq, a("bq"))]
        if c.stacked:
            wks = sb("wks", [P, 4, P])
            wks_hi, wks_lo = sb("wks_hi", [P, 4, P], F32R), sb("wks_lo", [P, 4, P], F32R)
            bks, own = sb("bks", [P, 4]), sb("own", [P, 4])
            bvr, bvm = sb("bvr", [3, c.v_cols]), sb("bvm", [3, 3])
            bvp = [sb(f"bvp{k}", [3, c.v_cols]) for k in range(3)]
            bv_rows = sb("bv_rows", [3, c.v_cols], BF16)
            loads += [(wks, a("wks")), (bks, a("bks")), (own, io["own"]), (bvr, a("bvr")), (bvm, io["three"])]
        else:
            pick = sb("pick", [c.K_ROWS, HU])
            wk = sb("wk", [P, H, P])
            loads += [(pick, a("pick")), (wk, a("wk"))]
            if c.v_cols:
                bv = sb("bv", [P, c.v_cols])
                loads += [(bv, a("bv"))]
        if c.fold_wo:
            wvt, wo = sb("wvt", [P, H, P]), sb("wo", [P, H, P])
            bvh, bo = sb("bvh", [P, H]), sb("bo", [P, 1])
            loads += [(wvt, a("wvt")), (wo, a("wo")), (bvh, a("bvh")), (bo, a("bo"))]
        else:
            loads += [(wfin, a("wfin")), (bfin, a("bfin"))]
        if c.key_bias:
            bk = sb("bk", [P, H])
            loads += [(bk, a("bk"))]
        if c.ones_column:
            spread = sb("spread", [P, P])
            loads += [(spread, io["spread"])]
        else:
            ones_f = sb("ones_f", [P, P])
        if c.v_cols:
            wv = sb("wv", [P, c.v_cols])
            wv_hi, wv_lo = sb("wv_hi", [P, c.v_cols], F32R), sb("wv_lo", [P, c.v_cols], F32R)
            loads += [(wv, a("wv"))]
        if c.own_affine:
            gx, bx = sb("gx", [P, D]), sb("bx", [P, D])
            loads += [(gx, a("gx")), (bx, a("bx"))]
        if c.k_affine:
            affine_c = sb("affine_c", [P, 4])
            loads += [(affine_c, a("affine"))]
        elif c.norm_source:
            gk, bkk = sb("gk", [P, D]), sb("bkk", [P, D])
            loads += [(gk, a("gk")), (bkk, a("bkk"))]

        xin = sb("xin", [P, SH, D])
        xr = sb("xr", [P, 2 if c.keep_norm else 1, SH, D])
        xn = sb("xn", [P, 2, SH, D])
        y = sb("y", [P, SH, D]) if c.norms == 2 else None
        xo = sb("xo", [P, SH, D])
        if c.C:
            cx = sb("cx", [P, CT, D])
        if c.norm_source:
            src = sb("src", [P, 2, T, D])
        if c.k_affine:
            kf = sb("kf", [P, 512])
        kt_hi, kt_lo = sb("kt_hi", [P, 2, JP], F32R), sb("kt_lo", [P, 2, JP], F32R)
        yt = sb("yt", [P, S])
        if c.stacked:
            qs = sb("qs", [P, S])
            qt = sb("qt", [P, c.QG, S])
            q_st = sb("q_st", [P, c.QS, W], F32R)
            k_st = sb("k_st", [P, 4, JP], F32R)
        else:
            qt = sb("qt", [P, c.QG, S])
            q_hi, q_lo = sb("q_hi", [P, c.QS, W], F32R), sb("q_lo", [P, c.QS, W], F32R)
            rows = sb("rows", [P, 2, W], BF16)
        if c.v_cols:
            v = sb("v", [P, T, c.v_cols])
        if c.key_bias:
            qb = sb("qb", [P, SH, H])
            r1 = sb("r1", [P, SH, H])
        mx = sb("mx", [P, 2, SH, HU, 1 if c.small else len(c.M_CH)])
        top = sb("top", [P, SH, HU])
        parts = sb("parts", [P, NP, SH, c.parts, HU], BF16)
        probs = sb("probs", [P, c.PS, W])
        RW = W if c.v_block == 128 else S
        on = sb("on", [P, NG, RW])
        den, rden = sb("den", [P, RW]), sb("rden", [P, RW])
        ft = sb("ft", [P, S])
        stats = lambda n, k: {"six": sb(f"{k}_six", [P, n, 6]), "mv": sb(f"{k}_mv", [P, n, 2]),
                              "var": sb(f"{k}_var", [P, n]), "rs": sb(f"{k}_rs", [P, n]), "tmp": sb(f"{k}_tmp", [P, n])}
        st_x = stats(SH, "st_x")
        if c.norm_source:
            st_c = stats(CT, "st_c")
        if c.ones_column:
            oraw = sb("oraw", [P, S])
        else:
            acc = sb("acc", [P, 2, W])
        if c.mask:
            mask_u8 = sb("mask_u8", [P, SH, J_CTX], U8)
            mask_n = sb("mask_n", [P, SH, JP], BF16)
            mask_t = sb("mask_t", [P, 2, T, S], BF16)
            junk, stub = sb("junk", [P, 4, 512], BF16), sb("stub", [P, 4])

        score = [pb(f"score{k}", [P, 512]) for k in range(2)]
        mpass = [pb(f"mpass{k}", [P, 512]) for k in range(2)]
        res = [pb(f"res{k}", [P, 512]) for k in range(2)]
        aux = [pb(f"aux{k}", [P, 512]) for k in range(2)]
        aux_b = [t[:, :].bitcast(BF16) for t in aux]

        w_in, x_got, c_got, x_put = sem("w_in"), sem("x_got"), sem("c_got"), sem("x_put")
        xo_free = sem("xo_free")
        zero_ok, const_ok, fold_mm, fold_ok = sem("zero_ok"), sem("const_ok"), sem("fold_mm"), sem("fold_ok")
        aux_full = [sem(f"aux_full{k}") for k in range(2)]
        aux_free = [sem(f"aux_free{k}") for k in range(2)]
        hi_ok = sem("hi_ok")
        norm_x_ok, norm_c_ok, c_free = sem("norm_x_ok"), sem("norm_c_ok"), sem("c_free")
        m_full, m_free, parts_ok, rows_ok = sem("m_full"), sem("m_free"), sem("parts_ok"), sem("rows_ok")
        stack_ok, raw_ok, low_ok = sem("stack_ok"), sem("raw_ok"), sem("low_ok")
        s_ok, exp_ok, pv_ok, acc_ok, oraw_ok, on_ok = [sem(n) for n in (
            "s_ok", "exp_ok", "pv_ok", "acc_ok", "oraw_ok", "on_ok")]
        ft_ok, xo_ok, mask_ok = sem("ft_ok"), sem("xo_ok"), sem("mask_ok")

        x_v = x_in.rearrange("(b h p) d -> b p h d", b=B, p=P)
        xo_v = x_out.rearrange("(b h p) d -> b p h d", b=B, p=P)
        C_DMAS = 3 if c.mask else 2
        half = lambda x: x.rearrange("p (h d) -> p h d", h=SH)
        summed = lambda n, q: n * NA + q // T * (T - 1) + max(q % T, 1)

        def run(eng, main, steps, plan=c.late):

            def batch(b, par, offs):
                for u in range(NU):
                    if 0 in offs:
                        main(b, par, u)
                    for kind, off, n in plan[u]:
                        if off in offs:
                            steps[kind](b + off, (par + off) % 2, n)

            batch(-1, 1, (1,))
            batch(0, 0, (0, 1))
            with eng.Fori(0, (B - 2) // 2) as i:
                batch(i * 2 + 1, 1, (-1, 0, 1))
                batch(i * 2 + 2, 0, (-1, 0, 1))
            batch(B - 1, 1, (-1, 0))
            batch(B, 0, (-1,))

        def nothing(b, par, n):
            pass

        def none_but(**steps):
            every = dict.fromkeys(("values", "results", "project", "finish", "norm_x", "stats", "rstd", "norm_c",
                                   "mask", "max", "max_parts", "keep", "sums", "recip", "scale") + c.PREP + c.MISC, nothing)
            every.update(steps)
            return every

        block = done.enter_context(nc.Block())

        @block.sync
        def _(sp):
            def load_source(b):
                sp.dma_start(cx[:, 0:CT - 1, :],
                             io["ctx"][b, 0:(CT - 1) * P, :].rearrange("(t p) d -> p t d", p=P)).then_inc(c_got, 16)
                sp.dma_start(cx[0:CTAIL, CT - 1, :], io["ctx"][b, (CT - 1) * P:J_CTX, :]).then_inc(c_got, 16)
                if c.mask:
                    sp.dma_start(mask_u8[:, :, :],
                                 io["mask"][b].rearrange("(h p) j -> p h j", p=P)).then_inc(c_got, 16)

            def load(n):
                sp.wait_ge(norm_x_ok, n)
                sp.dma_start(xin[:, :, :], x_v[n]).then_inc(x_got, 16)
                if c.C:
                    sp.wait_ge(c_free, n)
                    load_source(n)

            def store(n):
                sp.wait_ge(xo_ok, n + 1)
                sp.dma_start(xo_v[n], xo[:, :, :]).then_inc(x_put, 16)
                sp.wait_ge(x_put, n * 16 + 16)
                if c.keep_norm:
                    sp.nop().then_inc(xo_free, 16)
                elif not (isinstance(n, int) and n == B - 1):
                    sp.dma_start(xr[:, 0], x_v[n + 1]).then_inc(xo_free, 16)

            sp.dma_start(xin[:, :, :], x_v[0]).then_inc(x_got, 16)
            for tile, dram in loads:
                sp.dma_start(tile[:], dram).then_inc(w_in, 16)
            if c.keep_norm:
                sp.nop().then_inc(xo_free, 16)
            else:
                sp.dma_start(xr[:, 0], x_v[0]).then_inc(xo_free, 16)
            if c.C:
                sp.wait_ge(zero_ok, 1)
                load_source(0)
            load(1)
            load(2)
            with sp.Fori(0, B - 3) as n:
                load(n + 3)
                store(n)
            for n in range(B - 3, B):
                store(n)

        @block.tensor
        def _(pe):
            pe.wait_ge(w_in, 16 * len(loads))
            pe.wait_ge(const_ok, 3)
            if c.fold_wo:
                for h in range(H):
                    if h >= 2:
                        pe.wait_ge(fold_ok, h - 1)
                    pe.matmul(score[h % 2][:, 0:P], wvt[:, h, :], wo[:, h, :], start=True, stop=True).then_inc(fold_mm, 1)
                for h in range(H):
                    mm = pe.matmul(aux[0][:, 0:1], wo[:, h, :], bvh[:, h:h + 1], start=(h == 0), stop=(h == H - 1))
                mm.then_inc(fold_mm, 1)
                pe.wait_ge(fold_ok, H + 1)

            def claim(b, kind, n=0):
                s = c.bank[kind, n]
                k = c.use(s, b, kind, n)
                if not (isinstance(k, int) and k == 0):
                    pe.wait_ge(aux_free[s], k)
                return s

            def ready(b, kind, n=0, user=None):
                s = c.bank[kind, n]
                if user is None or c.bank[user] != s:
                    pe.wait_ge(aux_free[s], c.use(s, b, kind, n) + 1)

            def three(out, hi, lo, m_hi, m_lo, stop):
                pe.matmul(out, hi, m_hi, start=True, stop=False)
                pe.matmul(out, lo, m_hi, start=False, stop=False)
                return pe.matmul(out, hi, m_lo, start=False, stop=stop)

            def turn_c(b, par, k):
                if c.norm_source:
                    pe.wait_ge(raw_ok if c.k_affine else norm_c_ok, b * c.KB + (k + 1))
                elif c.LT:
                    pe.wait_ge(norm_x_ok, b + 1)
                elif k == 0:
                    pe.wait_ge(c_got, b * 16 * C_DMAS + 16 * C_DMAS)
                s = claim(b, "turn_c", k)
                tile = src[:, par] if c.norm_source else y if c.LT else cx
                for t in range(4 * k, min(4 * k + 4, T)):
                    mm = pe.transpose(aux[s][:, (t % 4) * P:(t % 4 + 1) * P], tile[:, t, :], ident[:, :])
                mm.then_inc(aux_full[s], 1)

            def turn_x(b, par, n):
                pe.wait_ge(norm_x_ok, b + 1)
                s = claim(b, "turn_x")
                for hf in range(SH):
                    tile = y[:, hf, :] if c.norms == 2 else xn[:, par, hf, :]
                    mm = pe.transpose(aux[s][:, hf * P:(hf + 1) * P], tile, ident[:, :])
                mm.then_inc(aux_full[s], 1)

            def query(b, par, g):
                ready(b, "turn_x", 0, ("query", g))
                s = claim(b, "query", g)
                pe.matmul(aux[s][:, 0:S], wq[:, g, :], yt[:, :], start=True, stop=True).then_inc(aux_full[s], 1)

            def keyed(b, par, p):
                if c.stacked:
                    return
                ready(b, "query", (p * HU + HU - 1) * c.QG // H, ("keyed", p))
                s = claim(b, "keyed", p)
                for e in range(HU):
                    h = p * HU + e
                    mm = pe.matmul(aux[s][:, e * S:(e + 1) * S], wk[:, h, :], qt[:, h * c.QG // H, :], start=True, stop=True)
                mm.then_inc(aux_full[s], 1)

            def query_bias(b, par, n):
                ready(b, "query", c.QG - 1, ("query_bias", 0))
                s = claim(b, "query_bias")
                hq = H // c.QG
                for hf in range(SH):
                    for g in range(c.QG):
                        mm = pe.matmul(aux[s][:, hf * H + g * hq:hf * H + (g + 1) * hq], qt[:, g, hf * P:(hf + 1) * P],
                                       bk[:, g * hq:(g + 1) * hq], start=True, stop=True)
                mm.then_inc(aux_full[s], 1)

            def keys(b, par, n):
                ready(b, "turn_c", c.KB - 1, ("keys", n))
                s = claim(b, "keys", n)
                per = -(-c.J // 512)
                g, at = n // per, n % per * 512
                w = slice(at, min(at + 512, JP))
                three(aux[s][:, 0:w.stop - at], wks_hi[:, g, :], wks_lo[:, g, :], kt_hi[:, par, w], kt_lo[:, par, w],
                      True).then_inc(aux_full[s], 1)

            def value_tile(b, par, n):
                ready(b, "turn_c", c.KB - 1, ("value_tile", n))
                s = claim(b, "value_tile", n)
                w = slice(n[0] * c.VB, (n[0] + 1) * c.VB)
                k = slice(n[1] * P, (n[1] + 1) * P)
                mm = three(aux[s][:, 0:c.VB], kt_hi[:, par, k], kt_lo[:, par, k], wv_hi[:, w], wv_lo[:, w], not c.stacked)
                if c.stacked:
                    mm = pe.matmul(aux[s][:, 0:c.VB], ones_b[0:3, :], bv_rows[:, w], start=False, stop=True)
                mm.then_inc(aux_full[s], 1)

            def turn_mask(b, par, k):
                pe.wait_ge(mask_ok, b * SH + SH)
                s = claim(b, "turn_mask", k)
                for t in range(4 * k, min(4 * k + 4, T)):
                    for hf in range(SH):
                        n = (t % 4) * S + hf * P
                        mm = pe.transpose(aux_b[s][:, n:n + P], mask_n[:, hf, t * P:(t + 1) * P], ident_b[:, :])
                mm.then_inc(aux_full[s], 1)

            def max_item(b, par, m):
                p, i = m // NI, m % NI
                if i == 0:
                    if c.stacked and p % 2 == 0:
                        ready(b, "keys", (p // 2 + 1) * -(-c.J // 512) - 1)
                    if not c.stacked:
                        ready(b, "keyed", p)
                    else:
                        pe.wait_ge(stack_ok, b * NP + (p + 1))
                n_at = b * NP * NI + m
                if not (isinstance(n_at, int) and n_at < 2):
                    pe.wait_ge(m_free, n_at - 1)
                slot = (par * NP + p) % c.QS
                e0, hf, ch = c.M_ITEMS[i]
                lo, hi = c.M_CH[ch]
                w = hi + hi % 2 - lo
                if c.k_affine and i == 0:
                    pe.wait_ge(low_ok, b * c.KB + c.KB)
                for k, e in enumerate(range(HU) if c.small else [e0]):
                    q = slice(e * S + hf * P, e * S + hf * P + P)
                    if c.stacked:
                        lhs, rhs = q_st[0:QROWS, slot, q], k_st[0:QROWS, p // 2, lo:lo + w]
                    else:
                        lhs, rhs = q_hi[:, slot, q], kt_hi[:, par, lo:lo + w]
                    mm = pe.matmul(mpass[m % 2][:, k * w:(k + 1) * w], lhs, rhs, start=True, stop=True)
                mm.then_inc(m_full, 1)

            def max_rows(b, par, p):
                pe.wait_ge(parts_ok, b * NP + (p + 1))
                s = claim(b, "max_rows", p)
                for hf in range(SH):
                    if c.stacked:
                        for e in range(HU):
                            at = e * S + hf * P
                            mm = pe.transpose(aux_b[s][QROWS:KROWS, at:at + P], parts[:, p, hf, :, e], ident_b[:, :],
                                              tile_position=(0, QROWS))
                    else:
                        mm = pe.transpose(aux_b[s][0:c.K_ROWS, hf * P:(hf + 1) * P],
                                          parts[:, p, hf, :, :].rearrange("p k e -> p (k e)"), ident_b[:, :])
                mm.then_inc(aux_full[s], 1)

            def main(b, par, u):
                p, t = u // T, u % T
                if t == 0:
                    pe.wait_ge(rows_ok, b * NP + (p + 1))
                    if u == 0 and c.mask:
                        ready(b, "turn_mask", c.KB - 1)
                if not (isinstance(b, int) and b == 0 and u < 2):
                    pe.wait_ge(exp_ok, b * NU + (u - 1))
                bank = score[(par * NU + u) % 2]
                slot = (par * NP + p) % c.QS
                k = slice(t * P, t * P + P)
                if c.stacked:
                    mm = pe.matmul(bank[:, 0:W], k_st[0:KROWS, p // 2, k], q_st[0:KROWS, slot, :], start=True, stop=True)
                else:
                    three(bank[:, 0:W], kt_hi[:, par, k], kt_lo[:, par, k], q_hi[:, slot, :], q_lo[:, slot, :], False)
                    if c.mask:
                        pe.matmul(bank[:, :].rearrange("p (e s) -> p e s", e=HU), ident_b[:, :],
                                  mask_t[:, par, t, :].unsqueeze(1).broadcast_to([P, HU, S]), start=False, stop=False)
                    mm = pe.matmul(bank[:, 0:W], ones_b[:, :], rows[:, (par * NP + p) % 2, :], start=False, stop=True)
                mm.then_inc(s_ok, 1)

            def values(b, par, u):
                p, t = u // T, u % T
                g = p // c.PPG
                rws = c.tail if t == T - 1 else P
                pe.wait_ge(exp_ok, b * NU + (u + 1))
                if p % c.PPG == 0 and t == 0 and not (isinstance(b, int) and b * NG + g < 2):
                    pe.wait_ge(on_ok, b * NG + g)
                if c.v_cols and t == 0 and p % (NP // 2) == 0:
                    ready(b, "value_tile", (p // (NP // 2), T - 1))
                bank = res[(par * NG + g) % 2]
                pr = probs[0:rws, (par * NU + u) % c.PS, :]
                if c.v_block == 128:
                    mm = pe.matmul(bank[:, 0:W], src[0:rws, par, t, :], pr, start=(t == 0), stop=(t == T - 1))
                else:
                    for e in range(HU):
                        h = p * HU + e
                        at = (h % (P // c.v_block)) * c.v_block
                        mm = pe.matmul(bank[at:at + c.v_block, 0:S], v[0:rws, t, h * c.v_block:(h + 1) * c.v_block],
                                       pr[:, e * S:(e + 1) * S], start=(t == 0), stop=(t == T - 1))
                mm.then_inc(pv_ok, 1)

            def results(b, par, g):
                s = claim(b, "results", g)
                if c.ones_column:
                    pe.wait_ge(oraw_ok, b * NG + (g + 1))
                    mm = pe.matmul(aux[s][:, 0:S], spread[:, :], oraw[:, :], start=True, stop=True)
                else:
                    pe.wait_ge(acc_ok, b * NA + (g + 1) * (T - 1))
                    ac = acc[:, (par * NP + g) % 2, :]
                    if c.v_block == 128:
                        mm = pe.matmul(aux[s][:, 0:W], ones_f[:, :], ac, start=True, stop=True)
                    else:
                        for e in range(HU):
                            mm = pe.matmul(aux[s][e * c.v_block:(e + 1) * c.v_block, 0:S], ones_f[:, 0:c.v_block],
                                           ac[:, e * S:(e + 1) * S], start=True, stop=True)
                mm.then_inc(aux_full[s], 1)

            def project(b, par, n):
                pe.wait_ge(on_ok, b * NG + (NG + 1))
                s = claim(b, "project")
                for k in range(c.FIN):
                    if c.v_block == 128 and HU == 2:
                        o = on[:, k // 2, (k % 2) * S:(k % 2 + 1) * S]
                    else:
                        o = on[:, k, 0:S]
                    mm = pe.matmul(aux[s][:, 0:S], wfin[:, k, :], o, start=(k == 0), stop=(k == c.FIN - 1))
                mm.then_inc(aux_full[s], 1)

            def finish(b, par, n):
                pe.wait_ge(ft_ok, b + 1)
                s = claim(b, "finish")
                for hf in range(SH):
                    mm = pe.transpose(aux[s][:, hf * P:(hf + 1) * P], ft[:, hf * P:(hf + 1) * P], ident[:, :])
                mm.then_inc(aux_full[s], 1)

            run(pe, main, none_but(values=values, results=results, project=project, finish=finish, turn_c=turn_c,
                                   turn_x=turn_x, query=query, keyed=keyed, query_bias=query_bias, keys=keys,
                                   value_tile=value_tile, turn_mask=turn_mask, max=max_item, max_rows=max_rows),
                plan=c.slots)

        @block.scalar
        def _(act):
            act.wait_ge(w_in, 16 * len(loads))

            def full(b, kind, n=0):
                s = c.bank[kind, n]
                act.wait_ge(aux_full[s], c.use(s, b, kind, n) + 1)
                return s

            def turn_c(b, par, k):
                w = min(4, T - 4 * k) * P
                s = full(b, "turn_c", k)
                if c.k_affine:
                    if not (isinstance(b, int) and b == 0 and k == 0):
                        act.wait_ge(low_ok, b * c.KB + k)
                    act.activation(kf[:, 0:w], aux[s][:, 0:w], ACT.Identity, bias=affine_c[:, 1:2],
                                   scale=affine_c[:, 0:1]).then_inc(aux_free[s], 1)
                    act.wait_ge(aux_free[s], c.use(s, b, "turn_c", k) + 1)
                    act.activation(kt_hi[:, par, k * 512:k * 512 + w], kf[:, 0:w], ACT.Copy).then_inc(hi_ok, 1)
                    return
                act.activation(kt_hi[:, par, k * 512:k * 512 + w], aux[s][:, 0:w], ACT.Copy).then_inc(hi_ok, 1)

            def turn_x(b, par, n):
                s = full(b, "turn_x")
                act.activation(yt[:, :], aux[s][:, 0:S], ACT.Copy).then_inc(aux_free[s], 1)

            def query(b, par, g):
                s = full(b, "query", g)
                if c.stacked:
                    act.activation(qt[:, g, :].bitcast(F32R), aux[s][:, 0:S], ACT.Identity, bias=bq[:, g:g + 1],
                                   scale=1.0).then_inc(hi_ok, 1)
                else:
                    act.activation(qt[:, g, :], aux[s][:, 0:S], ACT.Identity, bias=bq[:, g:g + 1],
                                   scale=1.0).then_inc(aux_free[s], 1)

            def keyed(b, par, p):
                if c.stacked:
                    k = c.bank["query", p // 2]
                    act.wait_ge(aux_free[k], c.use(k, b, "query", p // 2) + 1)
                    for e in range(HU):
                        h = p * HU + e
                        ins = act.activation(q_st[0:QROWS, (par * NP + p) % c.QS, e * S:(e + 1) * S],
                                             qt[0:QROWS, h // 4, :], ACT.Copy, scale=own[0:QROWS, h % 4:h % 4 + 1])
                    ins.then_inc(stack_ok, 1)
                else:
                    s = full(b, "keyed", p)
                    act.activation(q_hi[:, (par * NP + p) % c.QS, :], aux[s][:, 0:W], ACT.Copy).then_inc(hi_ok, 1)

            def keys(b, par, n):
                per = -(-c.J // 512)
                g, at = n // per, n % per * 512
                end = min(at + 512, JP)
                s = full(b, "keys", n)
                act.activation(k_st[:, g, at:end], aux[s][:, 0:end - at], ACT.Identity, bias=bks[:, g:g + 1],
                               scale=1.0).then_inc(hi_ok, 1)

            def value_tile(b, par, n):
                if c.stacked:
                    s = full(b, "value_tile", n)
                    act.activation(v[:, n[1], n[0] * c.VB:(n[0] + 1) * c.VB], aux[s][:, 0:c.VB],
                                   ACT.Copy).then_inc(aux_free[s], 1)

            def turn_mask(b, par, k):
                n = min(4, T - 4 * k)
                s = full(b, "turn_mask", k)
                act.activation(mask_t[:, par, 4 * k:4 * k + n, :], aux_b[s][:, 0:n * S].rearrange("p (t s) -> p t s", s=S),
                               ACT.Copy).then_inc(aux_free[s], 1)

            def results(b, par, g):
                s = full(b, "results", g)
                act.wait_ge(on_ok, b * NG + (g + 1))
                act.activation(den[:, :], aux[s][:, 0:RW], ACT.Copy).then_inc(aux_free[s], 1)

            def sums(b, par, g):
                if c.ones_column:
                    act.wait_ge(pv_ok, b * NU + (g + 1) * c.PPG * T)
                    act.activation(oraw[:, :], res[(par * NG + g) % 2][:, 0:S], ACT.Copy).then_inc(oraw_ok, 1)

            def main(b, par, u):
                act.wait_ge(s_ok, b * NU + (u + 1))
                if not (isinstance(b, int) and b * NU + u < c.PS):
                    act.wait_ge(pv_ok, b * NU + (u - c.PS + 1))
                    if not c.ones_column:
                        if u >= c.PS:
                            act.wait_ge(acc_ok, summed(b, u - c.PS))
                        else:
                            act.wait_ge(acc_ok, summed(b - 1, NU + u - c.PS))
                n = par * NU + u
                act.activation(probs[:, n % c.PS, :], score[n % 2][:, 0:W], ACT.Exp).then_inc(exp_ok, 1)

            run(act, main, none_but(results=results, sums=sums, query=query, turn_c=turn_c, turn_x=turn_x, keyed=keyed, keys=keys,
                                    value_tile=value_tile, turn_mask=turn_mask))

        if not c.ones_column:
            @block.gpsimd
            def _(pool):
                pool.memset(ones_f[:, :], 1.0).then_inc(const_ok, 1)
                def main(b, par, u):
                    p, t = u // T, u % T
                    rws = c.tail if t == T - 1 else P
                    n = par * NU + u
                    ac = acc[:, (par * NP + p) % 2, :]
                    if t:
                        pool.wait_ge(exp_ok, b * NU + (u + 1))
                    if t == 1:
                        pool.tensor_tensor(ac, probs[:, (n - 1) % c.PS, :], probs[:, n % c.PS, :], ALU.add).then_inc(acc_ok, 1)
                    elif t > 1:
                        pool.wait_ge(acc_ok, b * NA + (p * (T - 1) + t - 1))
                        pool.tensor_tensor(ac[0:rws], ac[0:rws], probs[0:rws, n % c.PS, :], ALU.add).then_inc(acc_ok, 1)

                def norm_c(b, par, k):
                    if c.k_affine:
                        return
                    lo, hi = max(4 * k, c.LT), min(4 * k + 4, T)
                    part = src[:, par, lo:hi, :]
                    pool.wait_ge(raw_ok, b * c.KB + (k + 1))
                    affine(pool, part, part, gk[:, :], bkk[:, :], hi - lo).then_inc(norm_c_ok, 1)

                if c.norm_source:
                    pool.wait_ge(w_in, 16 * len(loads))
                run(pool, main, none_but(norm_c=norm_c))

        @block.vector
        def _(dve):
            if c.stacked:
                dve.memset(q_st[:, :, :].bitcast(F32), 0.0)
            else:
                dve.memset(rows[:, :, :], 0.0)
            if c.mask:
                dve.memset(mask_n[:, :, :], 0.0)
            if c.C:
                dve.memset(cx[:, CT - 1, :], 0.0).then_inc(zero_ok, 1)
            dve.nop().then_inc(on_ok, 1)
            dve.memset(ones_b[:, :], 1.0)
            dve.wait_ge(w_in, 16 * len(loads))
            dve.tensor_copy(ident_b[:, :], ident[:, :]).then_inc(const_ok, 1)
            dve.tensor_scalar(wq[:, :, :], wq[:, :, :], c.scale, None, ALU.mult)
            dve.tensor_scalar(bq[:, :], bq[:, :], c.scale, None, ALU.mult)
            if c.v_cols:
                dve.tensor_copy(wv_hi[:, :], wv[:, :])
                dve.drain()
                dve.tensor_tensor(wv_lo[:, :], wv[:, :], wv_hi[:, :].bitcast(F32), ALU.subtract)
            if c.stacked:
                dve.tensor_copy(wks_hi[:, :, :], wks[:, :, :])
                dve.drain()
                dve.tensor_tensor(wks_lo[:, :, :], wks[:, :, :], wks_hi[:, :, :].bitcast(F32), ALU.subtract)
                dve.tensor_copy(bv_rows[:, :], bvr[:, :])
                dve.drain()
                dve.tensor_copy(bvp[0][:, :], bv_rows[:, :])
                dve.drain()
                dve.tensor_tensor(bvr[:, :], bvr[:, :], bvp[0][:, :], ALU.subtract)
                dve.drain()
                dve.tensor_copy(bv_rows[:, :], bvr[:, :])
                dve.drain()
                dve.tensor_copy(bvp[1][:, :], bv_rows[:, :])
                dve.drain()
                dve.tensor_tensor(bvp[2][:, :], bvr[:, :], bvp[1][:, :], ALU.subtract)
                dve.drain()
                for k in range(3):
                    dve.tensor_scalar(bvp[k][:, :], bvp[k][:, :], bvm[:, k:k + 1], None, ALU.mult)
                dve.drain()
                dve.tensor_tensor(bvp[0][:, :], bvp[0][:, :], bvp[1][:, :], ALU.add)
                dve.drain()
                dve.tensor_tensor(bv_rows[:, :], bvp[0][:, :], bvp[2][:, :], ALU.add)
            if c.ones_column:
                dve.nop().then_inc(const_ok, 1)
            dve.drain()
            dve.nop().then_inc(const_ok, 1)
            if c.fold_wo:
                for h in range(H):
                    dve.wait_ge(fold_mm, h + 1)
                    dve.tensor_copy(wfin[:, h, :], score[h % 2][:, 0:P]).then_inc(fold_ok, 1)
                dve.wait_ge(fold_mm, H + 1)
                dve.tensor_tensor(bfin[:, :], aux[0][:, 0:1], bo[:, :], ALU.add).then_inc(fold_ok, 1)

            def norm_x(b, par, n):
                dve.wait_ge(x_got, b * 16 + 16)
                ins = normalise(dve, xn[:, par], xin, st_x, SH)
                if c.norms == 2:
                    dve.drain()
                    normalise(dve, y[:, :, :], xn[:, par], st_x, SH)
                    dve.drain()
                    ins = affine(dve, y[:, :, :], y[:, :, :], gx[:, :], bx[:, :], SH)
                ins.then_inc(norm_x_ok, 1)
                if c.norm_source and c.LT:
                    dve.drain()
                    dve.tensor_copy(src[:, par, 0:SH, :], y[:, :, :])

            def keep(b, par, n):
                dve.tensor_copy(xr[:, par], xn[:, par])

            def stats_step(b, par, t):
                if t == 0:
                    dve.wait_ge(c_got, b * 16 * C_DMAS + 16 * C_DMAS)
                dve.bn_stats(st_c["six"][:, t, :], cx[:, t, :])

            def rstd(b, par, n):
                dve.drain()
                for t in range(CT):
                    dve.bn_aggr(st_c["mv"][:, t, :], st_c["six"][:, t, :])
                dve.drain()
                dve.tensor_copy(st_c["var"][:, :], st_c["mv"][:, :, 1])
                dve.drain()
                rsqrt_steps(dve, st_c["rs"][:, :], st_c["var"][:, :], st_c["tmp"][:, :], CT)

            def norm_c(b, par, k):
                lo, hi = max(4 * k, c.LT), min(4 * k + 4, T)
                for t in range(lo, hi):
                    n = t - c.LT
                    ins = dve.tensor_scalar(src[:, par, t, :], cx[:, n, :], st_c["mv"][:, n, 0:1],
                                            st_c["rs"][:, n:n + 1], ALU.subtract, ALU.mult)
                if hi == T:
                    ins.then_inc(c_free, 1)
                dve.drain()
                dve.nop().then_inc(raw_ok, 1)

            def full(b, kind, n=0):
                s = c.bank[kind, n]
                dve.wait_ge(aux_full[s], c.use(s, b, kind, n) + 1)
                return s

            def split(b, kind, n):
                dve.wait_ge(hi_ok, c.use("split", b, kind, n) + 1)
                return c.bank[kind, n]

            def turn_c(b, par, k):
                w = min(4, T - 4 * k) * P
                s = split(b, "turn_c", k)
                whole = kf if c.k_affine else aux[s]
                low = dve.tensor_tensor(kt_lo[:, par, k * 512:k * 512 + w], whole[:, 0:w],
                                        kt_hi[:, par, k * 512:k * 512 + w].bitcast(F32), ALU.subtract)
                low.then_inc(low_ok if c.k_affine else aux_free[s], 1)
                if c.C and k == c.KB - 1 and not c.norm_source and not c.mask:
                    dve.nop().then_inc(c_free, 1)

            def query(b, par, g):
                if c.stacked:
                    s = split(b, "query", g)
                    low = qt[32:64, g, :]
                    dve.scalar_tensor_tensor(low.bitcast(F32R), aux[s][32:64, 0:S], bq[32:64, g:g + 1], low, ALU.add,
                                             ALU.subtract).then_inc(aux_free[s], 1)

            def keyed(b, par, p):
                slot = (par * NP + p) % c.QS
                if c.stacked:
                    return
                s = split(b, "keyed", p)
                dve.tensor_tensor(q_lo[:, slot, :], aux[s][:, 0:W], q_hi[:, slot, :].bitcast(F32),
                                  ALU.subtract).then_inc(aux_free[s], 1)

            def keys(b, par, n):
                per = -(-c.J // 512)
                g, at = n // per, n % per * 512
                end = min(at + 512, JP)
                s = split(b, "keys", n)
                low = k_st[64:96, g, at:end]
                dve.scalar_tensor_tensor(low, aux[s][64:96, 0:end - at], bks[64:96, g:g + 1], low.bitcast(F32), ALU.add,
                                         ALU.subtract).then_inc(aux_free[s], 1)

            def value_tile(b, par, n):
                if not c.stacked:
                    w = slice(n[0] * c.VB, (n[0] + 1) * c.VB)
                    s = full(b, "value_tile", n)
                    dve.tensor_tensor(v[:, n[1], w], aux[s][:, 0:c.VB], bv[:, w], ALU.add).then_inc(aux_free[s], 1)

            def query_bias(b, par, n):
                view = lambda k: parts[:, :, :, k, :].rearrange("p n h e -> p h n e")
                whole = lambda x: x[:, :, :].rearrange("p h (n e) -> p h n e", e=HU)
                s = full(b, "query_bias")
                dve.tensor_copy(qb[:, :, :], aux[s][:, 0:SH * H].rearrange("p (h n) -> p h n", h=SH)).then_inc(aux_free[s], 1)
                dve.drain()
                for hf in range(SH):
                    dve.tensor_copy(view(0)[:, hf], whole(qb)[:, hf])
                dve.drain()
                for hf in range(SH):
                    dve.tensor_tensor(whole(r1)[:, hf], whole(qb)[:, hf], view(0)[:, hf], ALU.subtract)
                dve.drain()
                for hf in range(SH):
                    dve.tensor_copy(view(1)[:, hf], whole(r1)[:, hf])
                dve.drain()
                for hf in range(SH):
                    dve.tensor_tensor(view(2)[:, hf], whole(r1)[:, hf], view(1)[:, hf], ALU.subtract)

            def mask(b, par, hf):
                if hf == 0:
                    dve.wait_ge(c_got, b * 16 * C_DMAS + 16 * C_DMAS)
                ins = dve.tensor_scalar(mask_n[:, hf, 0:J_CTX], mask_u8[:, hf, :], MASKED, -MASKED, ALU.mult, ALU.add)
                ins.then_inc(mask_ok, 1)
                dve.drain()
                if hf == SH - 1:
                    dve.nop().then_inc(c_free, 1)

            def max_item(b, par, m):
                p, i = m // NI, m % NI
                two = (par * NP + p) % 2
                if c.mask and i % 4 == 0:
                    dve.drain()
                dve.wait_ge(m_full, b * NP * NI + (m + 1))
                e, hf, ch = c.M_ITEMS[i]
                if c.small:
                    dve.tensor_reduce(mx[:, two, hf, :, 0], mpass[m % 2][:, :].rearrange("p (e j) -> p e j", j=S), AX,
                                      ALU.max).then_inc(m_free, 1)
                    return
                lo, hi = c.M_CH[ch]
                out = mx[:, two, hf, e, ch:ch + 1]
                if c.mask:
                    dve.memset(stub[:, i % 4:i % 4 + 1], 0.0)
                    dve.tensor_tensor_reduce(junk[:, i % 4, 0:hi - lo], mpass[m % 2][:, 0:hi - lo], mask_n[:, hf, lo:hi], 1.0,
                                             LOWEST, ALU.add, ALU.max, out).then_inc(m_free, 1)
                else:
                    dve.tensor_reduce(out, mpass[m % 2][:, 0:hi - lo], AX, ALU.max).then_inc(m_free, 1)

            def max_parts(b, par, p):
                m = mx[:, (par * NP + p) % 2]
                dve.drain()
                if c.small:
                    best = m[:, :, :, 0]
                else:
                    best = top[:, :, :]
                    dve.tensor_reduce(best, m, AX, ALU.max)
                    dve.drain()
                if c.key_bias:
                    dve.tensor_tensor(best, best, qb[:, :, p * HU:(p + 1) * HU], ALU.add)
                    dve.drain()
                k = c.parts - 2
                dve.tensor_scalar(parts[:, p, :, k, :], best, -1.0, None, ALU.mult)
                dve.drain()
                dve.scalar_tensor_tensor(parts[:, p, :, k + 1, :], best, -1.0, parts[:, p, :, k, :],
                                         ALU.mult, ALU.subtract).then_inc(parts_ok, 1)

            def max_rows(b, par, p):
                s = full(b, "max_rows", p)
                if c.stacked:
                    dve.tensor_copy(q_st[QROWS:KROWS, (par * NP + p) % c.QS, :], aux_b[s][QROWS:KROWS, 0:W]).then_inc(aux_free[s], 1)
                    dve.drain()
                    dve.nop().then_inc(rows_ok, 1)
                    return
                two = (par * NP + p) % 2
                for e in range(HU):
                    ins = dve.tensor_scalar(rows[0:c.K_ROWS, two, e * S:(e + 1) * S], aux_b[s][0:c.K_ROWS, 0:S],
                                            pick[:, e:e + 1], None, ALU.mult)
                ins.then_inc(aux_free[s], 1)
                dve.drain()
                dve.nop().then_inc(rows_ok, 1)

            def recip(b, par, n):
                g, k = n
                w = slice(k * RW // c.RP, (k + 1) * RW // c.RP)
                if k == 0:
                    dve.drain()
                    s = c.bank["results", g]
                    dve.wait_ge(aux_free[s], c.use(s, b, "results", g) + 1)
                dve.reciprocal(rden[:, w], den[:, w])

            def scale(b, par, g):
                dve.drain()
                ins = dve.tensor_tensor(on[:, g, :], res[(par * NG + g) % 2][:, 0:RW], rden[:, :], ALU.mult)
                if c.k_affine:
                    dve.drain()
                    ins = dve.tensor_scalar(on[:, g, :], on[:, g, :], affine_c[:, 2:3], affine_c[:, 3:4], ALU.mult, ALU.add)
                ins.then_inc(on_ok, 1)

            def project(b, par, n):
                s = full(b, "project")
                dve.tensor_scalar(ft[:, :], aux[s][:, 0:S], bfin[:, 0:1], None, ALU.add).then_inc(aux_free[s], 1)
                dve.drain()
                dve.nop().then_inc(ft_ok, 1)

            def finish(b, par, n):
                dve.wait_ge(xo_free, b * 16 + 16)
                s = full(b, "finish")
                base = xr[:, par if c.keep_norm else 0]
                dve.tensor_tensor(xo[:, :, :], half(aux[s][:, 0:S]), base, ALU.add).then_inc(aux_free[s], 1)
                dve.drain()
                dve.nop().then_inc(xo_ok, 1)

            run(dve, nothing, none_but(recip=recip, scale=scale, project=project, finish=finish, norm_x=norm_x,
                                       stats=stats_step, rstd=rstd, norm_c=norm_c, turn_c=turn_c, query=query,
                                       keyed=keyed, keys=keys, value_tile=value_tile, query_bias=query_bias, mask=mask, keep=keep,
                                       max=max_item, max_parts=max_parts, max_rows=max_rows))


class Mixture:

    def __init__(self, name, E, chunks, routed, act, fill=0.0, scale=1.0, top1=False):
        self.name, self.E = name, E
        self.KC, self.KR = chunks, routed
        self.act = act
        self.fill, self.scale = fill, scale
        self.top1 = top1
        self.SEL = max(1, min(E, routed))
        self.share = max(1, routed // E)


MIXTURES = {
    "L0f": Mixture("L0f", 16, 18, 16, "silu", fill=-1.0, scale=2.5),
    "L1f": Mixture("L1f", 16, 6, 4, "silu", fill=LOWEST),
    "L2f": Mixture("L2f", 16, 9, 8, "relu2", fill=0.0, scale=2.5),
    "L3f": Mixture("L3f", 8, 32, 32, "gelu", top1=True),
}
G = 4


def build_mixture(nc, c, io, x_in, x_out, x_more=None):
    E, KC, KR, CN = c.E, c.KC, c.KR, N_CHUNK
    a = lambda key: io[f"{c.name}_{key}"]
    gated = c.act == "silu"
    EG = E // G
    with ExitStack() as ctx, ExitStack() as done:
        done.callback(lambda: clear(nc, sems))
        sb = lambda name, shape, dt=F32: ctx.enter_context(nc.sbuf_tensor(f"{c.name}_{name}", shape, dt))
        pb = lambda name, shape, dt=F32: ctx.enter_context(nc.psum_tensor(f"{c.name}_{name}", shape, dt))
        sems = []

        def sem(name):
            sems.append(ctx.enter_context(nc.semaphore(f"{c.name}_{name}")))
            return sems[-1]

        ident = sb("ident", [P, P])
        ident_b = sb("ident_b", [P, P], BF16)
        wr = sb("wr", [P, E])
        rb = sb("rb", [P, E])
        lower, upper = sb("lower", [P, E, E]), sb("upper", [P, E, E])
        sel_f = sb("sel_f", [3 * E, c.SEL, P])
        sel = sb("sel", [3 * E, c.SEL, P], BF16)
        w1, w2 = sb("w1", [P, KC, P]), sb("w2", [P, KC, P])
        loads = [(ident, io["ident"]), (wr, a("wr")), (rb, a("rb")), (lower, a("lower")), (upper, a("upper")),
                 (sel_f, a("sel")), (w1, a("w1")), (w2, a("w2"))]
        if gated:
            wu = sb("wu", [P, KC, P])
            loads.append((wu, a("wu")))
        if x_more is not None:
            gx, bx = sb("gx", [P, D]), sb("bx", [P, D])
            loads += [(gx, a("gx")), (bx, a("bx"))]
        xin = sb("xin", [P, CTILES, D])
        more = sb("more", [P, CTILES, D]) if x_more is not None else None
        y = sb("y", [P, CTILES, D])
        xo = sb("xo", [P, CTILES, D])
        yt = sb("yt", [P, CHUNK])
        score = sb("score", [P, CTILES, E])
        choice = sb("choice", [P, CTILES, E])
        rank = sb("rank", [P, CTILES, E])
        kept = sb("kept", [P, CTILES, E])
        pair = sb("pair", [P, CTILES, E, E])
        pair2 = sb("pair2", [P, CTILES, E, E])
        gsum = sb("gsum", [P, CTILES, G])
        wsum = sb("wsum", [P, CTILES, 1])
        comb = sb("comb", [P, CTILES, E])
        cparts = sb("cparts", [P, CTILES, P], BF16)
        cpart = lambda k: cparts[:, :, k * E:(k + 1) * E]
        ct = sb("ct", [3 * E, CHUNK], BF16)
        g1 = sb("g1", [P, 2, CHUNK])
        hid = sb("hid", [P, 2, CHUNK])
        ft = sb("ft", [P, CHUNK])
        st = {"six": sb("st_six", [P, CTILES, 6]), "mv": sb("st_mv", [P, CTILES, 2]), "var": sb("st_var", [P, CTILES]),
              "rs": sb("st_rs", [P, CTILES]), "tmp": sb("st_tmp", [P, CTILES])}
        hp = [pb(f"hp{k}", [P, CHUNK]) for k in range(2)]
        up = [pb(f"up{k}", [P, CHUNK]) for k in range(2)]
        wp = [pb(f"wp{k}", [P, CHUNK]) for k in range(2)]
        yp = pb("yp", [P, CHUNK])
        misc = pb("misc", [P, CHUNK])
        misc_b = misc[:, :].bitcast(BF16)

        w_in, x_got, const_ok, y_ok, ytp_ok, yt_ok, lg_ok, sc_ok, cp_ok, ctp_ok, ct_ok = [sem(n) for n in (
            "w_in", "x_got", "const_ok", "y_ok", "ytp_ok", "yt_ok", "lg_ok", "sc_ok", "cp_ok", "ctp_ok", "ct_ok")]
        hp_ok, g1_ok, hid_ok, dn_ok, ft_ok, ftp_ok, xo_ok, x_put = [sem(n) for n in (
            "hp_ok", "g1_ok", "hid_ok", "dn_ok", "ft_ok", "ftp_ok", "xo_ok", "x_put")]
        view = lambda x: x.rearrange("(c t p) d -> c p t d", t=CTILES, p=P)
        X_DMAS = 2 if x_more is not None else 1

        block = done.enter_context(nc.Block())

        @block.sync
        def _(sp):
            def load_x(n):
                sp.dma_start(xin[:, :, :], view(x_in)[n]).then_inc(x_got, 16)
                if x_more is not None:
                    sp.dma_start(more[:, :, :], view(x_more)[n]).then_inc(x_got, 16)

            load_x(0)
            for tile, dram in loads:
                sp.dma_start(tile[:], dram).then_inc(w_in, 16)
            with sp.Fori(0, CN - 1) as n:
                sp.wait_ge(xo_ok, n + 1)
                sp.dma_start(view(x_out)[n], xo[:, :, :]).then_inc(x_put, 16)
                sp.wait_ge(x_put, n * 16 + 16)
                load_x(n + 1)
            sp.wait_ge(xo_ok, CN)
            sp.dma_start(view(x_out)[CN - 1], xo[:, :, :]).then_inc(x_put, 16)
            sp.wait_ge(x_put, 16 * CN)

        @block.tensor
        def _(pe):
            pe.wait_ge(w_in, 16 * len(loads))
            pe.wait_ge(const_ok, 1)
            with pe.Fori(0, CN) as n:
                pe.wait_ge(y_ok, n + 1)
                for t in range(CTILES):
                    mm = pe.transpose(misc[:, t * P:(t + 1) * P], y[:, t, :], ident[:, :])
                mm.then_inc(ytp_ok, 1)
                pe.wait_ge(yt_ok, n + 1)
                for t in range(CTILES):
                    mm = pe.matmul(misc[:, t * E:(t + 1) * E], yt[:, t * P:(t + 1) * P], wr[:, :], start=True, stop=True)
                mm.then_inc(lg_ok, 1)

                def up_products(k):
                    if k >= 2:
                        pe.wait_ge(hid_ok, n * KC + k - 1)
                    mm = pe.matmul(hp[k % 2][:, :], w1[:, k, :], yt[:, :], start=True, stop=True)
                    if gated:
                        mm = pe.matmul(up[k % 2][:, :], wu[:, k, :], yt[:, :], start=True, stop=True)
                    if k < KR:
                        if k == 0:
                            pe.wait_ge(cp_ok, n + 1)
                            for t in range(CTILES):
                                pe_t = pe.transpose(misc_b[:, t * P:(t + 1) * P], cparts[:, t, :], ident_b[:, :])
                            pe_t.then_inc(ctp_ok, 1)
                            pe.wait_ge(ct_ok, n + 1)
                        mm = pe.matmul(wp[k % 2][:, :], sel[:, k // c.share, :], ct[:, :], start=True, stop=True)
                    mm.then_inc(hp_ok, 1)

                def down_product(k):
                    pe.wait_ge(hid_ok, n * KC + k + 1)
                    pe.matmul(yp[:, :], w2[:, k, :], hid[:, k % 2, :], start=(k == 0), stop=(k == KC - 1)).then_inc(dn_ok, 1)

                for k in range(KC):
                    up_products(k)
                    if k:
                        down_product(k - 1)
                down_product(KC - 1)
                pe.wait_ge(ft_ok, n + 1)
                for t in range(CTILES):
                    mm = pe.transpose(misc[:, t * P:(t + 1) * P], ft[:, t * P:(t + 1) * P], ident[:, :])
                mm.then_inc(ftp_ok, 1)
                pe.wait_ge(xo_ok, n + 1)

        @block.scalar
        def _(act):
            with act.Fori(0, CN) as n:
                act.wait_ge(ytp_ok, n + 1)
                act.activation(yt[:, :], misc[:, :], ACT.Copy).then_inc(yt_ok, 1)
                act.wait_ge(lg_ok, n + 1)
                act.activation(score[:, :, :], misc[:, 0:CTILES * E].rearrange("p (t e) -> p t e", t=CTILES),
                               ACT.Copy if c.top1 else ACT.Sigmoid).then_inc(sc_ok, 1)
                func = {"silu": ACT.Sigmoid, "relu2": ACT.Relu, "gelu": ACT.Gelu_apprx_tanh}[c.act]
                for k in range(KC):
                    act.wait_ge(hp_ok, n * KC + k + 1)
                    if k >= 2:
                        act.wait_ge(hid_ok, n * KC + k - 1)
                    act.activation(g1[:, k % 2, :], hp[k % 2][:, :], func).then_inc(g1_ok, 1)
                act.wait_ge(dn_ok, n * KC + KC)
                act.activation(ft[:, :], yp[:, :], ACT.Copy).then_inc(ft_ok, 1)

        def group_ranks(dve):
            v4 = lambda x: x[:, :, :].rearrange("p t (g k) -> p (t g) k", g=G)
            cv, rv = v4(choice), v4(rank)
            tmp = pair[:, :, :, :].rearrange("p t a b -> p (t a b)")
            n = CTILES * G
            for i in range(EG):
                others = [j for j in range(EG) if j != i]
                for q, j in enumerate(others):
                    slot = tmp[:, (i * EG + q) * n:(i * EG + q + 1) * n]
                    dve.tensor_tensor(slot, cv[:, :, j], cv[:, :, i], ALU.is_ge if j < i else ALU.is_gt)
            dve.drain()
            cell = lambda i, q: tmp[:, (i * EG + q) * n:(i * EG + q + 1) * n]
            for i in range(EG):
                dve.tensor_tensor(cell(i, 0), cell(i, 0), cell(i, 1), ALU.add)
            dve.drain()
            for i in range(EG):
                dve.tensor_tensor(rv[:, :, i], cell(i, 0), cell(i, 2), ALU.add)
            dve.drain()

        @block.vector
        def _(dve):
            dve.memset(cparts[:, :, :], 0.0)
            dve.drain()
            dve.wait_ge(w_in, 16 * len(loads))
            dve.tensor_copy(sel[:, :, :], sel_f[:, :, :])
            dve.tensor_copy(ident_b[:, :], ident[:, :]).then_inc(const_ok, 1)

            def ranks(x, w, n_t, out, scratch, scratch2):
                mine = x.unsqueeze(3).broadcast_to([P, n_t, w, w])
                others = x.unsqueeze(2).broadcast_to([P, n_t, w, w])
                s1, s2 = scratch[:, 0:n_t, 0:w, 0:w], scratch2[:, 0:n_t, 0:w, 0:w]
                low = lower[:, 0:w, 0:w].unsqueeze(1).broadcast_to([P, n_t, w, w])
                upp = upper[:, 0:w, 0:w].unsqueeze(1).broadcast_to([P, n_t, w, w])
                for t in range(n_t):
                    dve.tensor_tensor(s1[:, t], others[:, t], mine[:, t], ALU.is_ge)
                    dve.tensor_tensor(s2[:, t], others[:, t], mine[:, t], ALU.is_gt)
                dve.drain()
                for t in range(n_t):
                    dve.tensor_tensor(s1[:, t], s1[:, t], low[:, t], ALU.mult)
                    dve.tensor_tensor(s2[:, t], s2[:, t], upp[:, t], ALU.mult)
                dve.drain()
                for t in range(n_t):
                    dve.tensor_tensor(s1[:, t], s1[:, t], s2[:, t], ALU.add)
                dve.drain()
                for t in range(n_t):
                    dve.tensor_reduce(out[:, t], s1[:, t], AX, ALU.add)
                dve.drain()

            with dve.Fori(0, CN) as n:
                dve.wait_ge(x_got, n * 16 * X_DMAS + 16 * X_DMAS)
                ins = normalise(dve, y, xin, st, CTILES)
                if x_more is not None:
                    dve.drain()
                    ins = affine(dve, y[:, :, :], y[:, :, :], gx[:, :], bx[:, :], CTILES)
                ins.then_inc(y_ok, 1)
                dve.wait_ge(sc_ok, n + 1)
                bias = rb[:, :].unsqueeze(1).broadcast_to([P, CTILES, E])
                dve.tensor_tensor(choice[:, :, :], score[:, :, :], bias, ALU.add)
                dve.drain()
                if c.top1:
                    ranks(choice[:, :, :], E, CTILES, rank[:, :, :], pair, pair2)
                    dve.tensor_scalar(comb[:, :, :], rank[:, :, :], 0.5, None, ALU.is_lt)
                    dve.drain()
                else:
                    group_ranks(dve)
                    dve.tensor_scalar(kept[:, :, :], rank[:, :, :], 1.5, None, ALU.is_lt)
                    dve.drain()
                    dve.tensor_tensor(kept[:, :, :], kept[:, :, :], choice[:, :, :], ALU.mult)
                    dve.drain()
                    dve.tensor_reduce(gsum[:, :, :], kept[:, :, :].rearrange("p t (g k) -> p t g k", g=G), AX, ALU.add)
                    dve.drain()
                    ranks(gsum[:, :, :], G, CTILES, rank[:, :, 0:G], pair, pair2)
                    dve.tensor_scalar(gsum[:, :, :], rank[:, :, 0:G], 1.5, None, ALU.is_lt)
                    dve.drain()
                    for k in range(EG):
                        dve.tensor_copy(kept[:, :, :].rearrange("p t (g k) -> p t g k", g=G)[:, :, :, k], gsum[:, :, :])
                    dve.drain()
                    dve.tensor_tensor(choice[:, :, :], choice[:, :, :], kept[:, :, :], ALU.mult)
                    dve.tensor_scalar(kept[:, :, :], kept[:, :, :], -c.fill, c.fill, ALU.mult, ALU.add)
                    dve.drain()
                    dve.tensor_tensor(choice[:, :, :], choice[:, :, :], kept[:, :, :], ALU.add)
                    dve.drain()
                    ranks(choice[:, :, :], E, CTILES, rank[:, :, :], pair, pair2)
                    dve.scalar_tensor_tensor(comb[:, :, :], rank[:, :, :], 3.5, score[:, :, :], ALU.is_lt, ALU.mult)
                    dve.drain()
                    dve.tensor_reduce(wsum[:, :, 0], comb[:, :, :], AX, ALU.add)
                    dve.drain()
                    dve.tensor_scalar(wsum[:, :, :], wsum[:, :, :], 1e-20, None, ALU.add)
                    dve.drain()
                    dve.reciprocal(wsum[:, :, :], wsum[:, :, :])
                    dve.drain()
                    dve.tensor_scalar(wsum[:, :, :], wsum[:, :, :], c.scale, None, ALU.mult)
                    dve.drain()
                    dve.tensor_tensor(comb[:, :, :], comb[:, :, :], wsum[:, :, :].broadcast_to([P, CTILES, E]), ALU.mult)
                    dve.drain()
                dve.tensor_copy(cpart(0), comb[:, :, :])
                dve.drain()
                dve.tensor_tensor(comb[:, :, :], comb[:, :, :], cpart(0), ALU.subtract)
                dve.drain()
                dve.tensor_copy(cpart(1), comb[:, :, :])
                dve.drain()
                dve.tensor_tensor(cpart(2), comb[:, :, :], cpart(1), ALU.subtract).then_inc(cp_ok, 1)
                dve.wait_ge(ctp_ok, n + 1)
                dve.tensor_copy(ct[:, :], misc_b[0:3 * E, 0:CHUNK]).then_inc(ct_ok, 1)
                for k in range(KC):
                    dve.wait_ge(g1_ok, n * KC + k + 1)
                    if k >= 2:
                        dve.wait_ge(dn_ok, n * KC + k - 1)
                    gk, hk = g1[:, k % 2, :], hid[:, k % 2, :]
                    routed = k < KR
                    if c.act == "silu":
                        dve.tensor_tensor(gk, hp[k % 2][:, :], gk, ALU.mult)
                        dve.drain()
                        ins = dve.tensor_tensor(hk, up[k % 2][:, :], gk, ALU.mult)
                        if routed:
                            dve.drain()
                            ins = dve.tensor_tensor(hk, wp[k % 2][:, :], hk, ALU.mult)
                    elif c.act == "relu2":
                        ins = dve.tensor_tensor(hk, gk, gk, ALU.mult)
                        if routed:
                            dve.drain()
                            ins = dve.tensor_tensor(hk, wp[k % 2][:, :], hk, ALU.mult)
                    else:
                        ins = dve.tensor_tensor(hk, wp[k % 2][:, :], gk, ALU.mult)
                    ins.then_inc(hid_ok, 1)
                dve.wait_ge(ftp_ok, n + 1)
                if x_more is not None:
                    dve.tensor_tensor(xin[:, :, :], xin[:, :, :], more[:, :, :], ALU.add)
                    dve.drain()
                dve.tensor_tensor(xo[:, :, :], misc[:, :].rearrange("p (t d) -> p t d", t=CTILES), xin[:, :, :],
                                  ALU.add).then_inc(xo_ok, 1)


PHASES = ["L0a", "L0f", "L1a", "L1f", "L2a", "L2f", "L3a", "L3s", "L3f"]


def build(nc, io, out, phases=PHASES):
    x, before = io["x"], {}
    for n, name in enumerate(phases):
        last = n == len(phases) - 1
        x_out = out if last else nc.dram_tensor(f"x_{name}", [N_TOK, D], F32, kind="Internal").ap()
        before[name] = x
        if name in ATTENTIONS:
            build_attention(nc, ATTENTIONS[name], io, x, x_out)
        else:
            more = None
            if name == "L3f":
                more = before.get("L3s", io.get("x_more"))
            build_mixture(nc, MIXTURES[name], io, x, x_out, more)
        x = x_out


def layout(i):
    f = lambda k: np.asarray(i[k])
    c = np.ascontiguousarray
    zeros = lambda *s: np.zeros(s, np.float32)
    io = {"x": c(f("x").reshape(N_TOK, D)), "ctx": f("ctx_1024"), "mask": f("mask_BxSxS2_bk0"),
          "ident": np.eye(P, dtype=np.float32)}
    row = lambda v: c(np.broadcast_to(v, (P, v.shape[-1])))
    spread = zeros(P, P)
    for k in range(4):
        spread[32 * k + 8, 32 * k:32 * k + 32] = 1
    io["spread"] = spread
    io["three"] = np.eye(3, dtype=np.float32)
    own = zeros(4, 4, 8, 4)
    for k in range(4):
        own[0:3, k, :, k] = 1
    io["own"] = own.reshape(P, 4)

    def put(name, **arrays):
        for k, v in arrays.items():
            io[f"{name}_{k}"] = c(v)

    for name, a in ATTENTIONS.items():
        if a.stacked:
            continue
        pick = zeros(a.parts, a.HU, a.HU)
        for e in range(a.HU):
            pick[:, e, e] = 1
        put(name, pick=pick.reshape(a.K_ROWS, a.HU))
    def key_weights(wk, heads, dh):
        tiles = heads * dh // P
        out = zeros(P, heads, P)
        for h in range(heads):
            r = (h * dh) % P
            out[r:r + dh, h, :] = wk[:, h * dh:(h + 1) * dh].T
        return out

    def key_bias(bk, heads, dh):
        out = zeros(P, heads)
        for h in range(heads):
            r = (h * dh) % P
            out[r:r + dh, h] = bk[h * dh:(h + 1) * dh]
        return out

    def small_values(wv, bv):
        w, b = zeros(P, 16, 32), zeros(16, 32)
        w[:, :, 0:8] = wv.reshape(P, 16, 8)
        if bv is not None:
            b[:, 0:8] = bv.reshape(16, 8)
        b[:, 8] = 1
        return w.reshape(P, 512), np.broadcast_to(b.reshape(512), (3, 512))

    def small_keys(wk, bk):
        w, b = zeros(P, 4, 4, 32), zeros(4, 4, 32)
        w[:, :, 0:3, :] = wk.reshape(P, 4, 1, 32)
        if bk is not None:
            b[:, 0:3, :] = bk.reshape(4, 1, 32)
        b[:, 3, 0:2] = 1
        return w.reshape(P, 4, P), b.reshape(4, P).T

    def small_queries(wq, bq):
        w, b = zeros(P, 4, 4, 32), zeros(4, 4, 32)
        w[:, :, 0:3, :] = wq.reshape(P, 4, 1, 32)
        if bq is not None:
            b[:, 0:3, :] = bq.reshape(4, 1, 32)
        return w.reshape(P, 4, P), b.reshape(4, P).T

    def small_out(wo):
        w = zeros(4, 4, 32, P)
        w[:, :, 0:8, :] = wo.reshape(4, 4, 8, P)
        return w.reshape(4, P, P).transpose(1, 0, 2)

    g = lambda k: f("L0_xattn_" + k)
    put("L0a", wq=g("Wq").T.reshape(P, 1, P), bq=g("bq").reshape(P, 1), wk=g("Wk").reshape(P, 1, P),
        bk=g("bk").reshape(P, 1), wfin=g("Wv").T.reshape(P, 1, P), bfin=g("bv").reshape(P, 1), gx=row(g("g_t")),
        bx=row(g("b_t")), affine=np.stack([g("g_k"), g("b_k"), g("g_v"), g("b_v")], 1))
    g = lambda k: f("L1_xattn_" + k)
    wv, bv = small_values(g("Wv"), g("bv"))
    (wk, bk), (wq, bq) = small_keys(g("Wk"), g("bk")), small_queries(g("Wq"), g("bq"))
    put("L1a", wq=wq, bq=bq, wks=wk, bks=bk, wv=wv, bvr=bv, wfin=small_out(g("Wo")), bfin=g("bo").reshape(P, 1))
    g = lambda k: f("L2_xattn_" + k)
    put("L2a", wq=g("Wq").reshape(P, 8, P), bq=g("bq").reshape(8, P).T, wk=key_weights(g("Wk"), 16, 64),
        bk=key_bias(g("bk"), 16, 64), wv=g("Wv"), bv=row(g("bv")), wfin=g("Wo").reshape(8, P, P).transpose(1, 0, 2),
        bfin=g("bo").reshape(P, 1))
    g = lambda k: f("L3_xattn_" + k)
    wkv, bkv = g("Wkv"), g("bkv")
    put("L3a", wq=g("Wq").reshape(P, 8, P), bq=g("bq").reshape(8, P).T, wk=key_weights(wkv[:, 0:1024], 8, 128),
        bk=key_bias(bkv[0:1024], 8, 128), wvt=wkv[:, 1024:].reshape(P, 8, P).transpose(2, 1, 0),
        bvh=bkv[1024:].reshape(8, P).T, wo=g("Wo").reshape(8, P, P).transpose(1, 0, 2), bo=g("bo").reshape(P, 1),
        gx=row(g("gamma_lat")), bx=row(g("beta_lat")), gk=row(g("gamma_media")), bkk=row(g("beta_media")))
    g = lambda k: f("L3_ffn_" + k)
    wv, bv = small_values(g("w_qkv")[:, 256:384], None)
    (wk, bk), (wq, bq) = small_keys(g("w_qkv")[:, 128:256], None), small_queries(g("w_qkv")[:, 0:128], None)
    put("L3s", wq=wq, bq=bq, wks=wk, bks=bk, wv=wv, bvr=bv, wfin=small_out(g("w_proj")), bfin=zeros(P, 1),
        gx=row(g("ln1_w")), bx=row(g("ln1_b")))

    for name, m in MIXTURES.items():
        E = m.E
        lower, sel = np.tril(np.ones((E, E), np.float32), -1), zeros(3, E, m.SEL, P)
        per = max(1, E // m.SEL)
        for k in range(m.SEL):
            for q in range(per):
                w = P // per
                sel[:, k * per + q, k, q * w:(q + 1) * w] = 1
        put(name, lower=np.broadcast_to(lower, (P, E, E)), upper=np.broadcast_to(lower.T, (P, E, E)),
            sel=sel.reshape(3 * E, m.SEL, P))
    first = lambda w: w.transpose(1, 0, 2).reshape(P, -1)
    second = lambda w: w.reshape(-1, P, P).transpose(1, 0, 2)
    tiles = lambda w: w.reshape(P, -1, P)
    g = lambda k: f("L0_ffn_" + k)
    put("L0f", wr=g("router_w").T, rb=row(g("bias")), w1=tiles(np.concatenate([first(g("gate_w")), g("sh_gate_w")], 1)),
        wu=tiles(np.concatenate([first(g("up_w")), g("sh_up_w")], 1)),
        w2=second(np.concatenate([g("down_w").reshape(-1, P), g("sh_down_w")], 0)))
    g = lambda k: f("L1_ffn_" + k)
    put("L1f", wr=g("router_w").T, rb=row(g("correction_bias")),
        w1=tiles(np.concatenate([first(g("gate_w")), g("shared_gate_w").T], 1)),
        wu=tiles(np.concatenate([first(g("up_w")), g("shared_up_w").T], 1)),
        w2=second(np.concatenate([g("down_w").reshape(-1, P), g("shared_down_w").T], 0)))
    g = lambda k: f("L2_ffn_" + k)
    put("L2f", wr=g("Wg").T, rb=row(g("bias_corr")),
        w1=tiles(np.concatenate([g("W1").transpose(2, 0, 1).reshape(P, -1), g("Ws1").T], 1)),
        w2=second(np.concatenate([g("W2").transpose(0, 2, 1).reshape(-1, P), g("Ws2").T], 0)))
    g = lambda k: f("L3_ffn_" + k)
    put("L3f", wr=g("gate_w"), rb=row(g("gate_b")), w1=tiles(first(g("w1"))), w2=second(g("w2").reshape(-1, P)),
        gx=row(g("ln2_w")), bx=row(g("ln2_b")))
    return io


def kernel(**inputs):
    import concourse.bacc as bacc
    from concourse.bass_utils import run_bass_kernel_spmd

    arrays = layout(inputs)
    nc = bacc.Bacc("TRN2", target_bir_lowering=False, num_devices=1)
    io = {k: nc.dram_tensor(f"in_{k}", v.shape, mybir.dt.from_np(v.dtype), kind="ExternalInput").ap()
          for k, v in arrays.items()}
    out = nc.dram_tensor("out_x", [N_TOK, D], F32, kind="ExternalOutput").ap()
    build(nc, io, out)
    got = run_bass_kernel_spmd(nc, [{f"in_{k}": v for k, v in arrays.items()}], core_ids=[0])
    return got.results[0]["out_x"].reshape(B, S, D)
```

```python
from contextlib import ExitStack

import numpy as np

import concourse.bass as bass
from concourse import mybir

F32 = mybir.dt.float32
F32R = mybir.dt.float32r
BF16 = mybir.dt.bfloat16
I32 = mybir.dt.int32
U8 = mybir.dt.uint8
ALU = mybir.AluOpType
ACT = mybir.ActivationFunctionType
AX = mybir.AxisListType.X

P = 128
D = 128
B = 8
S = 256
SH = S // P
J_CTX = 1601
CT = -(-J_CTX // P)
CTAIL = J_CTX - (CT - 1) * P
N_TOK = B * S
CHUNK = 512
CTILES = CHUNK // P
N_CHUNK = N_TOK // CHUNK
EPS = 1e-5
MASKED = 1e30
LOWEST = -3.0e38


class Attention:

    def __init__(self, name, heads, head_dim, context=True, latents=False, norm_source=False, norms=1, v_cols=0,
                 v_block=128, key_bias=True, mask=False, own_affine=False, k_affine=False, fold_wo=False,
                 keep_norm=False, stacked=False):
        self.name, self.H, self.dh = name, heads, head_dim
        self.LT = SH if latents else 0
        self.C = CT if context else 0
        self.T = self.LT + self.C
        self.J = (S if latents else 0) + (J_CTX if context else 0)
        self.norm_source = norm_source
        self.k_affine = k_affine
        self.norms = norms
        self.own_affine = own_affine
        self.keep_norm = keep_norm
        self.v_cols = v_cols
        self.v_block = v_block
        self.VB = v_cols // 2
        self.stacked = stacked
        self.key_bias = key_bias and not stacked
        self.mask = mask
        self.fold_wo = fold_wo
        self.HU = min(heads, 2)
        self.W = self.HU * S
        self.NP = heads // self.HU
        self.QG = 4 if stacked else heads * head_dim // P
        self.PPG = 2 if v_block == 32 else 1
        self.NG = self.NP // self.PPG
        self.NU = self.NP * self.T
        self.parts = (3 if self.key_bias else 0) + 2
        self.K_ROWS = self.parts * self.HU
        self.scale = float(head_dim) ** -0.5
        self.ones_column = v_block == 32
        self.small = self.J <= S
        n_ch = -(-self.J // 512)
        step = -(-self.J // n_ch)
        step += step % 2
        self.M_CH = [(c, min(c + step, self.J)) for c in range(0, self.J, step)]
        self.M_ITEMS = [(0, hf, 0) for hf in range(SH)] if self.small else [
            (e, hf, c) for e in range(self.HU) for hf in range(SH) for c in range(len(self.M_CH))]
        self.NI = len(self.M_ITEMS)
        self.KB = -(-self.T // 4)
        self.FIN = heads if fold_wo else self.NG
        self.tail = CTAIL if context else P
        self.RP = 4
        self.QS = 8 if self.small else 2 if self.NP == 1 else 4
        self.PS = 2 if self.NU % 2 else 4
        self.slots = self.plan()
        self.count()
        self.late = self.readers()

    def plan(self):
        T, NP, NU, NI = self.T, self.NP, self.NU, self.NI
        slots = [[] for _ in range(NU)]

        def put(u, kind, off, n=0):
            slots[u].append((kind, off, n))

        for u in range(NU):
            put(u, "values", 0 if u >= 2 else -1, (u - 2) % NU)
        for g in range(self.NG):
            at = lambda k: (((g + 1) * self.PPG * T + 2 + k) % NU, -1 if (g + 1) * self.PPG * T + 2 + k >= NU else 0)
            for kind, k, n in [("results", 0, g)] + [
                    ("recip", 2 + (i // 2 if self.small else i), (g, i)) for i in range(self.RP)] + [
                    ("scale", 3 if self.small else 6, g)]:
                u, off = at(k)
                put(u, kind, off, n)
        put(7 if self.small else 9, "project", -1)
        put(9 if self.small else 11, "finish", -1)
        if self.name == "L0a":
            for k in range(3 * self.norms):
                put(k // 2, "norm_x", 1, k)
            for t in range(CT):
                put(t // 5, "stats", 1, t)
            put(2, "rstd", 1)
            put(3, "turn_x", 1)
            put(5, "query", 1, 0)
            put(6, "query_bias", 1)
            for k in range(self.KB):
                put(3 + k, "norm_c", 1, k)
                put(4 + k, "turn_c", 1, k)
            put(7, "keyed", 1, 0)
            for i in range(NI):
                put(9 + i * 2 // NI, "max", 1, i)
            put(10, "max_parts", 1, 0)
            put(11, "max_rows", 1, 0)
            return slots
        first = lambda p, t: p * T + t
        if self.small:
            for k in range(3 * self.norms):
                put(k // 2, "norm_x", 1, k)
            put(4, "turn_x", 1)
            put(5, "turn_c", 1, 0)
            put(11, "keep", 1)
            for g, u in enumerate((6, 8, 11, 12)):
                put(u, "query", 1, g)
            for g, u in enumerate((8, 10, 12)):
                put(u, "keys", 1, g)
            put(1, "keys", 0, 3)
            for t in range(T):
                put(2 * t, "value_tile", 0, (1, t))
                put(13 + t, "value_tile", 1, (0, t))
            for p in range(NP):
                at = lambda q: (0, q) if q < NP else (1, q - NP)
                put(first(p, 0), "keyed", *at(p + 4))
                off, q = at(p + 3)
                for i in range(NI):
                    put(first(p, i), "max", off, q * NI + i)
                put(first(p, 1), "max_parts", off, q)
                put(first(p, 1), "max_rows", *at(p + 2))
        else:
            for k in range(3 * self.norms):
                put(first(0, 11 - 3 * self.norms + k), "norm_x", 1, k)
            if self.norm_source:
                for t in range(CT):
                    put(first(0, 1 + t), "stats", 1, t)
                put(first(0, 14), "rstd", 1)
                for k in range(self.KB):
                    put(first(1, 1 + 3 * k), "norm_c", 1, k)
                    put(first(1, 3 + 3 * k), "turn_c", 1, k)
            else:
                for k in range(self.KB):
                    put(first(1, 1 + 3 * k), "turn_c", 1, k)
            put(first(0, 12), "turn_x", 1)
            if self.stacked:
                n = -(-self.J // 512)
                for g in range(4):
                    for k in range(n):
                        if g < 3:
                            put(first(2 * g + 2, 1 + 3 * k), "keys", 1, g * n + k)
                        else:
                            put(first(1, 2 + 3 * k), "keys", 0, g * n + k)
            if self.v_cols:
                for t in range(T):
                    put(3 + t * (4 * T - 8) // T, "value_tile", 0, (1, t))
                    put(first(4, 2) + t * (4 * T - 8) // T, "value_tile", 1, (0, t))
            deep = NP >= 8
            ahead = 3 if deep else 2
            at = lambda q: (0, q) if q < NP else (1, q - NP)
            for g in range(self.QG):
                put(first(NP - ahead - 1, 3 + g), "query", 1, g)
            for p in range(NP):
                put(first(p, 0), "keyed", *at(p + ahead))
                off, q = at(p + ahead - 1)
                for i in range(NI):
                    put(first(p, 1 + i * (T - 1 if deep else T - 4) // NI), "max", off, q * NI + i)
                put(first(p, 1 if deep else T - 3), "max_parts", *at(p + 1))
                put(first(p, 3 if deep else T - 2), "max_rows", *at(p + 1))
        if self.key_bias:
            put(first(NP - 2, 5) if NP >= 8 else first(NP - 1, 1), "query_bias", 1)
        if self.mask:
            for hf in range(SH):
                put(first(NP - 2, hf), "mask", 1, hf)
            for k in range(self.KB):
                put(first(NP - 1, 4 + 2 * k), "turn_mask", 1, k)
        order = {"mask": 0, "values": 2, "max": 3}
        for u in range(NU):
            slots[u].sort(key=lambda a: 5 if a == ("keyed", 1, 0) else order.get(a[0], 4))
            first_max = next((k for k, a in enumerate(slots[u]) if a[0] == "max"), None)
            if first_max is not None:
                slots[u].insert(0, slots[u].pop(first_max))
        aux = self.PREP + self.MISC
        assert all(sum(a[0] in aux and not (self.stacked and a[0] == "keyed") for a in s) <= 2 for s in slots)
        return slots

    PREP = ("turn_x", "query", "query_bias", "turn_c", "keyed", "keys", "value_tile", "turn_mask")
    MISC = ("max_rows", "results", "project", "finish")

    def count(self):
        kinds = [k for k in self.PREP + self.MISC if not (self.stacked and k == "keyed")]
        uses = [(a[0], a[2]) for s in self.slots for a in s if a[0] in kinds]
        self.bank = {use: k % 2 for k, use in enumerate(uses)}
        self.numbered = {}
        for what in (0, 1, "split"):
            split = ("turn_c", "query", "keys") if self.stacked else ("turn_c", "keyed")
            plan = [a for s in self.slots for a in s
                    if (a[0] in split if what == "split" else self.bank.get((a[0], a[2])) == what)]
            among = lambda *offs: {(a[0], a[2]): k for k, a in enumerate([a for a in plan if a[1] in offs])}
            off = {(a[0], a[2]): a[1] for a in plan}
            self.numbered[what] = off, [among(1), among(0, 1), among(-1, 0, 1), among(-1, 0), among(-1)]

    def readers(self):
        read = lambda a: (a[0], a[2]) in self.bank
        late = []
        for u in range(self.NU):
            before = [a for a in self.slots[u - 1] if read(a)]
            if u == 0:
                before = [(kind, off - 1, n) for kind, off, n in before]
            own = [(("sums",) + a[1:]) if a[0] == "results" else a for a in self.slots[u]
                   if not read(a) or a[0] == "results"]
            late.append([a for a in own if a[0] in ("mask", "max")] + before +
                        [a for a in own if a[0] not in ("mask", "max")])
        return late

    def use(self, what, b, kind, n=0):
        off, (r_1, r_01, r_all, r_10, r_last) = self.numbered[what]
        body = b - off[kind, n]
        if isinstance(body, int) and body == -1:
            return r_1[kind, n]
        if isinstance(body, int) and body == 0:
            return len(r_1) + r_01[kind, n]
        before = len(r_1) + len(r_01)
        if isinstance(body, int) and body == B - 1:
            return before + (B - 2) * len(r_all) + r_10[kind, n]
        if isinstance(body, int) and body == B:
            return before + (B - 2) * len(r_all) + len(r_10) + r_last[kind, n]
        return body * len(r_all) + (before - len(r_all) + r_all[kind, n])


ATTENTIONS = {
    "L0a": Attention("L0a", 1, 128, norm_source=True, norms=2, own_affine=True, k_affine=True),
    "L1a": Attention("L1a", 16, 8, v_cols=512, v_block=32, stacked=True),
    "L2a": Attention("L2a", 16, 64, v_cols=1024, v_block=64, mask=True),
    "L3a": Attention("L3a", 8, 128, latents=True, norm_source=True, norms=2, own_affine=True, fold_wo=True),
    "L3s": Attention("L3s", 16, 8, context=False, latents=True, norms=2, v_cols=512, v_block=32, own_affine=True,
                     keep_norm=True, stacked=True),
}


def clear(nc, sems):
    for s in sems:
        nc.sync.sem_clear(s)
    nc.all_engine_barrier()


def rsqrt_steps(dve, y, v, t, n):
    dve.tensor_scalar(v, v, EPS, None, ALU.add)
    dve.drain()
    dve.tensor_scalar(t.bitcast(I32), v.bitcast(I32), 1, None, ALU.logical_shift_right)
    dve.drain()
    dve.tensor_scalar(y.bitcast(I32), t.bitcast(I32), -1.0, 1597463007.0, ALU.mult, ALU.add)
    dve.tensor_scalar(v, v, -0.5, None, ALU.mult)
    dve.drain()
    for _ in range(3):
        dve.tensor_tensor(t, y, y, ALU.mult)
        dve.drain()
        dve.tensor_tensor(t, t, v, ALU.mult)
        dve.drain()
        dve.scalar_tensor_tensor(y, t, 1.5, y, ALU.add, ALU.mult)
        dve.drain()


def statistics(dve, src, st, n):
    for t in range(n):
        dve.bn_stats(st["six"][:, t, :], src[:, t, :])
    dve.drain()
    for t in range(n):
        dve.bn_aggr(st["mv"][:, t, :], st["six"][:, t, :])
    dve.drain()
    dve.tensor_copy(st["var"][:, 0:n], st["mv"][:, 0:n, 1])
    dve.drain()


def apply_norm(dve, out, src, st, n):
    for t in range(n):
        ins = dve.tensor_scalar(out[:, t, :], src[:, t, :], st["mv"][:, t, 0:1], st["rs"][:, t:t + 1],
                                ALU.subtract, ALU.mult)
    return ins


def affine(eng, out, src, g, b, n):
    eng.tensor_tensor(out, src, g.unsqueeze(1).broadcast_to([P, n, D]), ALU.mult)
    eng.drain()
    return eng.tensor_tensor(out, out, b.unsqueeze(1).broadcast_to([P, n, D]), ALU.add)


def build_attention(nc, c, io, x_in, x_out):
    T, H, W, HU, NP, NG, NU, NI = c.T, c.H, c.W, c.HU, c.NP, c.NG, c.NU, c.NI
    JP = T * P
    NA = NP * (T - 1)
    QROWS = 96
    KROWS = QROWS + 2
    a = lambda key: io[f"{c.name}_{key}"]
    with ExitStack() as ctx, ExitStack() as done:
        sb = lambda name, shape, dt=F32: ctx.enter_context(nc.sbuf_tensor(f"{c.name}_{name}", shape, dt))
        pb = lambda name, shape, dt=F32: ctx.enter_context(nc.psum_tensor(f"{c.name}_{name}", shape, dt))
        sems = []

        def sem(name):
            sems.append(ctx.enter_context(nc.semaphore(f"{c.name}_{name}")))
            return sems[-1]

        done.callback(lambda: clear(nc, sems))

        ident = sb("ident", [P, P])
        ident_b = sb("ident_b", [P, P], BF16)
        ones_b = sb("ones_b", [P, P], BF16)
        wq = sb("wq", [P, c.QG, P])
        bq = sb("bq", [P, c.QG])
        wfin = sb("wfin", [P, c.FIN, P])
        bfin = sb("bfin", [P, 1])
        loads = [(ident, io["ident"]), (wq, a("wq")), (bq, a("bq"))]
        if c.stacked:
            wks = sb("wks", [P, 4, P])
            wks_hi, wks_lo = sb("wks_hi", [P, 4, P], F32R), sb("wks_lo", [P, 4, P], F32R)
            bks, own = sb("bks", [P, 4]), sb("own", [P, 4])
            bvr, bvm = sb("bvr", [3, c.v_cols]), sb("bvm", [3, 3])
            bvp = [sb(f"bvp{k}", [3, c.v_cols]) for k in range(3)]
            bv_rows = sb("bv_rows", [3, c.v_cols], BF16)
            loads += [(wks, a("wks")), (bks, a("bks")), (own, io["own"]), (bvr, a("bvr")), (bvm, io["three"])]
        else:
            pick = sb("pick", [c.K_ROWS, HU])
            wk = sb("wk", [P, H, P])
            loads += [(pick, a("pick")), (wk, a("wk"))]
            if c.v_cols:
                bv = sb("bv", [P, c.v_cols])
                loads += [(bv, a("bv"))]
        if c.fold_wo:
            wvt, wo = sb("wvt", [P, H, P]), sb("wo", [P, H, P])
            bvh, bo = sb("bvh", [P, H]), sb("bo", [P, 1])
            loads += [(wvt, a("wvt")), (wo, a("wo")), (bvh, a("bvh")), (bo, a("bo"))]
        else:
            loads += [(wfin, a("wfin")), (bfin, a("bfin"))]
        if c.key_bias:
            bk, wqt = sb("bk", [P, H]), sb("wqt", [P, c.QG, P])
            wqb, bqb = sb("wqb", [P, H]), sb("bqb", [P, H])
            loads += [(bk, a("bk")), (wqt, a("wqt"))]
        if c.ones_column:
            spread = sb("spread", [P, P])
            loads += [(spread, io["spread"])]
        else:
            ones_f = sb("ones_f", [P, P])
        if c.v_cols:
            wv = sb("wv", [P, c.v_cols])
            wv_hi, wv_lo = sb("wv_hi", [P, c.v_cols], F32R), sb("wv_lo", [P, c.v_cols], F32R)
            loads += [(wv, a("wv"))]
        if c.own_affine:
            gx, bx = sb("gx", [P, D]), sb("bx", [P, D])
            loads += [(gx, a("gx")), (bx, a("bx"))]
        if c.k_affine:
            affine_c = sb("affine_c", [P, 4])
            loads += [(affine_c, a("affine"))]
        elif c.norm_source:
            gk, bkk = sb("gk", [P, D]), sb("bkk", [P, D])
            loads += [(gk, a("gk")), (bkk, a("bkk"))]

        xin = sb("xin", [P, SH, D])
        xr = sb("xr", [P, 2 if c.keep_norm else 1, SH, D])
        xn = sb("xn", [P, 2, SH, D])
        y = sb("y", [P, SH, D]) if c.norms == 2 else None
        xo = sb("xo", [P, SH, D])
        if c.C:
            cx = sb("cx", [P, CT, D])
        if c.norm_source:
            src = sb("src", [P, 2, T, D])
        if c.k_affine:
            kf = sb("kf", [P, 512])
        kt_hi, kt_lo = sb("kt_hi", [P, 2, JP], F32R), sb("kt_lo", [P, 2, JP], F32R)
        yt = sb("yt", [P, S])
        if c.stacked:
            qt = sb("qt", [P, c.QG, S])
            q_st = sb("q_st", [P, c.QS, W], F32R)
            k_st = sb("k_st", [P, 4, JP], F32R)
        else:
            qt = sb("qt", [P, c.QG, S])
            q_hi, q_lo = sb("q_hi", [P, c.QS, W], F32R), sb("q_lo", [P, c.QS, W], F32R)
            rows = sb("rows", [P, 2, W], BF16)
        if c.v_cols:
            v = sb("v", [P, T, c.v_cols])
        if c.key_bias:
            qb = sb("qb", [P, SH, H])
            r1 = sb("r1", [P, SH, H])
        mx = sb("mx", [P, 2, SH, HU, 1 if c.small else len(c.M_CH)])
        top = sb("top", [P, SH, HU])
        parts = sb("parts", [P, NP, SH, c.parts, HU], BF16)
        probs = sb("probs", [P, c.PS, W])
        RW = W if c.v_block == 128 else S
        on = sb("on", [P, NG, RW])
        den, rden = sb("den", [P, RW]), sb("rden", [P, RW])
        ft = sb("ft", [P, S])
        stats = lambda n, k: {"six": sb(f"{k}_six", [P, n, 6]), "mv": sb(f"{k}_mv", [P, n, 2]),
                              "var": sb(f"{k}_var", [P, n]), "rs": sb(f"{k}_rs", [P, n]), "tmp": sb(f"{k}_tmp", [P, n])}
        st_x = stats(SH, "st_x")
        if c.norm_source:
            st_c = stats(CT, "st_c")
        if c.ones_column:
            oraw = sb("oraw", [P, S])
        else:
            acc = sb("acc", [P, 2, W])
        if c.mask:
            mask_u8 = sb("mask_u8", [P, SH, J_CTX], U8)
            mask_n = sb("mask_n", [P, SH, JP], BF16)
            mask_t = sb("mask_t", [P, 2, T, S], BF16)
            junk, stub = sb("junk", [P, 4, 512], BF16), sb("stub", [P, 4])

        score = [pb(f"score{k}", [P, 512]) for k in range(2)]
        mpass = [pb(f"mpass{k}", [P, 512]) for k in range(2)]
        res = [pb(f"res{k}", [P, 512]) for k in range(2)]
        aux = [pb(f"aux{k}", [P, 512]) for k in range(2)]
        aux_b = [t[:, :].bitcast(BF16) for t in aux]

        w_in, x_got, c_got, x_put = sem("w_in"), sem("x_got"), sem("c_got"), sem("x_put")
        xo_free = sem("xo_free")
        zero_ok, const_ok, fold_mm, fold_ok = sem("zero_ok"), sem("const_ok"), sem("fold_mm"), sem("fold_ok")
        bias_mm, bias_ok = sem("bias_mm"), sem("bias_ok")
        aux_full = [sem(f"aux_full{k}") for k in range(2)]
        aux_free = [sem(f"aux_free{k}") for k in range(2)]
        hi_ok = sem("hi_ok")
        norm_x_ok, norm_c_ok, c_free = sem("norm_x_ok"), sem("norm_c_ok"), sem("c_free")
        m_full, m_free, parts_ok, rows_ok = sem("m_full"), sem("m_free"), sem("parts_ok"), sem("rows_ok")
        stack_ok, raw_ok, low_ok = sem("stack_ok"), sem("raw_ok"), sem("low_ok")
        s_ok, exp_ok, pv_ok, acc_ok, oraw_ok, on_ok = [sem(n) for n in (
            "s_ok", "exp_ok", "pv_ok", "acc_ok", "oraw_ok", "on_ok")]
        ft_ok, xo_ok, mask_ok = sem("ft_ok"), sem("xo_ok"), sem("mask_ok")

        x_v = x_in.rearrange("(b h p) d -> b p h d", b=B, p=P)
        xo_v = x_out.rearrange("(b h p) d -> b p h d", b=B, p=P)
        C_DMAS = 3 if c.mask else 2
        half = lambda x: x.rearrange("p (h d) -> p h d", h=SH)
        summed = lambda n, q: n * NA + q // T * (T - 1) + max(q % T, 1)

        def run(eng, main, steps, plan=c.late):

            def batch(b, par, offs):
                for u in range(NU):
                    if 0 in offs:
                        main(b, par, u)
                    for kind, off, n in plan[u]:
                        if off in offs:
                            steps[kind](b + off, (par + off) % 2, n)

            batch(-1, 1, (1,))
            batch(0, 0, (0, 1))
            with eng.Fori(0, (B - 2) // 2) as i:
                batch(i * 2 + 1, 1, (-1, 0, 1))
                batch(i * 2 + 2, 0, (-1, 0, 1))
            batch(B - 1, 1, (-1, 0))
            batch(B, 0, (-1,))

        def nothing(b, par, n):
            pass

        def none_but(**steps):
            every = dict.fromkeys(("values", "results", "project", "finish", "norm_x", "stats", "rstd", "norm_c",
                                   "mask", "max", "max_parts", "keep", "sums", "recip", "scale") + c.PREP + c.MISC, nothing)
            every.update(steps)
            return every

        block = done.enter_context(nc.Block())

        @block.sync
        def _(sp):
            def load_source(b):
                sp.dma_start(cx[:, 0:CT - 1, :],
                             io["ctx"][b, 0:(CT - 1) * P, :].rearrange("(t p) d -> p t d", p=P)).then_inc(c_got, 16)
                sp.dma_start(cx[0:CTAIL, CT - 1, :], io["ctx"][b, (CT - 1) * P:J_CTX, :]).then_inc(c_got, 16)
                if c.mask:
                    sp.dma_start(mask_u8[:, :, :],
                                 io["mask"][b].rearrange("(h p) j -> p h j", p=P)).then_inc(c_got, 16)

            def load(n):
                sp.wait_ge(norm_x_ok, n)
                sp.dma_start(xin[:, :, :], x_v[n]).then_inc(x_got, 16)
                if c.C:
                    sp.wait_ge(c_free, n)
                    load_source(n)

            def store(n):
                sp.wait_ge(xo_ok, n + 1)
                sp.dma_start(xo_v[n], xo[:, :, :]).then_inc(x_put, 16)
                sp.wait_ge(x_put, n * 16 + 16)
                if c.keep_norm:
                    sp.nop().then_inc(xo_free, 16)
                elif not (isinstance(n, int) and n == B - 1):
                    sp.dma_start(xr[:, 0], x_v[n + 1]).then_inc(xo_free, 16)

            sp.dma_start(xin[:, :, :], x_v[0]).then_inc(x_got, 16)
            for tile, dram in loads[0::2]:
                sp.dma_start(tile[:], dram).then_inc(w_in, 16)
            if c.keep_norm:
                sp.nop().then_inc(xo_free, 16)
            else:
                sp.dma_start(xr[:, 0], x_v[0]).then_inc(xo_free, 16)
            if c.C:
                sp.wait_ge(zero_ok, 1)
                load_source(0)
            load(1)
            load(2)
            with sp.Fori(0, B - 3) as n:
                load(n + 3)
                store(n)
            for n in range(B - 3, B):
                store(n)

        @block.tensor
        def _(pe):
            pe.wait_ge(w_in, 16 * len(loads))
            pe.wait_ge(const_ok, 3)
            if c.key_bias:
                hq = H // c.QG
                for g in range(c.QG):
                    w = slice(g * hq, (g + 1) * hq)
                    pe.matmul(aux[1][:, w], wqt[:, g, :], bk[:, w], start=True, stop=True)
                    mm = pe.matmul(aux[1][:, H + g * hq:H + (g + 1) * hq], bq[:, g:g + 1].broadcast_to([P, P]), bk[:, w],
                                   start=True, stop=True)
                mm.then_inc(bias_mm, 1)
                pe.wait_ge(bias_ok, 1)
            if c.fold_wo:
                for h in range(H):
                    if h >= 2:
                        pe.wait_ge(fold_ok, h - 1)
                    pe.matmul(score[h % 2][:, 0:P], wvt[:, h, :], wo[:, h, :], start=True, stop=True).then_inc(fold_mm, 1)
                for h in range(H):
                    mm = pe.matmul(aux[0][:, 0:1], wo[:, h, :], bvh[:, h:h + 1], start=(h == 0), stop=(h == H - 1))
                mm.then_inc(fold_mm, 1)
                pe.wait_ge(fold_ok, H + 1)

            def claim(b, kind, n=0):
                s = c.bank[kind, n]
                k = c.use(s, b, kind, n)
                if not (isinstance(k, int) and k == 0):
                    pe.wait_ge(aux_free[s], k)
                return s

            def ready(b, kind, n=0, user=None):
                s = c.bank[kind, n]
                if user is None or c.bank[user] != s:
                    pe.wait_ge(aux_free[s], c.use(s, b, kind, n) + 1)

            def three(out, hi, lo, m_hi, m_lo, stop):
                pe.matmul(out, hi, m_hi, start=True, stop=False)
                pe.matmul(out, lo, m_hi, start=False, stop=False)
                return pe.matmul(out, hi, m_lo, start=False, stop=stop)

            def turn_c(b, par, k):
                if c.norm_source:
                    pe.wait_ge(raw_ok if c.k_affine else norm_c_ok, b * c.KB + (k + 1))
                elif c.LT:
                    pe.wait_ge(norm_x_ok, b + 1)
                elif k == 0:
                    pe.wait_ge(c_got, b * 16 * C_DMAS + 16 * C_DMAS)
                s = claim(b, "turn_c", k)
                tile = src[:, par] if c.norm_source else y if c.LT else cx
                for t in range(4 * k, min(4 * k + 4, T)):
                    mm = pe.transpose(aux[s][:, (t % 4) * P:(t % 4 + 1) * P], tile[:, t, :], ident[:, :])
                mm.then_inc(aux_full[s], 1)

            def turn_x(b, par, n):
                pe.wait_ge(norm_x_ok, b + 1)
                s = claim(b, "turn_x")
                for hf in range(SH):
                    tile = y[:, hf, :] if c.norms == 2 else xn[:, par, hf, :]
                    mm = pe.transpose(aux[s][:, hf * P:(hf + 1) * P], tile, ident[:, :])
                mm.then_inc(aux_full[s], 1)

            def query(b, par, g):
                ready(b, "turn_x", 0, ("query", g))
                s = claim(b, "query", g)
                pe.matmul(aux[s][:, 0:S], wq[:, g, :], yt[:, :], start=True, stop=True).then_inc(aux_full[s], 1)

            def keyed(b, par, p):
                if c.stacked:
                    return
                ready(b, "query", (p * HU + HU - 1) * c.QG // H, ("keyed", p))
                s = claim(b, "keyed", p)
                for e in range(HU):
                    h = p * HU + e
                    mm = pe.matmul(aux[s][:, e * S:(e + 1) * S], wk[:, h, :], qt[:, h * c.QG // H, :], start=True, stop=True)
                mm.then_inc(aux_full[s], 1)

            def query_bias(b, par, n):
                ready(b, "turn_x", 0, ("query_bias", 0))
                s = claim(b, "query_bias")
                for hf in range(SH):
                    mm = pe.matmul(aux[s][:, hf * H:(hf + 1) * H], yt[:, hf * P:(hf + 1) * P], wqb[:, :], start=True, stop=True)
                mm.then_inc(aux_full[s], 1)

            def keys(b, par, n):
                ready(b, "turn_c", c.KB - 1, ("keys", n))
                s = claim(b, "keys", n)
                per = -(-c.J // 512)
                g, at = n // per, n % per * 512
                w = slice(at, min(at + 512, JP))
                three(aux[s][:, 0:w.stop - at], wks_hi[:, g, :], wks_lo[:, g, :], kt_hi[:, par, w], kt_lo[:, par, w],
                      True).then_inc(aux_full[s], 1)

            def value_tile(b, par, n):
                ready(b, "turn_c", c.KB - 1, ("value_tile", n))
                s = claim(b, "value_tile", n)
                w = slice(n[0] * c.VB, (n[0] + 1) * c.VB)
                k = slice(n[1] * P, (n[1] + 1) * P)
                mm = three(aux[s][:, 0:c.VB], kt_hi[:, par, k], kt_lo[:, par, k], wv_hi[:, w], wv_lo[:, w], not c.stacked)
                if c.stacked:
                    mm = pe.matmul(aux[s][:, 0:c.VB], ones_b[0:3, :], bv_rows[:, w], start=False, stop=True)
                mm.then_inc(aux_full[s], 1)

            def turn_mask(b, par, k):
                pe.wait_ge(mask_ok, b * SH + SH)
                s = claim(b, "turn_mask", k)
                for t in range(4 * k, min(4 * k + 4, T)):
                    for hf in range(SH):
                        n = (t % 4) * S + hf * P
                        mm = pe.transpose(aux_b[s][:, n:n + P], mask_n[:, hf, t * P:(t + 1) * P], ident_b[:, :])
                mm.then_inc(aux_full[s], 1)

            def max_item(b, par, m):
                p, i = m // NI, m % NI
                if i == 0:
                    if c.stacked and p % 2 == 0:
                        ready(b, "keys", (p // 2 + 1) * -(-c.J // 512) - 1)
                    if not c.stacked:
                        ready(b, "keyed", p)
                    else:
                        pe.wait_ge(stack_ok, b * NP + (p + 1))
                n_at = b * NP * NI + m
                if not (isinstance(n_at, int) and n_at < 2):
                    pe.wait_ge(m_free, n_at - 1)
                slot = (par * NP + p) % c.QS
                e0, hf, ch = c.M_ITEMS[i]
                lo, hi = c.M_CH[ch]
                w = hi + hi % 2 - lo
                if c.k_affine and i == 0:
                    pe.wait_ge(low_ok, b * c.KB + c.KB)
                for k, e in enumerate(range(HU) if c.small else [e0]):
                    q = slice(e * S + hf * P, e * S + hf * P + P)
                    if c.stacked:
                        lhs, rhs = q_st[0:QROWS, slot, q], k_st[0:QROWS, p // 2, lo:lo + w]
                    else:
                        lhs, rhs = q_hi[:, slot, q], kt_hi[:, par, lo:lo + w]
                    mm = pe.matmul(mpass[m % 2][:, k * w:(k + 1) * w], lhs, rhs, start=True, stop=True)
                mm.then_inc(m_full, 1)

            def max_rows(b, par, p):
                pe.wait_ge(parts_ok, b * NP + (p + 1))
                s = claim(b, "max_rows", p)
                for hf in range(SH):
                    if c.stacked:
                        for e in range(HU):
                            at = e * S + hf * P
                            mm = pe.transpose(aux_b[s][QROWS:KROWS, at:at + P], parts[:, p, hf, :, e], ident_b[:, :],
                                              tile_position=(0, QROWS))
                    else:
                        mm = pe.transpose(aux_b[s][0:c.K_ROWS, hf * P:(hf + 1) * P],
                                          parts[:, p, hf, :, :].rearrange("p k e -> p (k e)"), ident_b[:, :])
                mm.then_inc(aux_full[s], 1)

            def main(b, par, u):
                p, t = u // T, u % T
                if t == 0:
                    if c.stacked:
                        ready(b, "max_rows", p)
                    else:
                        pe.wait_ge(rows_ok, b * NP + (p + 1))
                    if u == 0 and c.mask:
                        ready(b, "turn_mask", c.KB - 1)
                if not (isinstance(b, int) and b == 0 and u < 2):
                    pe.wait_ge(exp_ok, b * NU + (u - 1))
                bank = score[(par * NU + u) % 2]
                slot = (par * NP + p) % c.QS
                k = slice(t * P, t * P + P)
                if c.stacked:
                    mm = pe.matmul(bank[:, 0:W], k_st[0:KROWS, p // 2, k], q_st[0:KROWS, slot, :], start=True, stop=True)
                else:
                    three(bank[:, 0:W], kt_hi[:, par, k], kt_lo[:, par, k], q_hi[:, slot, :], q_lo[:, slot, :], False)
                    if c.mask:
                        pe.matmul(bank[:, :].rearrange("p (e s) -> p e s", e=HU), ident_b[:, :],
                                  mask_t[:, par, t, :].unsqueeze(1).broadcast_to([P, HU, S]), start=False, stop=False)
                    mm = pe.matmul(bank[:, 0:W], ones_b[:, :], rows[:, (par * NP + p) % 2, :], start=False, stop=True)
                mm.then_inc(s_ok, 1)

            def values(b, par, u):
                p, t = u // T, u % T
                g = p // c.PPG
                rws = c.tail if t == T - 1 else P
                pe.wait_ge(exp_ok, b * NU + (u + 1))
                if p % c.PPG == 0 and t == 0 and not (isinstance(b, int) and b * NG + g < 2):
                    pe.wait_ge(on_ok, b * NG + g)
                if c.v_cols and t == 0 and p % (NP // 2) == 0:
                    ready(b, "value_tile", (p // (NP // 2), T - 1))
                bank = res[(par * NG + g) % 2]
                pr = probs[0:rws, (par * NU + u) % c.PS, :]
                if c.v_block == 128:
                    mm = pe.matmul(bank[:, 0:W], src[0:rws, par, t, :], pr, start=(t == 0), stop=(t == T - 1))
                else:
                    for e in range(HU):
                        h = p * HU + e
                        at = (h % (P // c.v_block)) * c.v_block
                        mm = pe.matmul(bank[at:at + c.v_block, 0:S], v[0:rws, t, h * c.v_block:(h + 1) * c.v_block],
                                       pr[:, e * S:(e + 1) * S], start=(t == 0), stop=(t == T - 1))
                mm.then_inc(pv_ok, 1)

            def results(b, par, g):
                s = claim(b, "results", g)
                if c.ones_column:
                    pe.wait_ge(oraw_ok, b * NG + (g + 1))
                    mm = pe.matmul(aux[s][:, 0:S], spread[:, :], oraw[:, :], start=True, stop=True)
                else:
                    pe.wait_ge(acc_ok, b * NA + (g + 1) * (T - 1))
                    ac = acc[:, (par * NP + g) % 2, :]
                    if c.v_block == 128:
                        mm = pe.matmul(aux[s][:, 0:W], ones_f[:, :], ac, start=True, stop=True)
                    else:
                        for e in range(HU):
                            mm = pe.matmul(aux[s][e * c.v_block:(e + 1) * c.v_block, 0:S], ones_f[:, 0:c.v_block],
                                           ac[:, e * S:(e + 1) * S], start=True, stop=True)
                mm.then_inc(aux_full[s], 1)

            def project(b, par, n):
                pe.wait_ge(on_ok, b * NG + (NG + 1))
                s = claim(b, "project")
                for k in range(c.FIN):
                    if c.v_block == 128 and HU == 2:
                        o = on[:, k // 2, (k % 2) * S:(k % 2 + 1) * S]
                    else:
                        o = on[:, k, 0:S]
                    mm = pe.matmul(aux[s][:, 0:S], wfin[:, k, :], o, start=(k == 0), stop=(k == c.FIN - 1))
                mm.then_inc(aux_full[s], 1)

            def finish(b, par, n):
                pe.wait_ge(ft_ok, b + 1)
                s = claim(b, "finish")
                for hf in range(SH):
                    mm = pe.transpose(aux[s][:, hf * P:(hf + 1) * P], ft[:, hf * P:(hf + 1) * P], ident[:, :])
                mm.then_inc(aux_full[s], 1)

            run(pe, main, none_but(values=values, results=results, project=project, finish=finish, turn_c=turn_c,
                                   turn_x=turn_x, query=query, keyed=keyed, query_bias=query_bias, keys=keys,
                                   value_tile=value_tile, turn_mask=turn_mask, max=max_item, max_rows=max_rows),
                plan=c.slots)

        @block.scalar
        def _(act):
            for tile, dram in loads[1::2]:
                act.dma_start(tile[:], dram).then_inc(w_in, 16)
            act.wait_ge(w_in, 16 * len(loads))

            def full(b, kind, n=0):
                s = c.bank[kind, n]
                act.wait_ge(aux_full[s], c.use(s, b, kind, n) + 1)
                return s

            def turn_c(b, par, k):
                w = min(4, T - 4 * k) * P
                s = full(b, "turn_c", k)
                if c.k_affine:
                    if not (isinstance(b, int) and b == 0 and k == 0):
                        act.wait_ge(low_ok, b * c.KB + k)
                    act.activation(kf[:, 0:w], aux[s][:, 0:w], ACT.Identity, bias=affine_c[:, 1:2],
                                   scale=affine_c[:, 0:1]).then_inc(aux_free[s], 1)
                    act.wait_ge(aux_free[s], c.use(s, b, "turn_c", k) + 1)
                    act.activation(kt_hi[:, par, k * 512:k * 512 + w], kf[:, 0:w], ACT.Copy).then_inc(hi_ok, 1)
                    return
                act.activation(kt_hi[:, par, k * 512:k * 512 + w], aux[s][:, 0:w], ACT.Copy).then_inc(hi_ok, 1)

            def turn_x(b, par, n):
                s = full(b, "turn_x")
                act.activation(yt[:, :], aux[s][:, 0:S], ACT.Copy).then_inc(aux_free[s], 1)

            def query(b, par, g):
                s = full(b, "query", g)
                if c.stacked:
                    act.activation(qt[:, g, :].bitcast(F32R), aux[s][:, 0:S], ACT.Identity, bias=bq[:, g:g + 1],
                                   scale=1.0).then_inc(hi_ok, 1)
                else:
                    act.activation(qt[:, g, :], aux[s][:, 0:S], ACT.Identity, bias=bq[:, g:g + 1],
                                   scale=1.0).then_inc(aux_free[s], 1)

            def keyed(b, par, p):
                if c.stacked:
                    k = c.bank["query", p // 2]
                    act.wait_ge(aux_free[k], c.use(k, b, "query", p // 2) + 1)
                    for e in range(HU):
                        h = p * HU + e
                        ins = act.activation(q_st[0:QROWS, (par * NP + p) % c.QS, e * S:(e + 1) * S],
                                             qt[0:QROWS, h // 4, :], ACT.Copy, scale=own[0:QROWS, h % 4:h % 4 + 1])
                    ins.then_inc(stack_ok, 1)
                else:
                    s = full(b, "keyed", p)
                    act.activation(q_hi[:, (par * NP + p) % c.QS, :], aux[s][:, 0:W], ACT.Copy).then_inc(hi_ok, 1)

            def keys(b, par, n):
                per = -(-c.J // 512)
                g, at = n // per, n % per * 512
                end = min(at + 512, JP)
                s = full(b, "keys", n)
                act.activation(k_st[:, g, at:end], aux[s][:, 0:end - at], ACT.Identity, bias=bks[:, g:g + 1],
                               scale=1.0).then_inc(hi_ok, 1)

            def value_tile(b, par, n):
                if c.stacked:
                    s = full(b, "value_tile", n)
                    act.activation(v[:, n[1], n[0] * c.VB:(n[0] + 1) * c.VB], aux[s][:, 0:c.VB],
                                   ACT.Copy).then_inc(aux_free[s], 1)

            def max_rows(b, par, p):
                if c.stacked:
                    s = full(b, "max_rows", p)
                    act.activation(q_st[QROWS:KROWS, (par * NP + p) % c.QS, :], aux_b[s][QROWS:KROWS, 0:W],
                                   ACT.Copy).then_inc(aux_free[s], 1)

            def turn_mask(b, par, k):
                n = min(4, T - 4 * k)
                s = full(b, "turn_mask", k)
                act.activation(mask_t[:, par, 4 * k:4 * k + n, :], aux_b[s][:, 0:n * S].rearrange("p (t s) -> p t s", s=S),
                               ACT.Copy).then_inc(aux_free[s], 1)

            def results(b, par, g):
                s = full(b, "results", g)
                act.wait_ge(on_ok, b * NG + (g + 1))
                act.activation(den[:, :], aux[s][:, 0:RW], ACT.Copy).then_inc(aux_free[s], 1)

            def sums(b, par, g):
                if c.ones_column:
                    act.wait_ge(pv_ok, b * NU + (g + 1) * c.PPG * T)
                    act.activation(oraw[:, :], res[(par * NG + g) % 2][:, 0:S], ACT.Copy).then_inc(oraw_ok, 1)

            def main(b, par, u):
                act.wait_ge(s_ok, b * NU + (u + 1))
                if not (isinstance(b, int) and b * NU + u < c.PS):
                    act.wait_ge(pv_ok, b * NU + (u - c.PS + 1))
                    if not c.ones_column:
                        if u >= c.PS:
                            act.wait_ge(acc_ok, summed(b, u - c.PS))
                        else:
                            act.wait_ge(acc_ok, summed(b - 1, NU + u - c.PS))
                n = par * NU + u
                act.activation(probs[:, n % c.PS, :], score[n % 2][:, 0:W], ACT.Exp).then_inc(exp_ok, 1)

            run(act, main, none_but(results=results, sums=sums, query=query, turn_c=turn_c, turn_x=turn_x, keyed=keyed, keys=keys,
                                    value_tile=value_tile, turn_mask=turn_mask, max_rows=max_rows))

        if not c.ones_column:
            @block.gpsimd
            def _(pool):
                pool.memset(ones_f[:, :], 1.0).then_inc(const_ok, 1)
                def main(b, par, u):
                    p, t = u // T, u % T
                    rws = c.tail if t == T - 1 else P
                    n = par * NU + u
                    ac = acc[:, (par * NP + p) % 2, :]
                    if t:
                        pool.wait_ge(exp_ok, b * NU + (u + 1))
                    if t == 1:
                        pool.tensor_tensor(ac, probs[:, (n - 1) % c.PS, :], probs[:, n % c.PS, :], ALU.add).then_inc(acc_ok, 1)
                    elif t > 1:
                        pool.wait_ge(acc_ok, b * NA + (p * (T - 1) + t - 1))
                        pool.tensor_tensor(ac[0:rws], ac[0:rws], probs[0:rws, n % c.PS, :], ALU.add).then_inc(acc_ok, 1)

                def norm_c(b, par, k):
                    if c.k_affine:
                        return
                    lo, hi = max(4 * k, c.LT), min(4 * k + 4, T)
                    part = src[:, par, lo:hi, :]
                    pool.wait_ge(raw_ok, b * c.KB + (k + 1))
                    affine(pool, part, part, gk[:, :], bkk[:, :], hi - lo).then_inc(norm_c_ok, 1)

                if c.norm_source:
                    pool.wait_ge(w_in, 16 * len(loads))
                run(pool, main, none_but(norm_c=norm_c))

        @block.vector
        def _(dve):
            if c.stacked:
                dve.memset(q_st[:, :, :].bitcast(F32), 0.0)
            else:
                dve.memset(rows[:, :, :], 0.0)
            if c.mask:
                dve.memset(mask_n[:, :, :], 0.0)
            if c.C:
                dve.memset(cx[:, CT - 1, :], 0.0).then_inc(zero_ok, 1)
            dve.nop().then_inc(on_ok, 1)
            dve.memset(ones_b[:, :], 1.0)
            dve.wait_ge(w_in, 16 * len(loads))
            dve.tensor_copy(ident_b[:, :], ident[:, :]).then_inc(const_ok, 1)
            dve.tensor_scalar(wq[:, :, :], wq[:, :, :], c.scale, None, ALU.mult)
            dve.tensor_scalar(bq[:, :], bq[:, :], c.scale, None, ALU.mult)
            if c.v_cols:
                dve.tensor_copy(wv_hi[:, :], wv[:, :])
                dve.drain()
                dve.tensor_tensor(wv_lo[:, :], wv[:, :], wv_hi[:, :].bitcast(F32), ALU.subtract)
            if c.stacked:
                dve.tensor_copy(wks_hi[:, :, :], wks[:, :, :])
                dve.drain()
                dve.tensor_tensor(wks_lo[:, :, :], wks[:, :, :], wks_hi[:, :, :].bitcast(F32), ALU.subtract)
                dve.tensor_copy(bv_rows[:, :], bvr[:, :])
                dve.drain()
                dve.tensor_copy(bvp[0][:, :], bv_rows[:, :])
                dve.drain()
                dve.tensor_tensor(bvr[:, :], bvr[:, :], bvp[0][:, :], ALU.subtract)
                dve.drain()
                dve.tensor_copy(bv_rows[:, :], bvr[:, :])
                dve.drain()
                dve.tensor_copy(bvp[1][:, :], bv_rows[:, :])
                dve.drain()
                dve.tensor_tensor(bvp[2][:, :], bvr[:, :], bvp[1][:, :], ALU.subtract)
                dve.drain()
                for k in range(3):
                    dve.tensor_scalar(bvp[k][:, :], bvp[k][:, :], bvm[:, k:k + 1], None, ALU.mult)
                dve.drain()
                dve.tensor_tensor(bvp[0][:, :], bvp[0][:, :], bvp[1][:, :], ALU.add)
                dve.drain()
                dve.tensor_tensor(bv_rows[:, :], bvp[0][:, :], bvp[2][:, :], ALU.add)
            if c.ones_column:
                dve.nop().then_inc(const_ok, 1)
            dve.drain()
            dve.nop().then_inc(const_ok, 1)
            if c.key_bias:
                dve.wait_ge(bias_mm, 1)
                dve.tensor_scalar(wqb[:, :], aux[1][:, 0:H], c.scale, None, ALU.mult)
                dve.tensor_copy(bqb[:, :], aux[1][:, H:2 * H])
                dve.drain()
                dve.nop().then_inc(bias_ok, 1)
            if c.fold_wo:
                for h in range(H):
                    dve.wait_ge(fold_mm, h + 1)
                    dve.tensor_copy(wfin[:, h, :], score[h % 2][:, 0:P]).then_inc(fold_ok, 1)
                dve.wait_ge(fold_mm, H + 1)
                dve.tensor_tensor(bfin[:, :], aux[0][:, 0:1], bo[:, :], ALU.add).then_inc(fold_ok, 1)

            def norm_x(b, par, n):
                norm, step = n // 3, n % 3
                before, after = (xin, xn[:, par]) if norm == 0 else (xn[:, par], y)
                if n == 0:
                    dve.wait_ge(x_got, b * 16 + 16)
                if step == 0:
                    statistics(dve, before, st_x, SH)
                    return
                if step == 1:
                    rsqrt_steps(dve, st_x["rs"][:, :], st_x["var"][:, :], st_x["tmp"][:, :], SH)
                    return
                ins = apply_norm(dve, after, before, st_x, SH)
                if norm < c.norms - 1:
                    dve.drain()
                    return
                if c.own_affine:
                    dve.drain()
                    ins = affine(dve, y[:, :, :], y[:, :, :], gx[:, :], bx[:, :], SH)
                ins.then_inc(norm_x_ok, 1)
                if c.norm_source and c.LT:
                    dve.drain()
                    dve.tensor_copy(src[:, par, 0:SH, :], y[:, :, :])

            def keep(b, par, n):
                dve.tensor_copy(xr[:, par], xn[:, par])

            def stats_step(b, par, t):
                if t == 0:
                    dve.wait_ge(c_got, b * 16 * C_DMAS + 16 * C_DMAS)
                dve.bn_stats(st_c["six"][:, t, :], cx[:, t, :])

            def rstd(b, par, n):
                dve.drain()
                for t in range(CT):
                    dve.bn_aggr(st_c["mv"][:, t, :], st_c["six"][:, t, :])
                dve.drain()
                dve.tensor_copy(st_c["var"][:, :], st_c["mv"][:, :, 1])
                dve.drain()
                rsqrt_steps(dve, st_c["rs"][:, :], st_c["var"][:, :], st_c["tmp"][:, :], CT)

            def norm_c(b, par, k):
                lo, hi = max(4 * k, c.LT), min(4 * k + 4, T)
                for t in range(lo, hi):
                    n = t - c.LT
                    ins = dve.tensor_scalar(src[:, par, t, :], cx[:, n, :], st_c["mv"][:, n, 0:1],
                                            st_c["rs"][:, n:n + 1], ALU.subtract, ALU.mult)
                if hi == T:
                    ins.then_inc(c_free, 1)
                dve.drain()
                dve.nop().then_inc(raw_ok, 1)

            def full(b, kind, n=0):
                s = c.bank[kind, n]
                dve.wait_ge(aux_full[s], c.use(s, b, kind, n) + 1)
                return s

            def split(b, kind, n):
                dve.wait_ge(hi_ok, c.use("split", b, kind, n) + 1)
                return c.bank[kind, n]

            def turn_c(b, par, k):
                w = min(4, T - 4 * k) * P
                s = split(b, "turn_c", k)
                whole = kf if c.k_affine else aux[s]
                low = dve.tensor_tensor(kt_lo[:, par, k * 512:k * 512 + w], whole[:, 0:w],
                                        kt_hi[:, par, k * 512:k * 512 + w].bitcast(F32), ALU.subtract)
                low.then_inc(low_ok if c.k_affine else aux_free[s], 1)
                if c.C and k == c.KB - 1 and not c.norm_source and not c.mask:
                    dve.nop().then_inc(c_free, 1)

            def query(b, par, g):
                if c.stacked:
                    s = split(b, "query", g)
                    low = qt[32:64, g, :]
                    dve.scalar_tensor_tensor(low.bitcast(F32R), aux[s][32:64, 0:S], bq[32:64, g:g + 1], low, ALU.add,
                                             ALU.subtract).then_inc(aux_free[s], 1)

            def keyed(b, par, p):
                slot = (par * NP + p) % c.QS
                if c.stacked:
                    return
                s = split(b, "keyed", p)
                dve.tensor_tensor(q_lo[:, slot, :], aux[s][:, 0:W], q_hi[:, slot, :].bitcast(F32),
                                  ALU.subtract).then_inc(aux_free[s], 1)

            def keys(b, par, n):
                per = -(-c.J // 512)
                g, at = n // per, n % per * 512
                end = min(at + 512, JP)
                s = split(b, "keys", n)
                low = k_st[64:96, g, at:end]
                dve.scalar_tensor_tensor(low, aux[s][64:96, 0:end - at], bks[64:96, g:g + 1], low.bitcast(F32), ALU.add,
                                         ALU.subtract).then_inc(aux_free[s], 1)

            def value_tile(b, par, n):
                if not c.stacked:
                    w = slice(n[0] * c.VB, (n[0] + 1) * c.VB)
                    s = full(b, "value_tile", n)
                    dve.tensor_tensor(v[:, n[1], w], aux[s][:, 0:c.VB], bv[:, w], ALU.add).then_inc(aux_free[s], 1)

            def query_bias(b, par, n):
                view = lambda k: parts[:, :, :, k, :].rearrange("p n h e -> p h n e")
                whole = lambda x: x[:, :, :].rearrange("p h (n e) -> p h n e", e=HU)
                s = full(b, "query_bias")
                dve.tensor_tensor(qb[:, :, :], aux[s][:, 0:SH * H].rearrange("p (h n) -> p h n", h=SH),
                                  bqb[:, :].unsqueeze(1).broadcast_to([P, SH, H]), ALU.add).then_inc(aux_free[s], 1)
                dve.drain()
                for hf in range(SH):
                    dve.tensor_copy(view(0)[:, hf], whole(qb)[:, hf])
                dve.drain()
                for hf in range(SH):
                    dve.tensor_tensor(whole(r1)[:, hf], whole(qb)[:, hf], view(0)[:, hf], ALU.subtract)
                dve.drain()
                for hf in range(SH):
                    dve.tensor_copy(view(1)[:, hf], whole(r1)[:, hf])
                dve.drain()
                for hf in range(SH):
                    dve.tensor_tensor(view(2)[:, hf], whole(r1)[:, hf], view(1)[:, hf], ALU.subtract)

            def mask(b, par, hf):
                if hf == 0:
                    dve.wait_ge(c_got, b * 16 * C_DMAS + 16 * C_DMAS)
                ins = dve.tensor_scalar(mask_n[:, hf, 0:J_CTX], mask_u8[:, hf, :], MASKED, -MASKED, ALU.mult, ALU.add)
                ins.then_inc(mask_ok, 1)
                dve.drain()
                if hf == SH - 1:
                    dve.nop().then_inc(c_free, 1)

            def max_item(b, par, m):
                p, i = m // NI, m % NI
                two = (par * NP + p) % 2
                if c.mask and i % 4 == 0:
                    dve.drain()
                dve.wait_ge(m_full, b * NP * NI + (m + 1))
                e, hf, ch = c.M_ITEMS[i]
                if c.small:
                    dve.tensor_reduce(mx[:, two, hf, :, 0], mpass[m % 2][:, :].rearrange("p (e j) -> p e j", j=S), AX,
                                      ALU.max).then_inc(m_free, 1)
                    return
                lo, hi = c.M_CH[ch]
                out = mx[:, two, hf, e, ch:ch + 1]
                if c.mask:
                    dve.memset(stub[:, i % 4:i % 4 + 1], 0.0)
                    dve.tensor_tensor_reduce(junk[:, i % 4, 0:hi - lo], mpass[m % 2][:, 0:hi - lo], mask_n[:, hf, lo:hi], 1.0,
                                             LOWEST, ALU.add, ALU.max, out).then_inc(m_free, 1)
                else:
                    dve.tensor_reduce(out, mpass[m % 2][:, 0:hi - lo], AX, ALU.max).then_inc(m_free, 1)

            def max_parts(b, par, p):
                m = mx[:, (par * NP + p) % 2]
                dve.drain()
                if c.small:
                    best = m[:, :, :, 0]
                else:
                    best = top[:, :, :]
                    dve.tensor_reduce(best, m, AX, ALU.max)
                    dve.drain()
                if c.key_bias:
                    dve.tensor_tensor(best, best, qb[:, :, p * HU:(p + 1) * HU], ALU.add)
                    dve.drain()
                k = c.parts - 2
                dve.tensor_scalar(parts[:, p, :, k, :], best, -1.0, None, ALU.mult)
                dve.drain()
                dve.scalar_tensor_tensor(parts[:, p, :, k + 1, :], best, -1.0, parts[:, p, :, k, :],
                                         ALU.mult, ALU.subtract).then_inc(parts_ok, 1)

            def max_rows(b, par, p):
                if c.stacked:
                    return
                s = full(b, "max_rows", p)
                two = (par * NP + p) % 2
                for e in range(HU):
                    ins = dve.tensor_scalar(rows[0:c.K_ROWS, two, e * S:(e + 1) * S], aux_b[s][0:c.K_ROWS, 0:S],
                                            pick[:, e:e + 1], None, ALU.mult)
                ins.then_inc(aux_free[s], 1)
                dve.drain()
                dve.nop().then_inc(rows_ok, 1)

            def recip(b, par, n):
                g, k = n
                w = slice(k * RW // c.RP, (k + 1) * RW // c.RP)
                if k == 0:
                    dve.drain()
                    s = c.bank["results", g]
                    dve.wait_ge(aux_free[s], c.use(s, b, "results", g) + 1)
                dve.reciprocal(rden[:, w], den[:, w])

            def scale(b, par, g):
                dve.drain()
                ins = dve.tensor_tensor(on[:, g, :], res[(par * NG + g) % 2][:, 0:RW], rden[:, :], ALU.mult)
                if c.k_affine:
                    dve.drain()
                    ins = dve.tensor_scalar(on[:, g, :], on[:, g, :], affine_c[:, 2:3], affine_c[:, 3:4], ALU.mult, ALU.add)
                ins.then_inc(on_ok, 1)

            def project(b, par, n):
                s = full(b, "project")
                dve.tensor_scalar(ft[:, :], aux[s][:, 0:S], bfin[:, 0:1], None, ALU.add).then_inc(aux_free[s], 1)
                dve.drain()
                dve.nop().then_inc(ft_ok, 1)

            def finish(b, par, n):
                dve.wait_ge(xo_free, b * 16 + 16)
                s = full(b, "finish")
                base = xr[:, par if c.keep_norm else 0]
                dve.tensor_tensor(xo[:, :, :], half(aux[s][:, 0:S]), base, ALU.add).then_inc(aux_free[s], 1)
                dve.drain()
                dve.nop().then_inc(xo_ok, 1)

            run(dve, nothing, none_but(recip=recip, scale=scale, project=project, finish=finish, norm_x=norm_x,
                                       stats=stats_step, rstd=rstd, norm_c=norm_c, turn_c=turn_c, query=query,
                                       keyed=keyed, keys=keys, value_tile=value_tile, query_bias=query_bias, mask=mask, keep=keep,
                                       max=max_item, max_parts=max_parts, max_rows=max_rows))


class Mixture:

    def __init__(self, name, E, chunks, routed, act, fill=0.0, scale=1.0, top1=False):
        self.name, self.E = name, E
        self.KC, self.KR = chunks, routed
        self.act = act
        self.fill, self.scale = fill, scale
        self.top1 = top1
        self.SEL = max(1, min(E, routed))
        self.share = max(1, routed // E)
        stages = self.STAGES_1 if top1 else self.STAGES_4
        self.norm = max(1, chunks // 8)
        self.turn = self.norm + 1
        start = self.norm + 3
        last = max(chunks - 3, start)
        at = {"statistics": max(0, self.norm - 2), "rsqrt": self.norm - 1, "norm": self.norm}
        at.update({s: start + k * (last - start) // (len(stages) - 1) for k, s in enumerate(stages)})
        self.stages = [[s for s in at if at[s] == k] for k in range(chunks)]
        self.turn_w = last + 1
        self.copy_w = min(last + 2, chunks - 1)

    STAGES_1 = ("choice", "compare", "count", "best", "parts")
    STAGES_4 = ("choice", "groups", "keep", "compare", "count", "weights", "parts")


MIXTURES = {
    "L0f": Mixture("L0f", 16, 18, 16, "silu", fill=-1.0, scale=2.5),
    "L1f": Mixture("L1f", 16, 6, 4, "silu", fill=LOWEST),
    "L2f": Mixture("L2f", 16, 9, 8, "relu2", fill=0.0, scale=2.5),
    "L3f": Mixture("L3f", 8, 32, 32, "gelu", top1=True),
}
G = 4


def build_mixture(nc, c, io, x_in, x_out, x_more=None):
    E, KC, KR, CN = c.E, c.KC, c.KR, N_CHUNK
    a = lambda key: io[f"{c.name}_{key}"]
    gated = c.act == "silu"
    EG = E // G
    with ExitStack() as ctx, ExitStack() as done:
        done.callback(lambda: clear(nc, sems))
        sb = lambda name, shape, dt=F32: ctx.enter_context(nc.sbuf_tensor(f"{c.name}_{name}", shape, dt))
        pb = lambda name, shape, dt=F32: ctx.enter_context(nc.psum_tensor(f"{c.name}_{name}", shape, dt))
        sems = []

        def sem(name):
            sems.append(ctx.enter_context(nc.semaphore(f"{c.name}_{name}")))
            return sems[-1]

        ident = sb("ident", [P, P])
        ident_b = sb("ident_b", [P, P], BF16)
        wr = sb("wr", [P, E])
        rb = sb("rb", [P, E])
        lower, upper = sb("lower", [P, E, E]), sb("upper", [P, E, E])
        sel_f = sb("sel_f", [3 * E, c.SEL, P])
        sel = sb("sel", [3 * E, c.SEL, P], BF16)
        w1, w2 = sb("w1", [P, KC, P]), sb("w2", [P, KC, P])
        loads = [(ident, io["ident"]), (wr, a("wr")), (rb, a("rb")), (lower, a("lower")), (upper, a("upper")),
                 (sel_f, a("sel"))]
        big_loads = [(w1, a("w1")), (w2, a("w2"))]
        if gated:
            wu = sb("wu", [P, KC, P])
            big_loads.append((wu, a("wu")))
        if x_more is not None:
            gx, bx = sb("gx", [P, D]), sb("bx", [P, D])
            loads += [(gx, a("gx")), (bx, a("bx"))]
        xin = sb("xin", [P, CTILES, D])
        xr = sb("xr", [P, CTILES, D])
        more = sb("more", [P, CTILES, D]) if x_more is not None else None
        y = sb("y", [P, CTILES, D])
        xo = sb("xo", [P, CTILES, D])
        yt = sb("yt", [P, 2, CHUNK])
        score = sb("score", [P, CTILES, E])
        choice = sb("choice", [P, CTILES, E])
        rank = sb("rank", [P, CTILES, E])
        kept = sb("kept", [P, CTILES, E])
        pair = sb("pair", [P, CTILES, E, E])
        pair2 = sb("pair2", [P, CTILES, E, E])
        gsum = sb("gsum", [P, CTILES, G])
        wsum = sb("wsum", [P, CTILES, 1])
        comb = sb("comb", [P, CTILES, E])
        cparts = sb("cparts", [P, CTILES, P], BF16)
        cpart = lambda k: cparts[:, :, k * E:(k + 1) * E]
        ct = sb("ct", [3 * E, 2, CHUNK], BF16)
        g1 = sb("g1", [P, 2, CHUNK])
        hid = sb("hid", [P, 2, CHUNK])
        ft = sb("ft", [P, CHUNK])
        st = {"six": sb("st_six", [P, CTILES, 6]), "mv": sb("st_mv", [P, CTILES, 2]), "var": sb("st_var", [P, CTILES]),
              "rs": sb("st_rs", [P, CTILES]), "tmp": sb("st_tmp", [P, CTILES])}
        hp = [pb(f"hp{k}", [P, CHUNK]) for k in range(2)]
        up = [pb(f"up{k}", [P, CHUNK]) for k in range(2)]
        wp = [pb(f"wp{k}", [P, CHUNK]) for k in range(2)]
        yp = pb("yp", [P, CHUNK])
        misc = pb("misc", [P, CHUNK])
        misc_b = misc[:, :].bitcast(BF16)

        w_in, x_got, const_ok, y_ok, ytp_ok, yt_ok, lg_ok, sc_ok, cp_ok, ctp_ok, ct_ok = [sem(n) for n in (
            "w_in", "x_got", "const_ok", "y_ok", "ytp_ok", "yt_ok", "lg_ok", "sc_ok", "cp_ok", "ctp_ok", "ct_ok")]
        hp_ok, g1_ok, hid_ok, dn_ok, ft_ok, ftp_ok, xo_ok, x_put = [sem(n) for n in (
            "hp_ok", "g1_ok", "hid_ok", "dn_ok", "ft_ok", "ftp_ok", "xo_ok", "x_put")]
        xr_got, w_big = sem("xr_got"), sem("w_big")
        view = lambda x: x.rearrange("(c t p) d -> c p t d", t=CTILES, p=P)
        R_DMAS = 2 if x_more is not None else 1

        def run(eng, hidden, route, finish, finish_at=1):

            def chunk(n, par, next_too):
                for k in range(KC):
                    hidden(n, par, k)
                    if k == finish_at and not (isinstance(n, int) and n == 0):
                        finish(n - 1)
                    if next_too:
                        route(n + 1, 1 - par, k)

            for k in range(KC):
                route(0, 0, k)
            chunk(0, 0, True)
            with eng.Fori(0, (CN - 2) // 2) as i:
                chunk(i * 2 + 1, 1, True)
                chunk(i * 2 + 2, 0, True)
            chunk(CN - 1, 1, False)
            finish(CN - 1)

        block = done.enter_context(nc.Block())

        @block.sync
        def _(sp):
            def load_x(n):
                sp.dma_start(xin[:, :, :], view(x_in)[n]).then_inc(x_got, 16)

            def load_residual(n):
                sp.dma_start(xr[:, :, :], view(x_in)[n]).then_inc(xr_got, 16)
                if x_more is not None:
                    sp.dma_start(more[:, :, :], view(x_more)[n]).then_inc(xr_got, 16)

            def store_x(n):
                sp.wait_ge(xo_ok, n + 1)
                sp.dma_start(view(x_out)[n], xo[:, :, :]).then_inc(x_put, 16)
                sp.wait_ge(x_put, n * 16 + 16)

            load_x(0)
            for tile, dram in loads[0::2]:
                sp.dma_start(tile[:], dram).then_inc(w_in, 16)
            for tile, dram in big_loads[0::2]:
                sp.dma_start(tile[:], dram).then_inc(w_big, 16)
            load_residual(0)
            sp.wait_ge(y_ok, 1)
            load_x(1)
            with sp.Fori(0, CN - 2) as n:
                sp.wait_ge(y_ok, n + 2)
                load_x(n + 2)
                store_x(n)
                load_residual(n + 1)
            store_x(CN - 2)
            load_residual(CN - 1)
            store_x(CN - 1)

        @block.tensor
        def _(pe):
            pe.wait_ge(w_in, 16 * len(loads))
            pe.wait_ge(const_ok, 1)
            two = lambda par, k: (par * KC + k) % 2

            def products(n, par, k):
                if not (isinstance(n, int) and n * KC + k < 2):
                    pe.wait_ge(hid_ok, n * KC + (k - 1))
                mm = pe.matmul(hp[two(par, k)][:, :], w1[:, k, :], yt[:, par, :], start=True, stop=True)
                if gated:
                    mm = pe.matmul(up[two(par, k)][:, :], wu[:, k, :], yt[:, par, :], start=True, stop=True)
                if k >= KR:
                    mm.then_inc(hp_ok, 1)

            def weigh(n, par, k):
                if k < KR:
                    if k == 0:
                        pe.wait_ge(ct_ok, n + 1)
                    pe.matmul(wp[two(par, k)][:, :], sel[:, k // c.share, :], ct[:, par, :], start=True,
                              stop=True).then_inc(hp_ok, 1)

            def down_product(n, par, k):
                if k == 0 and not (isinstance(n, int) and n == 0):
                    pe.wait_ge(ft_ok, n)
                pe.wait_ge(hid_ok, n * KC + (k + 1))
                pe.matmul(yp[:, :], w2[:, k, :], hid[:, two(par, k), :], start=(k == 0),
                          stop=(k == KC - 1)).then_inc(dn_ok, 1)

            def hidden(n, par, k):
                if k == 0:
                    if isinstance(n, int) and n == 0:
                        pe.wait_ge(w_big, 16 * len(big_loads))
                        products(n, par, 0)
                    weigh(n, par, 0)
                if k + 1 < KC:
                    products(n, par, k + 1)
                    weigh(n, par, k + 1)
                elif not (isinstance(n, int) and n == CN - 1):
                    products(n + 1, 1 - par, 0)
                down_product(n, par, k)

            def route(n, par, k):
                if k == c.turn:
                    if not (isinstance(n, int) and n < 2):
                        pe.wait_ge(xo_ok, n - 1)
                    pe.wait_ge(y_ok, n + 1)
                    for t in range(CTILES):
                        mm = pe.transpose(misc[:, t * P:(t + 1) * P], y[:, t, :], ident[:, :])
                    mm.then_inc(ytp_ok, 1)
                if k == c.turn + 1:
                    pe.wait_ge(yt_ok, n + 1)
                    for t in range(CTILES):
                        mm = pe.matmul(misc[:, t * E:(t + 1) * E], yt[:, par, t * P:(t + 1) * P], wr[:, :],
                                       start=True, stop=True)
                    mm.then_inc(lg_ok, 1)
                if k == c.turn_w:
                    pe.wait_ge(cp_ok, n + 1)
                    for t in range(CTILES):
                        mm = pe.transpose(misc_b[:, t * P:(t + 1) * P], cparts[:, t, :], ident_b[:, :])
                    mm.then_inc(ctp_ok, 1)

            def finish(n):
                if isinstance(n, int) and n == CN - 1:
                    pe.wait_ge(xo_ok, n)
                pe.wait_ge(ft_ok, n + 1)
                for t in range(CTILES):
                    mm = pe.transpose(misc[:, t * P:(t + 1) * P], ft[:, t * P:(t + 1) * P], ident[:, :])
                mm.then_inc(ftp_ok, 1)

            run(pe, hidden, route, finish)

        @block.scalar
        def _(act):
            for tile, dram in loads[1::2]:
                act.dma_start(tile[:], dram).then_inc(w_in, 16)
            for tile, dram in big_loads[1::2]:
                act.dma_start(tile[:], dram).then_inc(w_big, 16)
            func = {"silu": ACT.Sigmoid, "relu2": ACT.Relu, "gelu": ACT.Gelu_apprx_tanh}[c.act]

            def hidden(n, par, k):
                act.wait_ge(hp_ok, n * KC + (k + 1))
                if not (isinstance(n, int) and n == 0 and k < 2):
                    act.wait_ge(hid_ok, n * KC + (k - 1))
                act.activation(g1[:, (par * KC + k) % 2, :], hp[(par * KC + k) % 2][:, :], func).then_inc(g1_ok, 1)

            def route(n, par, k):
                if k == c.turn + 1:
                    act.wait_ge(ytp_ok, n + 1)
                    act.activation(yt[:, par, :], misc[:, :], ACT.Copy).then_inc(yt_ok, 1)
                if k == c.turn + 2:
                    act.wait_ge(lg_ok, n + 1)
                    act.activation(score[:, :, :], misc[:, 0:CTILES * E].rearrange("p (t e) -> p t e", t=CTILES),
                                   ACT.Copy if c.top1 else ACT.Sigmoid).then_inc(sc_ok, 1)

            def finish(n):
                act.wait_ge(dn_ok, n * KC + KC)
                act.activation(ft[:, :], yp[:, :], ACT.Copy).then_inc(ft_ok, 1)

            run(act, hidden, route, finish, finish_at=0)

        def group_ranks(dve):
            v4 = lambda x: x[:, :, :].rearrange("p t (g k) -> p (t g) k", g=G)
            cv, rv = v4(choice), v4(rank)
            tmp = pair[:, :, :, :].rearrange("p t a b -> p (t a b)")
            n = CTILES * G
            for i in range(EG):
                others = [j for j in range(EG) if j != i]
                for q, j in enumerate(others):
                    slot = tmp[:, (i * EG + q) * n:(i * EG + q + 1) * n]
                    dve.tensor_tensor(slot, cv[:, :, j], cv[:, :, i], ALU.is_ge if j < i else ALU.is_gt)
            dve.drain()
            cell = lambda i, q: tmp[:, (i * EG + q) * n:(i * EG + q + 1) * n]
            for i in range(EG):
                dve.tensor_tensor(cell(i, 0), cell(i, 0), cell(i, 1), ALU.add)
            dve.drain()
            for i in range(EG):
                dve.tensor_tensor(rv[:, :, i], cell(i, 0), cell(i, 2), ALU.add)
            dve.drain()

        @block.vector
        def _(dve):
            dve.memset(cparts[:, :, :], 0.0)
            dve.drain()
            dve.wait_ge(w_in, 16 * len(loads))
            dve.tensor_copy(sel[:, :, :], sel_f[:, :, :])
            dve.tensor_copy(ident_b[:, :], ident[:, :]).then_inc(const_ok, 1)

            def grid(x, w, m):
                return x.unsqueeze(3 if m else 2).broadcast_to([P, CTILES, w, w])

            def compare(x, w):
                mine, others = grid(x, w, True), grid(x, w, False)
                s1, s2 = pair[:, :, 0:w, 0:w], pair2[:, :, 0:w, 0:w]
                for t in range(CTILES):
                    dve.tensor_tensor(s1[:, t], others[:, t], mine[:, t], ALU.is_ge)
                    dve.tensor_tensor(s2[:, t], others[:, t], mine[:, t], ALU.is_gt)
                dve.drain()

            def count(w, out):
                s1, s2 = pair[:, :, 0:w, 0:w], pair2[:, :, 0:w, 0:w]
                for t in range(CTILES):
                    dve.tensor_tensor(s1[:, t], s1[:, t], lower[:, 0:w, 0:w], ALU.mult)
                    dve.tensor_tensor(s2[:, t], s2[:, t], upper[:, 0:w, 0:w], ALU.mult)
                dve.drain()
                for t in range(CTILES):
                    dve.tensor_tensor(s1[:, t], s1[:, t], s2[:, t], ALU.add)
                dve.drain()
                for t in range(CTILES):
                    dve.tensor_reduce(out[:, t], s1[:, t], AX, ALU.add)
                dve.drain()

            def stage(what, n):
                if what == "statistics":
                    dve.wait_ge(x_got, n * 16 + 16)
                    statistics(dve, xin, st, CTILES)
                elif what == "rsqrt":
                    rsqrt_steps(dve, st["rs"][:, :], st["var"][:, :], st["tmp"][:, :], CTILES)
                elif what == "norm":
                    ins = apply_norm(dve, y, xin, st, CTILES)
                    if x_more is not None:
                        dve.drain()
                        ins = affine(dve, y[:, :, :], y[:, :, :], gx[:, :], bx[:, :], CTILES)
                    ins.then_inc(y_ok, 1)
                elif what == "choice":
                    dve.wait_ge(sc_ok, n + 1)
                    bias = rb[:, :].unsqueeze(1).broadcast_to([P, CTILES, E])
                    dve.tensor_tensor(choice[:, :, :], score[:, :, :], bias, ALU.add)
                    dve.drain()
                elif what == "groups":
                    group_ranks(dve)
                    dve.tensor_scalar(kept[:, :, :], rank[:, :, :], 1.5, None, ALU.is_lt)
                    dve.drain()
                    dve.tensor_tensor(kept[:, :, :], kept[:, :, :], choice[:, :, :], ALU.mult)
                    dve.drain()
                    dve.tensor_reduce(gsum[:, :, :], kept[:, :, :].rearrange("p t (g k) -> p t g k", g=G), AX, ALU.add)
                    dve.drain()
                elif what == "keep":
                    compare(gsum[:, :, :], G)
                    count(G, rank[:, :, 0:G])
                    dve.tensor_scalar(gsum[:, :, :], rank[:, :, 0:G], 1.5, None, ALU.is_lt)
                    dve.drain()
                    for k in range(EG):
                        dve.tensor_copy(kept[:, :, :].rearrange("p t (g k) -> p t g k", g=G)[:, :, :, k], gsum[:, :, :])
                    dve.drain()
                    dve.tensor_tensor(choice[:, :, :], choice[:, :, :], kept[:, :, :], ALU.mult)
                    dve.tensor_scalar(kept[:, :, :], kept[:, :, :], -c.fill, c.fill, ALU.mult, ALU.add)
                    dve.drain()
                    dve.tensor_tensor(choice[:, :, :], choice[:, :, :], kept[:, :, :], ALU.add)
                    dve.drain()
                elif what == "compare":
                    compare(choice[:, :, :], E)
                elif what == "count":
                    count(E, rank[:, :, :])
                elif what == "best":
                    dve.tensor_scalar(comb[:, :, :], rank[:, :, :], 0.5, None, ALU.is_lt)
                    dve.drain()
                elif what == "weights":
                    dve.scalar_tensor_tensor(comb[:, :, :], rank[:, :, :], 3.5, score[:, :, :], ALU.is_lt, ALU.mult)
                    dve.drain()
                    dve.tensor_reduce(wsum[:, :, 0], comb[:, :, :], AX, ALU.add)
                    dve.drain()
                    dve.tensor_scalar(wsum[:, :, :], wsum[:, :, :], 1e-20, None, ALU.add)
                    dve.drain()
                    dve.reciprocal(wsum[:, :, :], wsum[:, :, :])
                    dve.drain()
                    dve.tensor_scalar(wsum[:, :, :], wsum[:, :, :], c.scale, None, ALU.mult)
                    dve.drain()
                    dve.tensor_tensor(comb[:, :, :], comb[:, :, :], wsum[:, :, :].broadcast_to([P, CTILES, E]), ALU.mult)
                    dve.drain()
                else:
                    dve.tensor_copy(cpart(0), comb[:, :, :])
                    dve.drain()
                    dve.tensor_tensor(comb[:, :, :], comb[:, :, :], cpart(0), ALU.subtract)
                    dve.drain()
                    dve.tensor_copy(cpart(1), comb[:, :, :])
                    dve.drain()
                    dve.tensor_tensor(cpart(2), comb[:, :, :], cpart(1), ALU.subtract).then_inc(cp_ok, 1)

            def route(n, par, k):
                for what in c.stages[k]:
                    stage(what, n)
                if k == c.copy_w:
                    dve.wait_ge(ctp_ok, n + 1)
                    dve.tensor_copy(ct[:, par, :], misc_b[0:3 * E, 0:CHUNK]).then_inc(ct_ok, 1)

            def hidden(n, par, k):
                s = (par * KC + k) % 2
                dve.wait_ge(g1_ok, n * KC + (k + 1))
                if not (isinstance(n, int) and n * KC + k < 2):
                    dve.wait_ge(dn_ok, n * KC + (k - 1))
                gk, hk = g1[:, s, :], hid[:, s, :]
                routed = k < KR
                if c.act == "silu":
                    dve.tensor_tensor(gk, hp[s][:, :], gk, ALU.mult)
                    dve.drain()
                    ins = dve.tensor_tensor(hk, up[s][:, :], gk, ALU.mult)
                    if routed:
                        dve.drain()
                        ins = dve.tensor_tensor(hk, wp[s][:, :], hk, ALU.mult)
                elif c.act == "relu2":
                    ins = dve.tensor_tensor(hk, gk, gk, ALU.mult)
                    if routed:
                        dve.drain()
                        ins = dve.tensor_tensor(hk, wp[s][:, :], hk, ALU.mult)
                else:
                    ins = dve.tensor_tensor(hk, wp[s][:, :], gk, ALU.mult)
                ins.then_inc(hid_ok, 1)

            def finish(n):
                dve.wait_ge(xr_got, n * 16 * R_DMAS + 16 * R_DMAS)
                if x_more is not None:
                    dve.tensor_tensor(xr[:, :, :], xr[:, :, :], more[:, :, :], ALU.add)
                    dve.drain()
                dve.wait_ge(ftp_ok, n + 1)
                dve.tensor_tensor(xo[:, :, :], misc[:, :].rearrange("p (t d) -> p t d", t=CTILES), xr[:, :, :],
                                  ALU.add).then_inc(xo_ok, 1)

            run(dve, hidden, route, finish)


PHASES = ["L0a", "L0f", "L1a", "L1f", "L2a", "L2f", "L3a", "L3s", "L3f"]


def build(nc, io, out, phases=PHASES):
    x, before = io["x"], {}
    for n, name in enumerate(phases):
        last = n == len(phases) - 1
        x_out = out if last else nc.dram_tensor(f"x_{name}", [N_TOK, D], F32, kind="Internal").ap()
        before[name] = x
        if name in ATTENTIONS:
            build_attention(nc, ATTENTIONS[name], io, x, x_out)
        else:
            more = None
            if name == "L3f":
                more = before.get("L3s", io.get("x_more"))
            build_mixture(nc, MIXTURES[name], io, x, x_out, more)
        x = x_out


def layout(i):
    f = lambda k: np.asarray(i[k])
    c = np.ascontiguousarray
    zeros = lambda *s: np.zeros(s, np.float32)
    io = {"x": c(f("x").reshape(N_TOK, D)), "ctx": f("ctx_1024"), "mask": f("mask_BxSxS2_bk0"),
          "ident": np.eye(P, dtype=np.float32)}
    row = lambda v: c(np.broadcast_to(v, (P, v.shape[-1])))
    spread = zeros(P, P)
    for k in range(4):
        spread[32 * k + 8, 32 * k:32 * k + 32] = 1
    io["spread"] = spread
    io["three"] = np.eye(3, dtype=np.float32)
    own = zeros(4, 4, 8, 4)
    for k in range(4):
        own[0:3, k, :, k] = 1
    io["own"] = own.reshape(P, 4)

    def put(name, **arrays):
        for k, v in arrays.items():
            io[f"{name}_{k}"] = c(v)

    for name, a in ATTENTIONS.items():
        if a.stacked:
            continue
        pick = zeros(a.parts, a.HU, a.HU)
        for e in range(a.HU):
            pick[:, e, e] = 1
        put(name, pick=pick.reshape(a.K_ROWS, a.HU))
    def key_weights(wk, heads, dh):
        tiles = heads * dh // P
        out = zeros(P, heads, P)
        for h in range(heads):
            r = (h * dh) % P
            out[r:r + dh, h, :] = wk[:, h * dh:(h + 1) * dh].T
        return out

    def key_bias(bk, heads, dh):
        out = zeros(P, heads)
        for h in range(heads):
            r = (h * dh) % P
            out[r:r + dh, h] = bk[h * dh:(h + 1) * dh]
        return out

    def small_values(wv, bv):
        w, b = zeros(P, 16, 32), zeros(16, 32)
        w[:, :, 0:8] = wv.reshape(P, 16, 8)
        if bv is not None:
            b[:, 0:8] = bv.reshape(16, 8)
        b[:, 8] = 1
        return w.reshape(P, 512), np.broadcast_to(b.reshape(512), (3, 512))

    def small_keys(wk, bk):
        w, b = zeros(P, 4, 4, 32), zeros(4, 4, 32)
        w[:, :, 0:3, :] = wk.reshape(P, 4, 1, 32)
        if bk is not None:
            b[:, 0:3, :] = bk.reshape(4, 1, 32)
        b[:, 3, 0:2] = 1
        return w.reshape(P, 4, P), b.reshape(4, P).T

    def small_queries(wq, bq):
        w, b = zeros(P, 4, 4, 32), zeros(4, 4, 32)
        w[:, :, 0:3, :] = wq.reshape(P, 4, 1, 32)
        if bq is not None:
            b[:, 0:3, :] = bq.reshape(4, 1, 32)
        return w.reshape(P, 4, P), b.reshape(4, P).T

    def small_out(wo):
        w = zeros(4, 4, 32, P)
        w[:, :, 0:8, :] = wo.reshape(4, 4, 8, P)
        return w.reshape(4, P, P).transpose(1, 0, 2)

    g = lambda k: f("L0_xattn_" + k)
    put("L0a", wq=g("Wq").T.reshape(P, 1, P), wqt=g("Wq").reshape(P, 1, P), bq=g("bq").reshape(P, 1), wk=g("Wk").reshape(P, 1, P),
        bk=g("bk").reshape(P, 1), wfin=g("Wv").T.reshape(P, 1, P), bfin=g("bv").reshape(P, 1), gx=row(g("g_t")),
        bx=row(g("b_t")), affine=np.stack([g("g_k"), g("b_k"), g("g_v"), g("b_v")], 1))
    g = lambda k: f("L1_xattn_" + k)
    wv, bv = small_values(g("Wv"), g("bv"))
    (wk, bk), (wq, bq) = small_keys(g("Wk"), g("bk")), small_queries(g("Wq"), g("bq"))
    put("L1a", wq=wq, bq=bq, wks=wk, bks=bk, wv=wv, bvr=bv, wfin=small_out(g("Wo")), bfin=g("bo").reshape(P, 1))
    g = lambda k: f("L2_xattn_" + k)
    put("L2a", wq=g("Wq").reshape(P, 8, P), wqt=g("Wq").T.reshape(8, P, P).transpose(1, 0, 2), bq=g("bq").reshape(8, P).T, wk=key_weights(g("Wk"), 16, 64),
        bk=key_bias(g("bk"), 16, 64), wv=g("Wv"), bv=row(g("bv")), wfin=g("Wo").reshape(8, P, P).transpose(1, 0, 2),
        bfin=g("bo").reshape(P, 1))
    g = lambda k: f("L3_xattn_" + k)
    wkv, bkv = g("Wkv"), g("bkv")
    put("L3a", wq=g("Wq").reshape(P, 8, P), wqt=g("Wq").T.reshape(8, P, P).transpose(1, 0, 2), bq=g("bq").reshape(8, P).T, wk=key_weights(wkv[:, 0:1024], 8, 128),
        bk=key_bias(bkv[0:1024], 8, 128), wvt=wkv[:, 1024:].reshape(P, 8, P).transpose(2, 1, 0),
        bvh=bkv[1024:].reshape(8, P).T, wo=g("Wo").reshape(8, P, P).transpose(1, 0, 2), bo=g("bo").reshape(P, 1),
        gx=row(g("gamma_lat")), bx=row(g("beta_lat")), gk=row(g("gamma_media")), bkk=row(g("beta_media")))
    g = lambda k: f("L3_ffn_" + k)
    wv, bv = small_values(g("w_qkv")[:, 256:384], None)
    (wk, bk), (wq, bq) = small_keys(g("w_qkv")[:, 128:256], None), small_queries(g("w_qkv")[:, 0:128], None)
    put("L3s", wq=wq, bq=bq, wks=wk, bks=bk, wv=wv, bvr=bv, wfin=small_out(g("w_proj")), bfin=zeros(P, 1),
        gx=row(g("ln1_w")), bx=row(g("ln1_b")))

    for name, m in MIXTURES.items():
        E = m.E
        lower, sel = np.tril(np.ones((E, E), np.float32), -1), zeros(3, E, m.SEL, P)
        per = max(1, E // m.SEL)
        for k in range(m.SEL):
            for q in range(per):
                w = P // per
                sel[:, k * per + q, k, q * w:(q + 1) * w] = 1
        put(name, lower=np.broadcast_to(lower, (P, E, E)), upper=np.broadcast_to(lower.T, (P, E, E)),
            sel=sel.reshape(3 * E, m.SEL, P))
    first = lambda w: w.transpose(1, 0, 2).reshape(P, -1)
    second = lambda w: w.reshape(-1, P, P).transpose(1, 0, 2)
    tiles = lambda w: w.reshape(P, -1, P)
    g = lambda k: f("L0_ffn_" + k)
    put("L0f", wr=g("router_w").T, rb=row(g("bias")), w1=tiles(np.concatenate([first(g("gate_w")), g("sh_gate_w")], 1)),
        wu=tiles(np.concatenate([first(g("up_w")), g("sh_up_w")], 1)),
        w2=second(np.concatenate([g("down_w").reshape(-1, P), g("sh_down_w")], 0)))
    g = lambda k: f("L1_ffn_" + k)
    put("L1f", wr=g("router_w").T, rb=row(g("correction_bias")),
        w1=tiles(np.concatenate([first(g("gate_w")), g("shared_gate_w").T], 1)),
        wu=tiles(np.concatenate([first(g("up_w")), g("shared_up_w").T], 1)),
        w2=second(np.concatenate([g("down_w").reshape(-1, P), g("shared_down_w").T], 0)))
    g = lambda k: f("L2_ffn_" + k)
    put("L2f", wr=g("Wg").T, rb=row(g("bias_corr")),
        w1=tiles(np.concatenate([g("W1").transpose(2, 0, 1).reshape(P, -1), g("Ws1").T], 1)),
        w2=second(np.concatenate([g("W2").transpose(0, 2, 1).reshape(-1, P), g("Ws2").T], 0)))
    g = lambda k: f("L3_ffn_" + k)
    put("L3f", wr=g("gate_w"), rb=row(g("gate_b")), w1=tiles(first(g("w1"))), w2=second(g("w2").reshape(-1, P)),
        gx=row(g("ln2_w")), bx=row(g("ln2_b")))
    return io


def kernel(**inputs):
    import concourse.bacc as bacc
    from concourse.bass_utils import run_bass_kernel_spmd

    arrays = layout(inputs)
    nc = bacc.Bacc("TRN2", target_bir_lowering=False, num_devices=1)
    io = {k: nc.dram_tensor(f"in_{k}", v.shape, mybir.dt.from_np(v.dtype), kind="ExternalInput").ap()
          for k, v in arrays.items()}
    out = nc.dram_tensor("out_x", [N_TOK, D], F32, kind="ExternalOutput").ap()
    build(nc, io, out)
    got = run_bass_kernel_spmd(nc, [{f"in_{k}": v for k, v in arrays.items()}], core_ids=[0])
    return got.results[0]["out_x"].reshape(B, S, D)
```
